# Optimizing a Trainium2 kernel written in Bass

```python
import numpy as np
import jax
import jax.numpy as jnp

def _softmax(x, axis=-1):
    return jax.nn.softmax(x, axis=axis)

def _gelu(x):
    return jax.nn.gelu(x, approximate=True)

def _silu(x):
    return jax.nn.silu(x)

def _sigmoid(x):
    return jax.nn.sigmoid(x)

def _layernorm(x, axis=-1, eps=1e-05):
    m = jnp.mean(x, axis=axis, keepdims=True)
    v = jnp.var(x, axis=axis, keepdims=True)
    return (x - m) / jnp.sqrt(v + eps)

def _scatter_add(tgt, idx, src, axis=0):
    return tgt.at[idx].add(src)

def _segment_sum(src, seg, n):
    return jax.ops.segment_sum(src, seg, n)
kernel_name = 'mk_macaron_d2_jaxref_r8_ec32c8'

def setup_inputs(seed: int=0):
    np.random.seed(seed)
    _w = jnp.asarray

    def _L0_attn_setup():
        import jax, jax.numpy as jnp
        import numpy as np
        import math
        from jax import lax
        B, T, HID, H, J = (4, 256, 128, 8, 2)
        EPS = 1e-06
        LN_EPS = 1e-05

        def _alibi_slopes(n):

            def pow2(m):
                start = 2 ** (-2 ** (-(math.log2(m) - 3)))
                return [start * start ** i for i in range(m)]
            if math.log2(n).is_integer():
                return np.array(pow2(n), dtype=np.float32)
            c = 2 ** int(math.floor(math.log2(n)))
            s = pow2(c) + _alibi_slopes(2 * c).tolist()[:n - c]
            return np.array(s, dtype=np.float32)

        def _deltanet(x, Wq, Wk, Wv, Wbeta, bbeta, Wmix, bmix, Wgate, bgate, Wout, bout, ln_g, ln_b):
            b, t, hid = x.shape
            h = Wgate.shape[0]
            j = Wbeta.shape[0] // h
            d = hid // h
            r = jnp.asarray(np.exp(-_alibi_slopes(h)))[None, :, None]
            q = (jax.nn.elu(x @ Wq.T) + 1.0).reshape(b, t, h, d)
            k = (jax.nn.elu(x @ Wk.T) + 1.0).reshape(b, t, h, d)
            v = (x @ Wv.T).reshape(b, t, h, d)
            beta = (x @ Wbeta.T + bbeta).reshape(b, t, h, j)
            mix = (x @ Wmix.T + bmix).reshape(b, t, h, j)
            gate = jax.nn.sigmoid(x @ Wgate.T + bgate)

            def step(carry, inp):
                S, z = carry
                q_t, k_t, v_t, beta_t, mix_t, g_t = inp
                beta_eff = jnp.minimum(jax.nn.sigmoid(beta_t) * r, 0.9999)
                outer = jnp.einsum('bhd,bhe->bhde', k_t, v_t).astype(jnp.float32)[:, :, None]
                S = S * beta_eff[..., None, None] + g_t[:, :, None, None, None] * outer
                z = z * beta_eff[..., None] + g_t[:, :, None, None] * k_t[:, :, None, :]
                num = jnp.einsum('bhd,bhjde->bhje', q_t, S)
                denom = jnp.einsum('bhd,bhjd->bhj', q_t, z) + EPS
                w = jax.nn.softmax(mix_t, axis=-1)[..., None]
                y_t = jnp.sum(num / denom[..., None] * w, axis=2)
                return ((S, z), y_t)
            S0 = jnp.zeros((b, h, j, d, d), jnp.float32)
            z0 = jnp.zeros((b, h, j, d), jnp.float32)
            tm = lambda a: jnp.swapaxes(a, 0, 1)
            _, yT = lax.scan(step, (S0, z0), (tm(q), tm(k), tm(v), tm(beta), tm(mix), tm(gate)))
            y = jnp.swapaxes(yT, 0, 1).reshape(b, t, hid).astype(x.dtype)
            out = y @ Wout.T + bout
            hres = x + out
            mu = jnp.mean(hres, axis=-1, keepdims=True)
            var = jnp.mean(jnp.square(hres - mu), axis=-1, keepdims=True)
            return (hres - mu) / jnp.sqrt(var + LN_EPS) * ln_g + ln_b
        key = jax.random.key(seed)
        ks = jax.random.split(key, 9)
        sc = 0.02
        return {'x': jax.random.normal(ks[0], (B, T, HID), jnp.float32), 'Wq': jax.random.normal(ks[1], (HID, HID), jnp.float32) * sc, 'Wk': jax.random.normal(ks[2], (HID, HID), jnp.float32) * sc, 'Wv': jax.random.normal(ks[3], (HID, HID), jnp.float32) * sc, 'Wbeta': jax.random.normal(ks[4], (H * J, HID), jnp.float32) * sc, 'bbeta': jnp.full((H * J,), 2.1972, jnp.float32), 'Wmix': jax.random.normal(ks[5], (H * J, HID), jnp.float32) * sc, 'bmix': jnp.zeros((H * J,), jnp.float32), 'Wgate': jax.random.normal(ks[6], (H, HID), jnp.float32) * sc, 'bgate': jnp.zeros((H,), jnp.float32), 'Wout': jax.random.normal(ks[7], (HID, HID), jnp.float32) * sc, 'bout': jnp.zeros((HID,), jnp.float32), 'ln_g': jnp.ones((HID,), jnp.float32), 'ln_b': jnp.zeros((HID,), jnp.float32)}
    _L0_attn_in = _L0_attn_setup()

    def _L0_ffn_setup():
        import jax, jax.numpy as jnp
        import numpy as np
        B, S, K, N = (8, 1024, 128, 128)
        key = jax.random.key(seed)
        k1, k2, k3, k4 = jax.random.split(key, 4)
        x = jax.random.normal(k1, (B, S, K), dtype=jnp.float32)
        CB = jnp.clip(jnp.round(jax.random.normal(k2, (N, K), dtype=jnp.float32) * 42.0), -127.0, 127.0)
        SCB = jax.random.uniform(k3, (N,), dtype=jnp.float32, minval=0.5, maxval=2.0)
        bias = jax.random.normal(k4, (N,), dtype=jnp.float32) * 0.02
        return {'x': x, 'CB': CB, 'SCB': SCB, 'bias': bias}
    _L0_ffn_in = _L0_ffn_setup()

    def _L1_attn_setup():
        import jax, jax.numpy as jnp
        import numpy as np
        EPS = 1e-05

        def _proj_ln(x, W, b, g, beta):
            y = jnp.einsum('blc,cd->bld', x, W) + b
            mu = jnp.mean(y, axis=-1, keepdims=True)
            var = jnp.var(y, axis=-1, keepdims=True)
            return (y - mu) * jax.lax.rsqrt(var + EPS) * g + beta
        key = jax.random.key(seed)
        B, L, C, H = (4, 256, 128, 128)
        ks = jax.random.split(key, 7)
        s_in = 1.0 / np.sqrt(C)
        inp = {'input_sequence': jax.random.normal(ks[0], (B, L, C), jnp.float32), 'Wk': jax.random.normal(ks[1], (C, H), jnp.float32) * s_in, 'bk': jnp.zeros((H,), jnp.float32), 'gk': jnp.ones((H,), jnp.float32), 'betak': jnp.zeros((H,), jnp.float32), 'Wq': jax.random.normal(ks[2], (C, H), jnp.float32) * s_in, 'bq': jnp.zeros((H,), jnp.float32), 'gq': jnp.ones((H,), jnp.float32), 'betaq': jnp.zeros((H,), jnp.float32), 'Wv': jax.random.normal(ks[3], (C, C), jnp.float32) * s_in, 'bv': jnp.zeros((C,), jnp.float32), 'gv': jnp.ones((C,), jnp.float32), 'betav': jnp.zeros((C,), jnp.float32)}
        return inp
    _L1_attn_in = _L1_attn_setup()

    def _L1_ffn_setup():
        import jax, jax.numpy as jnp
        import numpy as np
        D_MODEL = 128
        N_HEAD = 16
        HEAD_DIM = D_MODEL // N_HEAD
        D_FF = 512
        N_EXPERTS = 4
        EPS = 1e-05

        def _layer_norm(x, gamma, beta):
            mu = jnp.mean(x, axis=-1, keepdims=True)
            var = jnp.mean((x - mu) ** 2, axis=-1, keepdims=True)
            return (x - mu) / jnp.sqrt(var + EPS) * gamma + beta
        key = jax.random.key(seed)
        ks = jax.random.split(key, 20)
        f32 = jnp.float32
        sc = 1.0 / np.sqrt(D_MODEL)
        scf = 1.0 / np.sqrt(D_FF)
        return {'src': jax.random.normal(ks[0], (4, 64, D_MODEL), f32), 'Wq': jax.random.normal(ks[1], (D_MODEL, D_MODEL), f32) * sc, 'bq': jnp.zeros((D_MODEL,), f32), 'Wk': jax.random.normal(ks[2], (D_MODEL, D_MODEL), f32) * sc, 'bk': jnp.zeros((D_MODEL,), f32), 'Wv': jax.random.normal(ks[3], (D_MODEL, D_MODEL), f32) * sc, 'bv': jnp.zeros((D_MODEL,), f32), 'Wo': jax.random.normal(ks[4], (D_MODEL, D_MODEL), f32) * sc, 'bo': jnp.zeros((D_MODEL,), f32), 'router_w': jax.random.normal(ks[5], (D_MODEL, 1), f32) * 0.05, 'router_b': jnp.zeros((1,), f32), 'W1': jax.random.normal(ks[6], (N_EXPERTS, D_MODEL, D_FF), f32) * sc, 'b1': jnp.zeros((N_EXPERTS, D_FF), f32), 'W2': jax.random.normal(ks[7], (N_EXPERTS, D_FF, D_MODEL), f32) * scf, 'b2': jnp.zeros((N_EXPERTS, D_MODEL), f32), 'ln1_g': jnp.ones((D_MODEL,), f32), 'ln1_b': jnp.zeros((D_MODEL,), f32), 'ln2_g': jnp.ones((D_MODEL,), f32), 'ln2_b': jnp.zeros((D_MODEL,), f32)}
    _L1_ffn_in = _L1_ffn_setup()
    _d = {'L0_attn_x': _L0_attn_in['x'], 'L0_attn_Wq': _L0_attn_in['Wq'], 'L0_attn_Wk': _L0_attn_in['Wk'], 'L0_attn_Wv': _L0_attn_in['Wv'], 'L0_attn_Wbeta': _L0_attn_in['Wbeta'], 'L0_attn_bbeta': _L0_attn_in['bbeta'], 'L0_attn_Wmix': _L0_attn_in['Wmix'], 'L0_attn_bmix': _L0_attn_in['bmix'], 'L0_attn_Wgate': _L0_attn_in['Wgate'], 'L0_attn_bgate': _L0_attn_in['bgate'], 'L0_attn_Wout': _L0_attn_in['Wout'], 'L0_attn_bout': _L0_attn_in['bout'], 'L0_attn_ln_g': _L0_attn_in['ln_g'], 'L0_attn_ln_b': _L0_attn_in['ln_b'], 'L0_ffn_CB': _L0_ffn_in['CB'], 'L0_ffn_SCB': _L0_ffn_in['SCB'], 'L0_ffn_bias': _L0_ffn_in['bias'], 'L1_attn_Wk': _L1_attn_in['Wk'], 'L1_attn_bk': _L1_attn_in['bk'], 'L1_attn_gk': _L1_attn_in['gk'], 'L1_attn_betak': _L1_attn_in['betak'], 'L1_attn_Wq': _L1_attn_in['Wq'], 'L1_attn_bq': _L1_attn_in['bq'], 'L1_attn_gq': _L1_attn_in['gq'], 'L1_attn_betaq': _L1_attn_in['betaq'], 'L1_attn_Wv': _L1_attn_in['Wv'], 'L1_attn_bv': _L1_attn_in['bv'], 'L1_attn_gv': _L1_attn_in['gv'], 'L1_attn_betav': _L1_attn_in['betav'], 'L1_ffn_Wq': _L1_ffn_in['Wq'], 'L1_ffn_bq': _L1_ffn_in['bq'], 'L1_ffn_Wk': _L1_ffn_in['Wk'], 'L1_ffn_bk': _L1_ffn_in['bk'], 'L1_ffn_Wv': _L1_ffn_in['Wv'], 'L1_ffn_bv': _L1_ffn_in['bv'], 'L1_ffn_Wo': _L1_ffn_in['Wo'], 'L1_ffn_bo': _L1_ffn_in['bo'], 'L1_ffn_router_w': _L1_ffn_in['router_w'], 'L1_ffn_router_b': _L1_ffn_in['router_b'], 'L1_ffn_W1': _L1_ffn_in['W1'], 'L1_ffn_b1': _L1_ffn_in['b1'], 'L1_ffn_W2': _L1_ffn_in['W2'], 'L1_ffn_b2': _L1_ffn_in['b2'], 'L1_ffn_ln1_g': _L1_ffn_in['ln1_g'], 'L1_ffn_ln1_b': _L1_ffn_in['ln1_b'], 'L1_ffn_ln2_g': _L1_ffn_in['ln2_g'], 'L1_ffn_ln2_b': _L1_ffn_in['ln2_b']}
    _x0 = _d['L0_attn_x']
    _d['L0_attn_x'] = jax.random.normal(jax.random.fold_in(jax.random.key(seed), 1), (16, 256, 128), dtype=_x0.dtype)
    del _x0
    return _d

def reference(L0_attn_x, L0_attn_Wq, L0_attn_Wk, L0_attn_Wv, L0_attn_Wbeta, L0_attn_bbeta, L0_attn_Wmix, L0_attn_bmix, L0_attn_Wgate, L0_attn_bgate, L0_attn_Wout, L0_attn_bout, L0_attn_ln_g, L0_attn_ln_b, L0_ffn_CB, L0_ffn_SCB, L0_ffn_bias, L1_attn_Wk, L1_attn_bk, L1_attn_gk, L1_attn_betak, L1_attn_Wq, L1_attn_bq, L1_attn_gq, L1_attn_betaq, L1_attn_Wv, L1_attn_bv, L1_attn_gv, L1_attn_betav, L1_ffn_Wq, L1_ffn_bq, L1_ffn_Wk, L1_ffn_bk, L1_ffn_Wv, L1_ffn_bv, L1_ffn_Wo, L1_ffn_bo, L1_ffn_router_w, L1_ffn_router_b, L1_ffn_W1, L1_ffn_b1, L1_ffn_W2, L1_ffn_b2, L1_ffn_ln1_g, L1_ffn_ln1_b, L1_ffn_ln2_g, L1_ffn_ln2_b):

    def _L0_attn_ref(x, Wq, Wk, Wv, Wbeta, bbeta, Wmix, bmix, Wgate, bgate, Wout, bout, ln_g, ln_b):
        import jax, jax.numpy as jnp
        import numpy as np
        import math
        from jax import lax
        B, T, HID, H, J = (4, 256, 128, 8, 2)
        EPS = 1e-06
        LN_EPS = 1e-05

        def _alibi_slopes(n):

            def pow2(m):
                start = 2 ** (-2 ** (-(math.log2(m) - 3)))
                return [start * start ** i for i in range(m)]
            if math.log2(n).is_integer():
                return np.array(pow2(n), dtype=np.float32)
            c = 2 ** int(math.floor(math.log2(n)))
            s = pow2(c) + _alibi_slopes(2 * c).tolist()[:n - c]
            return np.array(s, dtype=np.float32)

        def _deltanet(x, Wq, Wk, Wv, Wbeta, bbeta, Wmix, bmix, Wgate, bgate, Wout, bout, ln_g, ln_b):
            b, t, hid = x.shape
            h = Wgate.shape[0]
            j = Wbeta.shape[0] // h
            d = hid // h
            r = jnp.asarray(np.exp(-_alibi_slopes(h)))[None, :, None]
            q = (jax.nn.elu(x @ Wq.T) + 1.0).reshape(b, t, h, d)
            k = (jax.nn.elu(x @ Wk.T) + 1.0).reshape(b, t, h, d)
            v = (x @ Wv.T).reshape(b, t, h, d)
            beta = (x @ Wbeta.T + bbeta).reshape(b, t, h, j)
            mix = (x @ Wmix.T + bmix).reshape(b, t, h, j)
            gate = jax.nn.sigmoid(x @ Wgate.T + bgate)

            def step(carry, inp):
                S, z = carry
                q_t, k_t, v_t, beta_t, mix_t, g_t = inp
                beta_eff = jnp.minimum(jax.nn.sigmoid(beta_t) * r, 0.9999)
                outer = jnp.einsum('bhd,bhe->bhde', k_t, v_t).astype(jnp.float32)[:, :, None]
                S = S * beta_eff[..., None, None] + g_t[:, :, None, None, None] * outer
                z = z * beta_eff[..., None] + g_t[:, :, None, None] * k_t[:, :, None, :]
                num = jnp.einsum('bhd,bhjde->bhje', q_t, S)
                denom = jnp.einsum('bhd,bhjd->bhj', q_t, z) + EPS
                w = jax.nn.softmax(mix_t, axis=-1)[..., None]
                y_t = jnp.sum(num / denom[..., None] * w, axis=2)
                return ((S, z), y_t)
            S0 = jnp.zeros((b, h, j, d, d), jnp.float32)
            z0 = jnp.zeros((b, h, j, d), jnp.float32)
            tm = lambda a: jnp.swapaxes(a, 0, 1)
            _, yT = lax.scan(step, (S0, z0), (tm(q), tm(k), tm(v), tm(beta), tm(mix), tm(gate)))
            y = jnp.swapaxes(yT, 0, 1).reshape(b, t, hid).astype(x.dtype)
            out = y @ Wout.T + bout
            hres = x + out
            mu = jnp.mean(hres, axis=-1, keepdims=True)
            var = jnp.mean(jnp.square(hres - mu), axis=-1, keepdims=True)
            return (hres - mu) / jnp.sqrt(var + LN_EPS) * ln_g + ln_b
        return _deltanet(x, Wq, Wk, Wv, Wbeta, bbeta, Wmix, bmix, Wgate, bgate, Wout, bout, ln_g, ln_b)

    def _L0_ffn_ref(x, CB, SCB, bias):
        import jax, jax.numpy as jnp
        import numpy as np
        B, S, K, N = (8, 1024, 128, 128)
        out = jnp.einsum('bsk,nk->bsn', x, CB)
        out = out * (SCB * (1.0 / 127.0)) + bias
        return out

    def _L1_attn_ref(input_sequence, Wk, bk, gk, betak, Wq, bq, gq, betaq, Wv, bv, gv, betav):
        import jax, jax.numpy as jnp
        import numpy as np
        EPS = 1e-05

        def _proj_ln(x, W, b, g, beta):
            y = jnp.einsum('blc,cd->bld', x, W) + b
            mu = jnp.mean(y, axis=-1, keepdims=True)
            var = jnp.var(y, axis=-1, keepdims=True)
            return (y - mu) * jax.lax.rsqrt(var + EPS) * g + beta
        values = _proj_ln(input_sequence, Wv, bv, gv, betav)
        k = _proj_ln(input_sequence, Wk, bk, gk, betak)
        q = _proj_ln(input_sequence, Wq, bq, gq, betaq)
        scores = jnp.einsum('blc,bLc->blL', k, q)
        attn = jax.nn.softmax(scores, axis=-1)
        out = jnp.einsum('blL,bLc->blc', attn, values)
        return out + input_sequence

    def _L1_ffn_ref(src, Wq, bq, Wk, bk, Wv, bv, Wo, bo, router_w, router_b, W1, b1, W2, b2, ln1_g, ln1_b, ln2_g, ln2_b):
        import jax, jax.numpy as jnp
        import numpy as np
        D_MODEL = 128
        N_HEAD = 16
        HEAD_DIM = D_MODEL // N_HEAD
        D_FF = 512
        N_EXPERTS = 4
        EPS = 1e-05

        def _layer_norm(x, gamma, beta):
            mu = jnp.mean(x, axis=-1, keepdims=True)
            var = jnp.mean((x - mu) ** 2, axis=-1, keepdims=True)
            return (x - mu) / jnp.sqrt(var + EPS) * gamma + beta
        B, T, _ = src.shape
        q = (src @ Wq + bq).reshape(B, T, N_HEAD, HEAD_DIM)
        k = (src @ Wk + bk).reshape(B, T, N_HEAD, HEAD_DIM)
        v = (src @ Wv + bv).reshape(B, T, N_HEAD, HEAD_DIM)
        scale = HEAD_DIM ** (-0.5)
        scores = jnp.einsum('bqhd,bkhd->bhqk', q, k) * scale
        probs = jax.nn.softmax(scores, axis=-1)
        attn = jnp.einsum('bhqk,bkhd->bqhd', probs, v).reshape(B, T, D_MODEL)
        attn = attn @ Wo + bo
        x = _layer_norm(src + attn, ln1_g, ln1_b)
        keys = (x @ router_w + router_b)[..., 0]
        expert_idx = jnp.remainder(jnp.floor(keys).astype(jnp.int32), N_EXPERTS)
        ff_out = jnp.zeros_like(x)
        for e in range(N_EXPERTS):
            h = jax.nn.relu(x @ W1[e] + b1[e])
            y = h @ W2[e] + b2[e]
            ff_out = ff_out + jnp.where((expert_idx == e)[..., None], y, 0.0)
        return _layer_norm(x + ff_out, ln2_g, ln2_b)
    x = L0_attn_x
    x = x + 0.5 * _L0_ffn_ref(_layernorm(x, axis=-1), L0_ffn_CB, L0_ffn_SCB, L0_ffn_bias)
    x = x + _L0_attn_ref(_layernorm(x, axis=-1), L0_attn_Wq, L0_attn_Wk, L0_attn_Wv, L0_attn_Wbeta, L0_attn_bbeta, L0_attn_Wmix, L0_attn_bmix, L0_attn_Wgate, L0_attn_bgate, L0_attn_Wout, L0_attn_bout, L0_attn_ln_g, L0_attn_ln_b)
    x = x + 0.5 * _L0_ffn_ref(_layernorm(x, axis=-1), L0_ffn_CB, L0_ffn_SCB, L0_ffn_bias)
    x = x + 0.5 * _L1_ffn_ref(_layernorm(x, axis=-1), L1_ffn_Wq, L1_ffn_bq, L1_ffn_Wk, L1_ffn_bk, L1_ffn_Wv, L1_ffn_bv, L1_ffn_Wo, L1_ffn_bo, L1_ffn_router_w, L1_ffn_router_b, L1_ffn_W1, L1_ffn_b1, L1_ffn_W2, L1_ffn_b2, L1_ffn_ln1_g, L1_ffn_ln1_b, L1_ffn_ln2_g, L1_ffn_ln2_b)
    x = x + _L1_attn_ref(_layernorm(x, axis=-1), L1_attn_Wk, L1_attn_bk, L1_attn_gk, L1_attn_betak, L1_attn_Wq, L1_attn_bq, L1_attn_gq, L1_attn_betaq, L1_attn_Wv, L1_attn_bv, L1_attn_gv, L1_attn_betav)
    x = x + 0.5 * _L1_ffn_ref(_layernorm(x, axis=-1), L1_ffn_Wq, L1_ffn_bq, L1_ffn_Wk, L1_ffn_bk, L1_ffn_Wv, L1_ffn_bv, L1_ffn_Wo, L1_ffn_bo, L1_ffn_router_w, L1_ffn_router_b, L1_ffn_W1, L1_ffn_b1, L1_ffn_W2, L1_ffn_b2, L1_ffn_ln1_g, L1_ffn_ln1_b, L1_ffn_ln2_g, L1_ffn_ln2_b)
    return x

_drawn_inputs = setup_inputs


def setup_inputs(seed=0):
    import zlib

    import numpy as np

    out = dict(_drawn_inputs(seed))
    spreads = {'L0_attn_bbeta': (2.197200059890747, 0.6),
     'L0_attn_bmix': (0.0, 2.0),
     'L0_attn_bgate': (0.0, 0.8),
     'L0_attn_bout': (0.0, 0.3),
     'L0_attn_ln_g': (1.0, 0.2),
     'L0_attn_ln_b': (0.0, 0.1),
     'L1_attn_bk': (0.0, 0.348),
     'L1_attn_gk': (1.0, 0.2),
     'L1_attn_betak': (0.0, 0.1),
     'L1_attn_bq': (0.0, 0.68),
     'L1_attn_gq': (1.0, 0.2),
     'L1_attn_betaq': (0.0, 2.0),
     'L1_attn_bv': (0.0, 0.467),
     'L1_attn_gv': (1.0, 0.2),
     'L1_attn_betav': (0.0, 0.494),
     'L1_ffn_bq': (0.0, 0.8),
     'L1_ffn_bk': (0.0, 2.0),
     'L1_ffn_bv': (0.0, 0.268),
     'L1_ffn_bo': (0.0, 0.331),
     'L1_ffn_b1': (0.0, 0.793),
     'L1_ffn_b2': (0.0, 0.547),
     'L1_ffn_ln1_g': (1.0, 0.2),
     'L1_ffn_ln1_b': (0.0, 0.38),
     'L1_ffn_ln2_g': (1.0, 0.2),
     'L1_ffn_ln2_b': (0.0, 0.454)}
    factors = {'L0_attn_Wq': 8.0,
     'L0_attn_Wk': 8.0,
     'L0_attn_Wv': 8.0,
     'L0_attn_Wbeta': 8.0,
     'L0_attn_Wmix': 8.0,
     'L0_attn_Wgate': 8.0,
     'L0_attn_Wout': 7.724,
     'L0_ffn_bias': 7.929}
    for name, (base, spread) in spreads.items():
        noise = np.random.default_rng([zlib.crc32(name.encode()), seed]).standard_normal(out[name].shape)
        drawn = base * np.exp(spread * noise) if base else spread * noise
        out[name] = jnp.asarray(drawn.astype(out[name].dtype))
    for name, factor in factors.items():
        out[name] = (out[name] * factor).astype(out[name].dtype)
    return out
```

```python
from contextlib import ExitStack

import numpy as np

import concourse.bass as bass
from concourse import mybir

ALU = mybir.AluOpType
ACT = mybir.ActivationFunctionType
AX_X = mybir.AxisListType.X
F32 = mybir.dt.float32
BF16 = mybir.dt.bfloat16
I32 = mybir.dt.int32

P = 128
SEQS, T = 16, 256
TILES = SEQS * T // P
TP = 4
N = TP * P
PAIRS = TILES // TP
H0, J0, D0 = 8, 2, 16
HJ = H0 * J0
H1, D1 = 16, 8
FF, EXPERTS = 512, 4
CH = FF // P
SLOTS = 6
KROWS = SLOTS * D1 + 2
LN_EPS, DEN_EPS = 1e-5, 1e-6
PHASES = ("ffn", "linear", "ffn", "heads", "experts", "attn", "heads", "experts")

ROWS = ("scb", "qbias", "bmg", "bout", "lng", "lnb", "bv", "bo", "ln1g", "ln1b", "ln2g", "ln2b", "rw", "rb",
        "b2_0", "b2_1", "b2_2", "b2_3", "abk", "abq", "abv", "agk", "agq", "agv", "aek", "aeq", "aev")
ROW = {name: i for i, name in enumerate(ROWS)}
PACK = {}
_at = 0
for _name, _n in (("cbt", 128), ("q0", 128), ("k0", 128), ("vmg", 152), ("beta", 128), ("out0", 128), ("q1", 128),
                  ("k1", 128), ("v1", 128), ("o1", 128), ("kqv", 384), ("bq", 1), ("bk", 1), ("b1", 16), ("bbeta", 1),
                  ("decay", 1), ("hmask", 8), ("ident", 128), ("sel", HJ * P)):
    PACK[_name] = (_at, _n)
    _at += _n
PACKED = _at
BETA_ROWS = (0, 64, 96)


def later(count):
    return not isinstance(count, int) or count > 0


class Link:

    def __init__(self, engine, sem, index, per):
        self.engine, self.sem, self.start, self.per, self.k = engine, sem, index * per, per, 0

    def __call__(self, instruction):
        instruction.then_inc(self.sem, 1)
        self.k += 1
        self.engine.wait_ge(self.sem, self.start + self.k)

    def close(self):
        assert self.k == self.per, (self.k, self.per)


def over(ap, shape):
    return ap.to_broadcast(shape)


def program(nc, x, pack, rows, w1, w2, out):
    with ExitStack() as ctx:
        def sb(name, shape, dt=F32, scope=ctx):
            return scope.enter_context(nc.sbuf_tensor(name, shape, dt))

        def sem(name):
            return ctx.enter_context(nc.semaphore(name))

        bank = [ctx.enter_context(nc.psum_tensor(f"bank{i}", [P, 512], F32)) for i in range(8)]

        def tiles(b):
            return bank[b][:, :].rearrange("p (t c) -> p t c", t=TP)

        X = sb("X", [P, TILES, P])
        W = sb("W", [P, PACKED - HJ * P])
        R = sb("R", [P, len(ROWS), P])
        W1 = sb("W1", [P, EXPERTS, FF])
        W2 = sb("W2", [P, EXPERTS, CH, P])
        half = sb("half", [P, TP])
        tick = sb("tick", [P, 1])
        half12 = sb("half12", [P, 12])
        st = sb("st", [P, TP, 6])
        mv = sb("mv", [P, TP, 2])
        ve = sb("ve", [P, TP])
        rs = sb("rs", [P, TP])
        st2 = sb("st2", [P, TP, 6])
        mv2 = sb("mv2", [P, TP, 2])
        ve2 = sb("ve2", [P, TP])
        rs2 = sb("rs2", [P, TP])

        scr_q = nc.dram_tensor("scr_q", (2, SLOTS, P, T), BF16, kind="Internal").ap()
        scr_k = nc.dram_tensor("scr_k", (2, SLOTS, P, T), BF16, kind="Internal").ap()
        scr_m = nc.dram_tensor("scr_m", (2, 2, H1, T), BF16, kind="Internal").ap()
        LOADS = 3 + 2 * EXPERTS

        def wt(name):
            a, n = PACK[name]
            return W[:, a:a + n]

        def row(name):
            return R[:, ROW[name], :]

        def row4(name):
            return over(R[:, ROW[name]:ROW[name] + 1, :], [P, TP, P])

        with ExitStack() as early:
            FY = [sb(f"FY{i}", [P, TP, P], scope=early) for i in range(2)]
            FYT = [sb(f"FYT{i}", [P, N], scope=early) for i in range(2)]
            XB = [sb(f"XB{i}", [P, TP, P], scope=early) for i in range(2)]
            SEL = sb("SEL", [P, HJ, P], BF16, scope=early)
            I0 = sb("I0", [P, 512], scope=early)
            I1 = sb("I1", [P, 512], scope=early)
            nbb = sb("nbb", [P, 1], scope=early)
            Y0 = [sb(f"Y0_{i}", [P, TP, P], scope=early) for i in range(2)]
            YR0 = sb("YR0", [P, TP, P], scope=early)
            YT0 = sb("YT0", [P, N], scope=early)
            ex = sb("ex", [P, 2, N], scope=early)
            re = sb("re", [P, 2, N], scope=early)
            qf = sb("qf", [P, N], scope=early)
            kT = [sb(f"kT{i}", [P, N], scope=early) for i in range(2)]
            QX = [sb(f"QX{i}", [P, 2, H0, T], scope=early) for i in range(2)]
            selF = QX[0][:, :, :, :].rearrange("p b h t -> p (b h t)")[:, 0:HJ * P]
            bE = sb("bE", [P, N], scope=early)
            b1r = sb("b1r", [P, N], scope=early)
            b2r = sb("b2r", [P, N], scope=early)
            STK = [sb(f"STK{i}", [P, 2, 384], BF16, scope=early) for i in range(2)]
            MG = sb("MG", [P, TP, 24], scope=early)
            mx = sb("mx", [P, TP, H0], scope=early)
            E0 = sb("E0", [P, TP, 24], scope=early)
            E1 = sb("E1", [P, TP, 24], scope=early)
            SD = sb("SD", [P, TP, 16], scope=early)
            RD = sb("RD", [P, TP, 16], scope=early)
            WM = [sb(f"WM{i}", [P, TP, HJ], scope=early) for i in range(2)]
            VG = [sb(f"VG{i}", [P, TP, H0, 32], scope=early) for i in range(2)]
            DD0 = [sb(f"DD0_{i}", [P, 1024], scope=early) for i in range(2)]
            DD1 = [sb(f"DD1_{i}", [P, 512], scope=early) for i in range(2)]
            SS = [sb(f"SS{i}", [P, 768], scope=early) for i in range(2)]
            A0 = [sb(f"A0_{i}", [P, 4, T], scope=early) for i in range(2)]
            A1 = [sb(f"A1_{i}", [P, 4, P], scope=early) for i in range(2)]
            OT0 = [sb(f"OT0_{i}", [P, 4, T], scope=early) for i in range(2)]
            den = sb("den", [P, HJ], scope=early)
            rec = sb("rec", [P, HJ], scope=early)
            rw0 = sb("rw0", [P, HJ], scope=early)
            PR = sb("PR", [P, HJ, D0], scope=early)
            YO = sb("YO", [P, TP, P], scope=early)
            YOT = sb("YOT", [P, N], scope=early)
            HR = sb("HR", [P, TP, P], scope=early)
            HN = sb("HN", [P, TP, P], scope=early)
            HG = sb("HG", [P, TP, P], scope=early)

        late = ctx
        X1 = sb("X1", [P, TILES, P])
        QS = [sb(f"QS{i}", [P, 2, H1 // 2, T], BF16, scope=late) for i in range(2)]
        KS = [sb(f"KS{i}", [P, 2, H1 // 2, T], BF16, scope=late) for i in range(2)]
        V1 = [sb(f"V1_{i}", [P, TP, H1, 32], scope=late) for i in range(2)]
        VS = sb("VS", [P, TP, P], scope=late)
        PB = [sb(f"PB{i}", [P, 2, T], scope=late) for i in range(4)]
        YT1 = sb("YT1", [P, N], scope=late)
        Y1 = [sb(f"Y1_{i}", [P, TP, P], scope=late) for i in range(2)]
        YR1 = [sb(f"YR1_{i}", [P, TP, P], scope=late) for i in range(2)]
        qk32 = [sb(f"qk32_{i}", [P, N], scope=late) for i in range(2)]
        qkr = [sb(f"qkr_{i}", [P, N], scope=late) for i in range(2)]
        PQ = [sb(f"PQ_{i}", [P, 3, N], BF16, scope=late) for i in range(2)]
        OT1 = [sb(f"OT1_{i}", [P, 4, T], scope=late) for i in range(2)]
        NM = sb("NM", [P, TP, H1], scope=late)
        MH = [sb(f"MH{i}", [H1, 2, T], BF16, scope=late) for i in range(2)]
        ones = sb("ones", [2, H1 // 2 * T * 2], BF16, scope=late)
        rec1 = sb("rec1", [P, TP, H1], scope=late)
        AN = sb("AN", [P, TP, P], scope=late)
        ANT = sb("ANT", [P, N], scope=late)
        Z = sb("Z", [P, TP, P], scope=late)
        ZN = sb("ZN", [P, TP, P], scope=late)
        ZG = sb("ZG", [P, TP, P], scope=late)
        with ExitStack() as shared:
            XS = [sb(f"XS{i}", [P, TP, P], scope=shared) for i in range(2)]
            XT = [sb(f"XT{i}", [P, N], scope=shared) for i in range(2)]
            HB = [sb(f"HB{i}", [P, CH, N], scope=shared) for i in range(2)]
            YB = sb("YB", [P, TP, P], scope=shared)
            AC = Z
            KP = YB
            key = [sb(f"key{i}", [P, TP], scope=shared) for i in range(3)]
            kint = sb("kint", [P, TP], I32, scope=shared)
            MK = [sb(f"MK{i}", [P, EXPERTS, TP], scope=shared) for i in range(2)]
            EN = ZN
            EG = ZG
        with ExitStack() as shared:
            YV, YVT, kqT, PAT, PA, YX = Y1, YT1, qk32, qkr, OT1[0], VS
            KQV = [sb(f"KQV{i}", [P, TP, 3, P], scope=shared) for i in range(2)]
            st12 = sb("st12", [P, 12, 6], scope=shared)
            dif12, mean12, var12 = (sb(f"{k}12", [P, 12], scope=shared) for k in ("dif", "mean", "var"))
            ve12 = sb("ve12", [P, 12], scope=shared)
            rs12 = sb("rs12", [P, 12], scope=shared)
            nmx = sb("nmx", [P, TP], scope=shared)
            esum = sb("esum", [P, TP], scope=shared)
            rsum = sb("rsum", [P, TP], scope=shared)

        x_loaded, w_loaded, stored = sem("x_loaded"), sem("w_loaded"), sem("stored")
        setup_done = sem("setup_done")
        setup_link = sem("setup_link")
        consts_done = sem("consts_done")
        x_done = sem("x_done")

        class F:
            link = sem("ffn_link")
            var = sem("ffn_var")
            rstd = sem("ffn_rstd")
            norm = sem("ffn_norm")
            turned = sem("ffn_turned")
            copied = sem("ffn_copied")
            mm = sem("ffn_mm")
            xb = sem("ffn_xb")

        class L:
            link_ln = sem("lin_link_ln")
            link_beta = sem("lin_link_beta")
            link_gate = sem("lin_link_gate")
            link_post = sem("lin_link_post")
            link_out = sem("lin_link_out")
            var = sem("lin_var")
            rstd = sem("lin_rstd")
            norm = sem("lin_norm")
            turned = sem("lin_turned")
            copied = sem("lin_copied")
            qk = sem("lin_qk")
            exp4 = sem("lin_exp4")
            beta = sem("lin_beta")
            ebeta = sem("lin_ebeta")
            vmg = sem("lin_vmg")
            v_used = sem("lin_v_used")
            e0 = sem("lin_e0")
            e1 = sem("lin_e1")
            qf = sem("lin_qf")
            qx = sem("lin_qx")
            stk = sem("lin_stk")
            yr = sem("lin_yr")
            bc = sem("lin_bc")
            bcused = sem("lin_bcused")
            s = sem("lin_s")
            scopied = sem("lin_scopied")
            a0 = sem("lin_a0")
            a1 = sem("lin_a1")
            av = sem("lin_av")
            ocopied = sem("lin_ocopied")
            pt = sem("lin_pt")
            ptused = sem("lin_ptused")
            yo = sem("lin_yo")
            yoT = sem("lin_yoT")
            yoc = sem("lin_yoc")
            wo = sem("lin_wo")
            hr = sem("lin_hr")
            var2 = sem("lin_var2")
            rstd2 = sem("lin_rstd2")
            hn = sem("lin_hn")
            hg = sem("lin_hg")
            xd = sem("lin_xd")

        class A:
            ready = sem("heads_ready")
            vzero = sem("heads_vzero")
            ones = sem("heads_ones")
            link_ln = sem("heads_link_ln")
            link_m = sem("heads_link_m")
            link_n = sem("heads_link_n")
            link_z = sem("heads_link_z")
            var = sem("heads_var")
            rstd = sem("heads_rstd")
            norm = sem("heads_norm")
            turned = sem("heads_turned")
            copied = sem("heads_copied")
            q = sem("heads_q")
            k = sem("heads_k")
            v = sem("heads_v")
            qev = sem("heads_qev")
            kev = sem("heads_kev")
            vev = sem("heads_vev")
            vcopied = sem("heads_vcopied")
            hi = sem("heads_hi")
            r1 = sem("heads_r1")
            mid = sem("heads_mid")
            parts = sem("heads_parts")
            scr = sem("heads_scr")
            qkl0 = sem("heads_qkl0")
            qkl1 = sem("heads_qkl1")
            m0T = sem("heads_m0T")
            m1T = sem("heads_m1T")
            m0ev = sem("heads_m0ev")
            m1ev = sem("heads_m1ev")
            mwr0 = sem("heads_mwr0")
            mwr1 = sem("heads_mwr1")
            ml0 = sem("heads_ml0")
            ml1 = sem("heads_ml1")
            mx = sem("heads_mx")
            red = sem("heads_red")
            s = sem("heads_s")
            e = sem("heads_e")
            pv = sem("heads_pv")
            ocopied = sem("heads_ocopied")
            pt = sem("heads_pt")
            norm1 = sem("heads_norm1")
            anT = sem("heads_anT")
            anc = sem("heads_anc")
            wo = sem("heads_wo")
            yr = sem("heads_yr")
            z = sem("heads_z")
            var2 = sem("heads_var2")
            rstd2 = sem("heads_rstd2")
            zn = sem("heads_zn")
            zg = sem("heads_zg")
            x1 = sem("heads_x1")

        class E:
            link_key = sem("exp_link_key")
            link_ln = sem("exp_link_ln")
            xs = sem("exp_xs")
            turned = sem("exp_turned")
            xt = sem("exp_xt")
            h = sem("exp_h")
            relu = sem("exp_relu")
            y = sem("exp_y")
            yused = sem("exp_yused")
            mask = sem("exp_mask")
            acc = sem("exp_acc")
            var = sem("exp_var")
            rstd = sem("exp_rstd")
            norm = sem("exp_norm")
            g = sem("exp_g")
            b = sem("exp_b")

        class V:
            link_ln = sem("attn_link_ln")
            link_b = sem("attn_link_b")
            var = sem("attn_var")
            rstd = sem("attn_rstd")
            norm = sem("attn_norm")
            turned = sem("attn_turned")
            copied = sem("attn_copied")
            proj = sem("attn_proj")
            biased = sem("attn_biased")
            var12 = sem("attn_var12")
            rstd12 = sem("attn_rstd12")
            norm12 = sem("attn_norm12")
            g = sem("attn_g")
            kqv = sem("attn_kqv")
            kqT = sem("attn_kqT")
            kqc = sem("attn_kqc")
            s = sem("attn_s")
            nmx = sem("attn_nmx")
            e = sem("attn_e")
            pT = sem("attn_pT")
            pc = sem("attn_pc")
            av = sem("attn_av")
            yx = sem("attn_yx")
            sumr = sem("attn_sumr")

        schedule, runs, xp = [], {}, 1
        for name in PHASES:
            schedule.append((name, runs.get(name, 0), xp))
            runs[name] = runs.get(name, 0) + 1
            xp += name != "heads"

        def token_stats(dve, src, st_, mv_, ve_, link, var_sem):
            for t in range(TP):
                last = dve.bn_stats(st_[:, t, :], src(t))
            link(last)
            dve.memset(tick[:, :], 0.0)
            for t in range(TP):
                last = dve.bn_aggr(mv_[:, t, :], st_[:, t, :])
            link(last)
            dve.tensor_scalar(ve_[:, :], mv_[:, :, 1], LN_EPS, None, ALU.add).then_inc(var_sem, 1)

        def token_norm(dve, src, dst, mv_, rs_):
            for t in range(TP):
                last = dve.tensor_scalar(dst(t), src(t), mv_[:, t, 0:1], rs_[:, t:t + 1], ALU.subtract, ALU.mult)
            return last

        def pairs(engine, step):
            with engine.Fori(0, PAIRS // 2) as it:
                step(it)

        def linear_steps(engine, step):
            step(-1, 1, True, False, False)
            step(0, 0, True, True, False)
            with engine.Fori(0, PAIRS // 2 - 1) as it:
                step(it * 2 + 1, 1, True, True, True)
                step(it * 2 + 2, 0, True, True, True)
            step(PAIRS - 1, 1, False, True, True)
            step(PAIRS, 0, False, False, True)

        def heads_steps(engine, step):
            step(-1, 1, True, False, False, False)
            step(0, 0, True, True, False, False)
            step(1, 1, True, True, True, True)
            with engine.Fori(0, PAIRS // 2 - 2) as it:
                step(it * 2 + 2, 0, True, True, True, True, True, True)
                step(it * 2 + 3, 1, True, True, True, True, True, True)
            step(PAIRS - 2, 0, True, True, True, True, True, True)
            step(PAIRS - 1, 1, False, True, True, True, True, True)
            step(PAIRS, 0, False, False, True, True, True, True)
            step(PAIRS + 1, 1, False, False, False, False, True, True)

        def attn_steps(engine, step):
            step(-1, 1, True, False)
            step(0, 0, True, True)
            with engine.Fori(0, PAIRS // 2 - 1) as it:
                step(it * 2 + 1, 1, True, True)
                step(it * 2 + 2, 0, True, True)
            step(PAIRS - 1, 1, False, True)

        def run_phases(engine, phases):
            for name, run, xp in schedule:
                phases[name](run, xp)

        block = ctx.enter_context(nc.Block())

        @block.sync
        def _(sp):
            for n in range(PAIRS):
                sp.dma_start(X[:, TP * n:TP * n + TP, :],
                             x[N * n:N * n + N, :].rearrange("(t p) c -> p t c", p=P)).then_inc(x_loaded, 16)
            sp.dma_start(W[:, :], pack[:, 0:PACKED - HJ * P]).then_inc(w_loaded, 16)
            sp.dma_start(selF, pack[:, PACKED - HJ * P:PACKED]).then_inc(w_loaded, 16)
            sp.dma_start(R[:, :, :].rearrange("p r c -> p (r c)"),
                         rows.partition_broadcast(P)).then_inc(w_loaded, 16)
            for e in range(EXPERTS):
                sp.dma_start(W1[:, e, :], w1[e]).then_inc(w_loaded, 16)
                sp.dma_start(W2[:, e, :, :], w2[e].rearrange("(k p) c -> p k c", p=P)).then_inc(w_loaded, 16)

            def heads(run, xp):
                g8 = 8 * run

                def move_max(n, b, par):
                    written, loaded = (A.mwr0, A.mwr1)[b], (A.ml0, A.ml1)[b]
                    sp.wait_ge((A.m0ev, A.m1ev)[b], n + (g8 + 1))
                    sp.dma_start(scr_m[b].rearrange("s h t -> h s t"), MH[b][:, :, :]).then_inc(written, 16)
                    sp.wait_ge(written, n * 16 + (16 * g8 + 16))
                    for a in range(2):
                        r = 64 * a + SLOTS * D1
                        sp.dma_start(QS[par][r:r + 2, b, :, :],
                                     scr_m[b].rearrange("s (g a) t -> a s g t", a=2)[a]).then_inc(loaded, 16)

                def load_parts(n, b, par):
                    for a in range(2):
                        for scr, dst in ((scr_q, QS), (scr_k, KS)):
                            sp.dma_start(dst[par][64 * a:64 * a + SLOTS * D1, b, :, :].rearrange("p g t -> p (g t)"),
                                         scr[b, :, 64 * a:64 * a + 64, :].rearrange("s (d g) t -> s d (g t)", d=D1)
                                         ).then_inc((A.qkl0, A.qkl1)[b], 16)

                def step(n, par, pre, mx, att, prev, post=False, tail=False):
                    other = 1 - par
                    if prev:
                        move_max(n - 1, 1, other)
                    if pre:
                        sp.wait_ge(A.parts, n * 2 + (2 * g8 + 4))
                        if later(n * 64 + 64 * (g8 + 1)):
                            sp.wait_ge(A.qkl0, n * 64 + 64 * (g8 + 1))
                        if later(n * 64 + 64 * (g8 + 1)):
                            sp.wait_ge(A.qkl1, n * 64 + 64 * (g8 + 1))
                        for b in range(2):
                            h = slice(T * b, T * b + T)
                            for scr, pt, at, src in ((scr_q, PQ[0], 0, (0, 3)), (scr_q, PQ[0], 3, (0, 2)),
                                                     (scr_q, PQ[0], 5, (0, 1)), (scr_k, PQ[1], 0, (0, 0)),
                                                     (scr_k, PQ[1], 3, (1, 1)), (scr_k, PQ[1], 5, (2, 3))):
                                k = SLOTS - at if at == 5 else (3, 2)[at == 3]
                                if src[1] > src[0]:
                                    s = pt[:, src[0]:src[1], h]
                                else:
                                    s = over(pt[:, src[0]:src[0] + 1, h], [P, k, T])
                                sp.dma_start(scr[b, at:at + k].rearrange("s r t -> r s t"), s).then_inc(A.scr, 16)
                        sp.wait_ge(A.scr, n * 192 + 192 * (g8 + 2))
                        if prev:
                            sp.wait_ge(A.s, n * 32 + (32 * g8 - 16))
                        load_parts(n + 1, 0, other)
                    if mx:
                        move_max(n, 0, par)
                    if pre:
                        if prev:
                            sp.wait_ge(A.s, n * 32 + 32 * g8)
                        load_parts(n + 1, 1, other)

                if run == 0:
                    sp.wait_ge(A.ones, 1)
                    for b in range(2):
                        for a in range(2):
                            r = 64 * a + SLOTS * D1
                            sp.dma_start(KS[b][r:r + 2, :, :, :].rearrange("p b g t -> p (b g t)"),
                                         ones[:, :]).then_inc(A.ready, 16)
                heads_steps(sp, step)

            for name, run, xp in schedule:
                if name == "heads":
                    heads(run, xp)
            with sp.Fori(0, PAIRS) as n:
                sp.wait_ge(x_done, n + (8 * schedule[-1][2] + 1))
                sp.dma_start(out[bass.ds(n * N, N), :].rearrange("(t p) c -> p t c", p=P),
                             X[:, bass.ds(n * TP, TP), :]).then_inc(stored, 16)
            sp.wait_ge(stored, 16 * PAIRS)

        @block.gpsimd
        def _(pool):
            def power(var_sem, rstd_sem, count, ve_, rs_):
                pool.wait_ge(var_sem, count)
                pool.tensor_tensor(rs_[:, :], ve_[:, :], half[:, 0:ve_.shape[1]], ALU.pow).then_inc(rstd_sem, 1)

            def ffn(run, xp):
                def step(it):
                    n0 = it * 2
                    for b in range(2):
                        power(F.var, F.rstd, n0 + (8 * run + 1 + b), (ve, ve2)[b], (rs, rs2)[b])
                    for b in range(2):
                        pool.wait_ge(x_done, n0 + (8 * xp - 1 + b))
                        pool.tensor_tensor(XB[b][:, :, :], X[:, bass.ds((n0 + b) * TP, TP), :], row4("qbias"),
                                           ALU.add).then_inc(F.xb, 1)
                pairs(pool, step)

            def linear(run, xp):
                def step(n, par, pre, main, post):
                    if pre:
                        power(L.var, L.rstd, n + 2, ve, rs)
                    for i in range(8):
                        if main:
                            j = n * 8 + i
                            pool.wait_ge(L.bcused, j * 3 + 3)
                            pool.wait_ge(L.scopied, j * 2 + 2)
                            if later(j - 1):
                                pool.wait_ge(L.av, j - 1)
                            s = SS[i % 2][:, 512:768].rearrange("p (h o t) -> p h o t", h=2, o=1)
                            pool.tensor_tensor(A1[i % 2][:, :, :].rearrange("p (h j) t -> p h j t", h=2),
                                               DD1[i % 2][:, :].rearrange("p (h j t) -> p h j t", h=2, j=2),
                                               over(s, [P, 2, 2, P]), ALU.mult).then_inc(L.a1, 1)
                        if post and i == 6:
                            power(L.var2, L.rstd2, n, ve2, rs2)
                    if post:
                        pool.wait_ge(L.hn, n)
                        pool.tensor_tensor(HG[:, :, :], HN[:, :, :], row4("lng"), ALU.mult).then_inc(L.hg, 1)
                        pool.wait_ge(L.hg, n)
                        pool.tensor_tensor(HG[:, :, :], HG[:, :, :], row4("lnb"), ALU.add).then_inc(L.xd, 1)
                    if main:
                        pool.wait_ge(L.norm, n + 1)
                        if later(n):
                            pool.wait_ge(L.hr, n)
                        pool.tensor_tensor(YR0[:, :, :], Y0[par][:, :, :], row4("bout"), ALU.add).then_inc(L.yr, 1)
                linear_steps(pool, step)

            def heads(run, xp):
                g8 = 8 * run

                def step(n, par, pre, mx, att, prev, post=False, tail=False):
                    c = n + g8
                    if pre:
                        power(A.var, A.rstd, c + 2, ve, rs)
                    if mx:
                        pool.wait_ge(A.vev, c + 1)
                        if later(c * 32 - 32):
                            pool.wait_ge(A.pv, c * 32 - 32)
                        bv = over(row("bv").rearrange("p (o h d) -> p o h d", o=1, h=H1), [P, TP, H1, D1])
                        pool.tensor_tensor(V1[par][:, :, :, 0:D1],
                                           VS[:, :, :].rearrange("p t (h d) -> p t h d", h=H1), bv,
                                           ALU.add).then_inc(A.vcopied, 1)
                    if pre:
                        for h in range(2):
                            pool.wait_ge(A.hi, c * 2 + (3 + h))
                            pool.tensor_tensor(qkr[h][:, :], qk32[h][:, :], PQ[h][:, 0, :],
                                               ALU.subtract).then_inc(A.r1, 1)
                    if post:
                        power(A.var2, A.rstd2, c - 1, ve2, rs2)
                    if pre:
                        for h in range(2):
                            pool.wait_ge(A.mid, c * 2 + (3 + h))
                            pool.tensor_tensor(PQ[h][:, 2, :], qkr[h][:, :], PQ[h][:, 1, :],
                                               ALU.subtract).then_inc(A.parts, 1)
                    if post:
                        pool.wait_ge(A.zn, c - 1)
                        pool.tensor_tensor(ZG[:, :, :], ZN[:, :, :], row4("ln1g"), ALU.mult).then_inc(A.zg, 1)
                        pool.wait_ge(A.zg, c - 1)
                        pool.tensor_tensor(X1[:, bass.ds((n - 2) * TP, TP), :], ZG[:, :, :], row4("ln1b"),
                                           ALU.add).then_inc(A.x1, 1)
                    if mx:
                        pool.wait_ge(A.norm, c + 1)
                        if later(c - 1):
                            pool.wait_ge(A.z, c - 1)
                        pool.tensor_tensor(YR1[par][:, :, :], Y1[par][:, :, :], row4("bo"), ALU.add).then_inc(A.yr, 1)

                if run == 0:
                    pool.wait_ge(x_done, 8 * xp)
                    pool.memset(ones[:, :], 1.0).then_inc(A.ones, 1)
                    for b in range(2):
                        pool.memset(V1[b][:, :, :, :], 0.0).then_inc(A.vzero, 1)
                    pool.wait_ge(A.vzero, 2)
                    for b in range(2):
                        pool.memset(V1[b][:, :, :, D1:D1 + 1], 1.0).then_inc(A.vzero, 1)
                    pool.wait_ge(A.vzero, 4)
                heads_steps(pool, step)

            def experts(run, xp):
                def step(n, par, pre, main, post):
                    if post:
                        c = n + 8 * run
                        power(E.var, E.rstd, c, ve, rs)
                        pool.wait_ge(E.norm, c)
                        pool.tensor_tensor(EG[:, :, :], EN[:, :, :], row4("ln2g"), ALU.mult).then_inc(E.g, 1)
                        pool.wait_ge(E.g, c)
                        pool.tensor_tensor(EG[:, :, :], EG[:, :, :], row4("ln2b"), ALU.add).then_inc(E.b, 1)
                linear_steps(pool, step)

            def attn(run, xp):
                def rows3(name):
                    k = ROW[name]
                    return over(R[:, k:k + 3, :].rearrange("p (o k) c -> p o (k c)", o=1), [P, TP, 3 * P])

                def step(n, par, pre, main):
                    other = 1 - par
                    if pre:
                        power(V.var, V.rstd, n + 2, ve, rs)
                    if main:
                        pool.wait_ge(V.norm, n + 1)
                        pool.wait_ge(x_done, n + 8 * xp)
                        pool.tensor_tensor(YX[:, :, :], YV[par][:, :, :], X[:, bass.ds(n * TP, TP), :],
                                           ALU.add).then_inc(V.yx, 1)
                    if pre:
                        pool.wait_ge(V.var12, n + 2)
                        pool.tensor_tensor(rs12[:, :], ve12[:, :], half12[:, :], ALU.pow).then_inc(V.rstd12, 1)
                        pool.wait_ge(V.norm12, n + 2)
                        w = KQV[other][:, :, :, :].rearrange("p t k c -> p t (k c)")
                        pool.tensor_tensor(w, w, rows3("agk"), ALU.mult).then_inc(V.g, 1)
                        pool.wait_ge(V.g, n + 2)
                        pool.tensor_tensor(w, w, rows3("aek"), ALU.add).then_inc(V.kqv, 1)
                attn_steps(pool, step)

            pool.memset(half12[:, :], -0.5).then_inc(consts_done, 1)
            pool.memset(half[:, :], -0.5).then_inc(consts_done, 1)
            for b in range(2):
                pool.memset(VG[b][:, :, :, :], 0.0).then_inc(consts_done, 1)
            pool.wait_ge(consts_done, 4)
            pool.wait_ge(w_loaded, 16 * LOADS)
            pool.wait_ge(setup_done, 1)
            run_phases(pool, {"ffn": ffn, "linear": linear, "heads": heads, "experts": experts, "attn": attn})

        @block.scalar
        def _(act):
            def ffn(run, xp):
                def step(it):
                    n0 = it * 2
                    for b in range(2):
                        act.wait_ge(F.turned, n0 + (8 * run + 1 + b))
                        act.activation(FYT[b][:, :], bank[b][:, :], ACT.Copy).then_inc(F.copied, 1)
                pairs(act, step)

            def linear(run, xp):
                hmask = wt("hmask")

                def step(n, par, pre, main, post):
                    other = 1 - par
                    for i in range(8):
                        if main:
                            j = n * 8 + i
                            if later(j - 1):
                                act.wait_ge(L.a0, j - 1)
                            if later(j - 1):
                                act.wait_ge(L.a1, j - 1)
                            act.wait_ge(L.s, j * 2 + 1)
                            act.activation(SS[i % 2][:, 0:512], bank[2][:, :], ACT.Copy).then_inc(L.scopied, 1)
                            act.wait_ge(L.s, j * 2 + 2)
                            act.activation(SS[i % 2][:, 512:768], bank[3][:, 0:T], ACT.Copy).then_inc(L.scopied, 1)
                        if (i == 0 and post) or (i == 4 and main):
                            done = n * 2 + i // 4 - 1
                            act.wait_ge(L.av, done * 4 + 4)
                            if i == 4:
                                if later(done * 2 - 2):
                                    act.wait_ge(L.pt, done * 2 - 2)
                            for h in range(2):
                                act.activation(OT0[1 - i // 4][:, 2 * h:2 * h + 2, :],
                                               bank[4 + h][:, :].rearrange("p (r t) -> p r t", r=2),
                                               ACT.Copy).then_inc(L.ocopied, 1)
                        if pre and i == 2:
                            act.wait_ge(L.turned, n + 2)
                            if later(n + 1):
                                act.wait_ge(L.vmg, n + 1)
                            act.activation(YT0[:, :], bank[6][:, :], ACT.Copy).then_inc(L.copied, 1)
                        if pre and i == 3:
                            if later(n + 1):
                                act.wait_ge(L.qf, n + 1)
                            for h, b in ((0, 7), (1, 6)):
                                act.wait_ge(L.qk, n * 2 + (3 + h))
                                act.activation(ex[:, h, :], bank[b][:, :], ACT.Exp).then_inc(L.exp4, 1)
                                act.activation(re[:, h, :], bank[b][:, :], ACT.Relu).then_inc(L.exp4, 1)
                        if i == 4:
                            if pre:
                                act.wait_ge(L.beta, n + 2)
                                if later(n + 1):
                                    act.wait_ge(L.stk, n + 1)
                                act.activation(b1r[:, :], bank[7][:, :], ACT.Exp, bias=nbb[:, 0:1],
                                               scale=-1.0).then_inc(L.ebeta, 1)
                            if post:
                                act.wait_ge(L.yoT, n)
                                act.activation(YOT[:, :], bank[6][:, :], ACT.Copy).then_inc(L.yoc, 1)
                        if pre and i in (5, 6):
                            act.wait_ge(L.qf, n + 2)
                            for h in range(4 * (i - 5), 4 * (i - 5) + 4):
                                act.activation(QX[other][:, :, h, :], qf[:, :].rearrange("p (b t) -> p b t", b=2),
                                               ACT.Copy, scale=hmask[:, h:h + 1]).then_inc(L.qx, 1)
                        if pre and i == 7:
                            act.wait_ge(L.e0, n + 2)
                            act.activation(E1[:, :, :], E0[:, :, :], ACT.Exp).then_inc(L.e1, 1)
                linear_steps(act, step)

            def heads(run, xp):
                g8 = 8 * run

                def step(n, par, pre, mx, att, prev, post=False, tail=False):
                    c = n + g8
                    for i in range(32):
                        b, s = i // 16, i % 16
                        if att:
                            q = c * 32 + (i - 32)
                            act.wait_ge(A.s, q + 1)
                            if later(q - 3):
                                act.wait_ge(A.pv, q - 3)
                            act.activation(PB[i % 4][:, :, :], bank[i % 2][:, :].rearrange("p (k t) -> p k t", k=2),
                                           ACT.Exp).then_inc(A.e, 1)
                        if (i == 1 and tail) or (i == 17 and att):
                            blk = c * 2 + (-3 if i == 1 else -2)
                            act.wait_ge(A.pv, blk * 16 + 16)
                            if i == 17:
                                if later(blk * 2 - 2):
                                    act.wait_ge(A.pt, blk * 2 - 2)
                            for h in range(2):
                                act.activation(OT1[1 if i == 1 else 0][:, 2 * h:2 * h + 2, :],
                                               bank[4 + h][:, :].rearrange("p (r t) -> p r t", r=2),
                                               ACT.Copy).then_inc(A.ocopied, 1)
                        if pre and i == 8:
                            act.wait_ge(A.turned, c + 2)
                            if later(c + 1):
                                act.wait_ge(A.v, c + 1)
                            act.activation(YT1[:, :], bank[6][:, :], ACT.Copy).then_inc(A.copied, 1)
                        if post and i == 9:
                            act.wait_ge(A.anT, c - 1)
                            act.activation(ANT[:, :], bank[7][:, :], ACT.Copy).then_inc(A.anc, 1)
                        if pre and i == 13:
                            act.wait_ge(A.k, c + 2)
                            if later(c * 2 + 2):
                                act.wait_ge(A.parts, c * 2 + 2)
                            act.activation(qk32[1][:, :], bank[6][:, :], ACT.Identity,
                                           bias=wt("bk")[:, 0:1]).then_inc(A.kev, 1)
                        if pre and i == 15:
                            act.wait_ge(A.v, c + 2)
                            if later(c + 1):
                                act.wait_ge(A.vcopied, c + 1)
                            act.activation(VS[:, :, :], tiles(7), ACT.Copy).then_inc(A.vev, 1)
                heads_steps(act, step)

            def experts(run, xp):
                def load(n, par):
                    c = n + 8 * run
                    act.wait_ge(A.x1, c + 1)
                    if later(c * 4 - 7):
                        act.wait_ge(E.acc, c * 4 - 7)
                    act.activation(XS[par][:, :, :], X1[:, bass.ds(n * TP, TP), :], ACT.Copy).then_inc(E.xs, 1)

                def step(n, par, pre, main, post):
                    c = n + 8 * run
                    other = 1 - par
                    if pre:
                        load(n + 1, other)
                    for e in range(EXPERTS):
                        for k in range(CH):
                            if main:
                                u = c * 16 + (4 * e + k)
                                act.wait_ge(E.h, u + 1)
                                if later(c * 4 + (e - 1)):
                                    act.wait_ge(E.y, c * 4 + (e - 1))
                                b0 = PACK["b1"][0] + CH * e + k
                                act.activation(HB[e % 2][:, k, :], bank[k][:, :], ACT.Relu,
                                               bias=W[:, b0:b0 + 1]).then_inc(E.relu, 1)
                        if pre and e == 1:
                            act.wait_ge(E.turned, c + 2)
                            act.activation(XT[other][:, :], bank[6][:, :], ACT.Copy).then_inc(E.xt, 1)
                linear_steps(act, step)

            def attn(run, xp):
                def step(n, par, pre, main):
                    if main:
                        for h in range(2):
                            act.wait_ge(V.kqT, n * 2 + (1 + h))
                            act.activation(kqT[h][:, :], bank[3 + h][:, :], ACT.Copy).then_inc(V.kqc, 1)
                    if pre:
                        act.wait_ge(V.turned, n + 2)
                        if later(n * 4 + 4):
                            act.wait_ge(V.proj, n * 4 + 4)
                        act.activation(YVT[:, :], bank[0][:, :], ACT.Copy).then_inc(V.copied, 1)
                    if main:
                        for t in range(TP):
                            act.wait_ge(V.nmx, n * 2 + (1 + t // 2))
                            if later(n):
                                act.wait_ge(V.sumr, n)
                            act.activation(PA[:, t, :], bank[5 + t // 2][:, (t % 2) * T:(t % 2) * T + T], ACT.Exp,
                                           bias=nmx[:, t:t + 1], accum_out=esum[:, t:t + 1]).then_inc(V.e, 1)
                        for u in range(2):
                            act.wait_ge(V.pT, n * 2 + (1 + u))
                            act.activation(PAT[u][:, :], bank[3 + u][:, :], ACT.Copy).then_inc(V.pc, 1)
                attn_steps(act, step)

            act.wait_ge(w_loaded, 16 * LOADS)
            act.wait_ge(setup_done, 1)
            run_phases(act, {"ffn": ffn, "linear": linear, "heads": heads, "experts": experts, "attn": attn})

        @block.tensor
        def _(pe):
            ident = wt("ident")

            def ffn(run, xp):
                def step(it):
                    n0 = it * 2
                    for b in range(2):
                        pe.wait_ge(F.norm, n0 + (8 * run + 1 + b))
                        for t in range(TP):
                            last = pe.transpose(bank[b][:, t * P:(t + 1) * P], FY[b][:, t, :], ident)
                        last.then_inc(F.turned, 1)
                    for b in range(2):
                        pe.wait_ge(F.copied, n0 + (8 * run + 1 + b))
                        pe.wait_ge(x_done, n0 + (8 * xp - 1 + b))
                        for t in range(TP):
                            last = pe.matmul(bank[2 + b][:, t * P:(t + 1) * P], FYT[b][:, t * P:(t + 1) * P],
                                             wt("cbt"), start=True, stop=True)
                        last.then_inc(F.mm, 1)
                pairs(pe, step)

            def linear(run, xp):
                vm0 = PACK["vmg"][0]

                def sums(j, seq, par, s):
                    b = s // 4
                    s %= 4
                    pe.wait_ge(L.a0, j + 1)
                    pe.wait_ge(L.a1, j + 1)
                    if s % 2 == 0:
                        if later(seq * 2 + (s // 2 - 1)):
                            pe.wait_ge(L.ocopied, seq * 2 + (s // 2 - 1))
                    for c in range(4):
                        o = bank[4 + s // 2][32 * c:32 * c + 32, (s % 2) * T:(s % 2) * T + T]
                        v = VG[par]
                        pe.matmul(o, v[:, 2 * b, 2 * s + c // 2, :], A0[s % 2][:, c, :], start=True, stop=False)
                        last = pe.matmul(o[:, P:T], v[:, 2 * b + 1, 2 * s + c // 2, :], A1[s % 2][:, c, :],
                                         start=False, stop=True)
                    last.then_inc(L.av, 1)

                def step(n, par, pre, main, post):
                    other = 1 - par
                    for i in range(8):
                        b, s = i // 4, i % 4
                        j = n * 8 + i
                        if main:
                            if i == 0:
                                pe.wait_ge(L.stk, n + 1)
                                pe.wait_ge(L.qx, n * 8 + 8)
                                pe.wait_ge(L.v_used, n + 1)
                            for c in range(3):
                                if later(j * 3 + (c - 1)):
                                    pe.wait_ge(L.bcused, j * 3 + (c - 1))
                                for k in range(2 if c < 2 else 4):
                                    hj = 4 * s + 2 * c + k if c < 2 else 4 * s + k
                                    o, w = (k * T, T) if c < 2 else (k * P, P)
                                    last = pe.matmul(bank[(3 * i + c) % 2][:, o:o + w], SEL[:, hj, :],
                                                     STK[par][:, b, 0:T] if c < 2 else STK[par][:, b, T:T + P],
                                                     start=True, stop=True)
                                last.then_inc(L.bc, 1)
                            if later(j * 2 - 1):
                                pe.wait_ge(L.scopied, j * 2 - 1)
                            q = QX[par][:, b, 2 * s:2 * s + 2, :]
                            pe.matmul(bank[2][:, :], kT[par][:, b * T:b * T + P], q, start=True,
                                      stop=True).then_inc(L.s, 1)
                            if later(j * 2):
                                pe.wait_ge(L.scopied, j * 2)
                            pe.matmul(bank[3][:, 0:T], kT[par][:, b * T + P:b * T + T], q[:, :, P:T], start=True,
                                      stop=True).then_inc(L.s, 1)
                        if (i == 0 and post) or (i > 0 and main):
                            sums(j - 1, n * 2 + ((i - 1) // 4), par if i else other, (i - 1) % 8)
                        if post and i in (0, 1):
                            for t in (2 * i, 2 * i + 1):
                                pe.wait_ge(L.ocopied, n * 4 + (2 * i - 2))
                                if t >= 2:
                                    pe.wait_ge(L.ptused, n * 4 + (t - 5))
                                elif main:
                                    pe.wait_ge(L.v_used, n + 1)
                                else:
                                    pe.wait_ge(L.hr, n - 1)
                                for r in range(4):
                                    last = pe.transpose(bank[6 + t % 2][:, r * P:(r + 1) * P],
                                                        OT0[i][:, r, (t % 2) * P:(t % 2) * P + P], ident)
                                last.then_inc(L.pt, 1)
                        if pre and i == 2:
                            pe.wait_ge(L.norm, n + 2)
                            if later(n + 1):
                                pe.wait_ge(L.v_used, n + 1)
                            if later(n * 4 - 1):
                                pe.wait_ge(L.ptused, n * 4 - 1)
                            for t in range(TP):
                                last = pe.transpose(bank[6][:, t * P:(t + 1) * P], Y0[other][:, t, :], ident)
                            last.then_inc(L.turned, 1)
                        if pre and i == 3:
                            pe.wait_ge(L.copied, n + 2)
                            if later(n * 4):
                                pe.wait_ge(L.ptused, n * 4)
                            pe.matmul(bank[7][:, :], wt("q0"), YT0[:, :], start=True, stop=True).then_inc(L.qk, 1)
                            pe.matmul(bank[6][:, :], wt("k0"), YT0[:, :], start=True, stop=True).then_inc(L.qk, 1)
                        if i == 4:
                            if pre:
                                pe.wait_ge(L.exp4, n * 4 + 6)
                                pe.matmul(bank[7][:, :], wt("beta"), YT0[:, :], start=True,
                                          stop=True).then_inc(L.beta, 1)
                            if post:
                                if pre:
                                    pe.wait_ge(L.exp4, n * 4 + 8)
                                pe.wait_ge(L.yo, n * 4)
                                for t in range(TP):
                                    last = pe.transpose(bank[6][:, t * P:(t + 1) * P], YO[:, t, :], ident)
                                last.then_inc(L.yoT, 1)
                        if post and i == 5:
                            if pre:
                                pe.wait_ge(L.ebeta, n + 2)
                            pe.wait_ge(L.yoc, n)
                            for t in range(TP):
                                last = pe.matmul(bank[7][:, t * P:(t + 1) * P], YOT[:, t * P:(t + 1) * P],
                                                 wt("out0"), start=True, stop=True)
                            last.then_inc(L.wo, 1)
                        if pre and i == 6:
                            if not post:
                                pe.wait_ge(L.exp4, n * 4 + 8)
                                pe.wait_ge(L.ebeta, n + 2)
                            if later(n):
                                pe.wait_ge(L.hr, n)
                            for t in range(TP):
                                last = pe.matmul(bank[6 + t // 2][:, (t % 2) * T:(t % 2) * T + 152],
                                                 YT0[:, t * P:(t + 1) * P], W[:, vm0:vm0 + 152],
                                                 start=True, stop=True)
                            last.then_inc(L.vmg, 1)

                linear_steps(pe, step)

            def heads(run, xp):
                g8 = 8 * run

                def rows_of(s):
                    return s % 2, s // 2

                def weigh(q, par, seq, b, s):
                    pe.wait_ge(A.e, q + 1)
                    if s % 8 == 0:
                        if later(seq * 2 + (s // 8 - 1)):
                            pe.wait_ge(A.ocopied, seq * 2 + (s // 8 - 1))
                    o = bank[4 + s // 8][32 * (s % 4):32 * (s % 4) + 32, (s // 4 % 2) * T:(s // 4 % 2) * T + T]
                    for kt in range(2):
                        last = pe.matmul(o, V1[par][:, 2 * b + kt, s, :], PB[s % 4][:, kt, :],
                                         start=(kt == 0), stop=(kt == 1))
                    last.then_inc(A.pv, 1)

                def step(n, par, pre, mx, att, prev, post=False, tail=False):
                    c = n + g8
                    other = 1 - par
                    for i in range(32):
                        b, s = i // 16, i % 16
                        q = c * 32 + (i - 32)
                        if att:
                            a, g = rows_of(s)
                            if later(q - 1):
                                pe.wait_ge(A.e, q - 1)
                            if s == 0:
                                pe.wait_ge((A.ml0, A.ml1)[b], c * 32)
                                pe.wait_ge(A.vcopied, c)
                            for kt in range(2):
                                last = pe.matmul(bank[i % 2][:, kt * T:(kt + 1) * T],
                                                 KS[other][64 * a:64 * a + KROWS, b, g, kt * P:(kt + 1) * P],
                                                 QS[other][64 * a:64 * a + KROWS, b, g, :], start=True, stop=True)
                            last.then_inc(A.s, 1)
                        if mx:
                            qt, a, g = s // 8, s % 2, s % 8 // 2 * 2
                            if later(c * 32 + (i - 1)):
                                pe.wait_ge(A.red, c * 32 + (i - 1))
                            if s == 0:
                                pe.wait_ge((A.qkl0, A.qkl1)[b], c * 64 + 64)
                            for u in range(2):
                                r = slice(64 * a, 64 * a + SLOTS * D1)
                                last = pe.matmul(bank[2 + i % 2][:, u * T:(u + 1) * T],
                                                 QS[par][r, b, g + u, qt * P:(qt + 1) * P],
                                                 KS[par][r, b, g + u, :], start=True, stop=True)
                            last.then_inc(A.mx, 1)
                        if (i < 2 and tail) or (i >= 2 and att):
                            s2 = (i - 2) % 16
                            if i < 2:
                                weigh(q - 2, par, c * 2 - 3, 1, s2)
                            else:
                                weigh(q - 2, other, c * 2 + ((i - 2) // 16 - 2), (i - 2) // 16, s2)
                        if prev and i == 1:
                            pe.wait_ge(A.red, c * 32)
                            pe.wait_ge(A.vev, c + 1 if pre or n < PAIRS - 1 else 8 + g8)
                            if not mx:
                                pe.wait_ge(A.z, c - 2)
                            for t in range(2):
                                last = pe.transpose(bank[7][0:H1, t * P:(t + 1) * P], NM[:, 2 + t, :], ident)
                            last.then_inc(A.m1T, 1)
                        if post and 2 <= i < 6:
                            t = i - 2
                            if t >= 2 or not prev:
                                pe.wait_ge(A.norm1, c * 4 + (t - 9))
                            pe.wait_ge(A.ocopied, c * 4 + (2 * (t // 2) - 6))
                            pe.wait_ge((A.m0ev, A.m1ev)[t % 2], c if prev else 8 + g8)
                            if not prev:
                                pe.wait_ge(A.z, c - 2)
                            for r in range(4):
                                last = pe.transpose(bank[6 + t % 2][:, r * P:(r + 1) * P],
                                                    OT1[t // 2][:, r, (t % 2) * P:(t % 2) * P + P], ident)
                            last.then_inc(A.pt, 1)
                        if pre and i == 7:
                            pe.wait_ge(A.norm, c + 2)
                            if later(c * 4 - 5):
                                pe.wait_ge(A.norm1, c * 4 - 5)
                            if prev:
                                pe.wait_ge(A.m0ev, c)
                            if later(c + 1):
                                pe.wait_ge(A.kev, c + 1)
                            for t in range(TP):
                                last = pe.transpose(bank[6][:, t * P:(t + 1) * P], Y1[other][:, t, :], ident)
                            last.then_inc(A.turned, 1)
                        if post and i == 8:
                            pe.wait_ge(A.norm1, c * 4 - 4)
                            for t in range(TP):
                                last = pe.transpose(bank[7][:, t * P:(t + 1) * P], AN[:, t, :], ident)
                            last.then_inc(A.anT, 1)
                        if pre and i == 10:
                            pe.wait_ge(A.copied, c + 2)
                            pe.matmul(bank[6][:, :], wt("q1"), YT1[:, :], start=True, stop=True).then_inc(A.q, 1)
                        if post and i == 11:
                            pe.wait_ge(A.anc, c - 1)
                            for t in range(TP):
                                last = pe.matmul(bank[7][:, t * P:(t + 1) * P], ANT[:, t * P:(t + 1) * P],
                                                 wt("o1"), start=True, stop=True)
                            last.then_inc(A.wo, 1)
                        if pre and i == 12:
                            pe.wait_ge(A.qev, c + 2)
                            pe.matmul(bank[6][:, :], wt("k1"), YT1[:, :], start=True, stop=True).then_inc(A.k, 1)
                        if pre and i == 14:
                            if later(c - 1):
                                pe.wait_ge(A.z, c - 1)
                            if prev:
                                pe.wait_ge(A.m1ev, c)
                            if later(c + 1):
                                pe.wait_ge(A.vev, c + 1)
                            for t in range(TP):
                                last = pe.matmul(bank[7][:, t * P:(t + 1) * P], YT1[:, t * P:(t + 1) * P],
                                                 wt("v1"), start=True, stop=True)
                            last.then_inc(A.v, 1)
                        if mx and i == 18:
                            pe.wait_ge(A.red, c * 32 + 16)
                            if pre:
                                pe.wait_ge(A.kev, c + 2)
                            if later(c * 4 - 5):
                                pe.wait_ge(A.norm1, c * 4 - 5)
                            for t in range(2):
                                last = pe.transpose(bank[6][0:H1, t * P:(t + 1) * P], NM[:, t, :], ident)
                            last.then_inc(A.m0T, 1)

                pe.wait_ge(x_done, 8 * xp)
                if run == 0:
                    pe.wait_ge(A.ready, 64)
                heads_steps(pe, step)

            def experts(run, xp):
                def step(n, par, pre, main, post):
                    c = n + 8 * run
                    other = 1 - par
                    for e in range(EXPERTS):
                        if main:
                            if e == 0:
                                pe.wait_ge(E.xt, c + 1)
                            for k in range(CH):
                                if later(c * 16 + (4 * e + k - 3)):
                                    pe.wait_ge(E.relu, c * 16 + (4 * e + k - 3))
                                pe.matmul(bank[k][:, :], W1[:, e, k * P:(k + 1) * P], XT[par][:, :],
                                          start=True, stop=True).then_inc(E.h, 1)
                        if (e and main) or (e == 0 and post):
                            d = (e - 1) % 4
                            pe.wait_ge(E.relu, c * 16 + 4 * e)
                            if later(c * 4 + (e - 2)):
                                pe.wait_ge(E.yused, c * 4 + (e - 2))
                            for t in range(TP):
                                for k in range(CH):
                                    last = pe.matmul(bank[4 + d % 2][:, t * P:(t + 1) * P],
                                                     HB[d % 2][:, k, t * P:(t + 1) * P], W2[:, d, k, :],
                                                     start=(k == 0), stop=(k == CH - 1))
                            last.then_inc(E.y, 1)
                        if pre and e == 1:
                            pe.wait_ge(E.xs, c + 2)
                            for t in range(TP):
                                last = pe.transpose(bank[6][:, t * P:(t + 1) * P], XS[other][:, t, :], ident)
                            last.then_inc(E.turned, 1)
                pe.wait_ge(A.x1, 8 * run + 8)
                linear_steps(pe, step)

            def attn(run, xp):
                def step(n, par, pre, main):
                    other = 1 - par
                    if main:
                        pe.wait_ge(V.kqv, n + 1)
                        for h in range(2):
                            for t in range(TP):
                                last = pe.transpose(bank[3 + h][:, t * P:(t + 1) * P], KQV[par][:, t, h, :], ident)
                            last.then_inc(V.kqT, 1)
                    if main:
                        pe.wait_ge(V.kqc, n * 2 + 2)
                        for t in range(TP):
                            last = pe.matmul(bank[5 + t // 2][:, (t % 2) * T:(t % 2) * T + T],
                                             kqT[0][:, t * P:(t + 1) * P],
                                             kqT[1][:, (t // 2) * T:(t // 2) * T + T], start=True, stop=True)
                            if t % 2:
                                last.then_inc(V.s, 1)
                    if pre:
                        pe.wait_ge(V.norm, n + 2)
                        for t in range(TP):
                            last = pe.transpose(bank[0][:, t * P:(t + 1) * P], YV[other][:, t, :], ident)
                        last.then_inc(V.turned, 1)
                    if pre:
                        pe.wait_ge(V.copied, n + 2)
                        a0 = PACK["kqv"][0]
                        for t in range(TP):
                            if later(n * 4 + (t + 3)):
                                pe.wait_ge(V.biased, n * 4 + (t + 3))
                            pe.matmul(bank[1 + t % 2][:, 0:3 * P], YVT[:, t * P:(t + 1) * P], W[:, a0:a0 + 3 * P],
                                      start=True, stop=True).then_inc(V.proj, 1)
                    if main:
                        pe.wait_ge(V.e, n * 4 + 4)
                        for u in range(2):
                            for t in range(TP):
                                last = pe.transpose(bank[3 + u][:, t * P:(t + 1) * P], PA[:, t, u * P:(u + 1) * P],
                                                    ident)
                            last.then_inc(V.pT, 1)
                        pe.wait_ge(V.pc, n * 2 + 2)
                        pe.wait_ge(x_done, n + 8 * xp)
                        for t in range(TP):
                            for u in range(2):
                                last = pe.matmul(bank[7][:, t * P:(t + 1) * P], PAT[u][:, t * P:(t + 1) * P],
                                                 KQV[par][:, 2 * (t // 2) + u, 2, :], start=(u == 0), stop=(u == 1))
                        last.then_inc(V.av, 1)
                pe.wait_ge(x_done, 8 * xp)
                attn_steps(pe, step)

            pe.wait_ge(w_loaded, 16 * LOADS)
            pe.wait_ge(setup_done, 1)
            run_phases(pe, {"ffn": ffn, "linear": linear, "heads": heads, "experts": experts, "attn": attn})

        @block.vector
        def _(dve):
            def xs(n):
                return lambda t: X[:, bass.ds(n * TP + t, 1), :].rearrange("p o c -> p (o c)")

            def ffn(run, xp):
                def step(it):
                    n0 = it * 2
                    link = Link(dve, F.link, it + 4 * run, 4)
                    for b in range(2):
                        dve.wait_ge(x_done, n0 + (8 * xp - 7 + b))
                        token_stats(dve, xs(n0 + b), (st, st2)[b], (mv, mv2)[b], (ve, ve2)[b], link, F.var)
                    for b in range(2):
                        dve.wait_ge(F.rstd, n0 + (8 * run + 1 + b))
                        token_norm(dve, xs(n0 + b), lambda t, b=b: FY[b][:, t, :], (mv, mv2)[b],
                                   (rs, rs2)[b]).then_inc(F.norm, 1)
                    for b in range(2):
                        dve.wait_ge(F.mm, n0 + (8 * run + 1 + b))
                        dve.wait_ge(F.xb, n0 + (8 * run + 1 + b))
                        dve.tensor_tensor(X[:, bass.ds((n0 + b) * TP, TP), :], tiles(2 + b), XB[b][:, :, :],
                                          ALU.add).then_inc(x_done, 1)
                    link.close()
                pairs(dve, step)

            def linear(run, xp):
                def finish_tile(link, n, t, other):
                    ps = bank[6 + t % 2][:, :].rearrange("p (h e) -> p h e", e=32)
                    dve.wait_ge(L.pt, n * 4 + (t - 3))
                    link(dve.tensor_scalar(den[:, :], ps[:, :, D0], DEN_EPS, None, ALU.add))
                    link(dve.reciprocal(rec[:, :], den[:, :]))
                    link(dve.tensor_tensor(rw0[:, :], rec[:, :], WM[other][:, t, :], ALU.mult))
                    dve.tensor_tensor(PR[:, :, :], ps[:, :, 0:D0], over(rw0[:, :].unsqueeze(2), [P, HJ, D0]),
                                      ALU.mult).then_inc(L.ptused, 1)
                    dve.wait_ge(L.ptused, n * 4 + (t - 3))
                    pr = PR[:, :, :].rearrange("p (h j) e -> p h j e", j=J0)
                    dve.tensor_tensor(YO[:, t, :].rearrange("p (h e) -> p h e", e=D0), pr[:, :, 0, :],
                                      pr[:, :, 1, :], ALU.add).then_inc(L.yo, 1)

                def slot(n, i):
                    j = n * 8 + i
                    if later(j - 1):
                        dve.wait_ge(L.a0, j - 1)
                    for c in range(3):
                        dve.wait_ge(L.bc, j * 3 + (c + 1))
                        if c == 2:
                            if later(j - 1):
                                dve.wait_ge(L.a1, j - 1)
                        dst = DD0[i % 2][:, 512 * c:512 * c + 512] if c < 2 else DD1[i % 2][:, :]
                        dve.tensor_tensor_scan(dst, bank[(3 * i + c) % 2][:, :], (I0 if c < 2 else I1)[:, :], 0.0,
                                               ALU.mult, ALU.add).then_inc(L.bcused, 1)
                    dve.wait_ge(L.bcused, j * 3 + 2)
                    dve.wait_ge(L.scopied, j * 2 + 1)
                    if later(j - 1):
                        dve.wait_ge(L.av, j - 1)
                    s = SS[i % 2][:, 0:512].rearrange("p (h o t) -> p h o t", h=2, o=1)
                    dve.tensor_tensor(A0[i % 2][:, :, :].rearrange("p (h j) t -> p h j t", h=2),
                                      DD0[i % 2][:, :].rearrange("p (h j t) -> p h j t", h=2, j=2),
                                      over(s, [P, 2, 2, T]), ALU.mult).then_inc(L.a0, 1)

                def step(n, par, pre, main, post):
                    other = 1 - par
                    if pre:
                        link_ln, link_beta = Link(dve, L.link_ln, n + 1, 2), Link(dve, L.link_beta, n + 1, 9)
                        link_gate = Link(dve, L.link_gate, n + 1, 4)
                    if post:
                        link_post, link_out = Link(dve, L.link_post, n - 1, 12), Link(dve, L.link_out, n - 1, 2)
                    for i in range(8):
                        if pre and i == 0:
                            dve.wait_ge(x_done, n + (8 * xp - 6))
                            token_stats(dve, xs(n + 1), st, mv, ve, link_ln, L.var)
                        if main:
                            slot(n, i)
                        if post and i in (0, 1):
                            for t in (2 * i, 2 * i + 1):
                                finish_tile(link_post, n, t, other)
                        if pre and i == 1:
                            dve.wait_ge(L.rstd, n + 2)
                            if later(n):
                                dve.wait_ge(L.yr, n)
                            token_norm(dve, xs(n + 1), lambda t: Y0[other][:, t, :], mv, rs).then_inc(L.norm, 1)
                        if pre and i == 4:
                            if later(n * 8 + 8):
                                dve.wait_ge(L.qx, n * 8 + 8)
                            dve.wait_ge(L.exp4, n * 4 + 6)
                            dve.scalar_tensor_tensor(out=qf[:, :], in0=ex[:, 0, :], scalar=1.0, in1=re[:, 0, :],
                                                     op0=ALU.min, op1=ALU.add)
                            dve.wait_ge(L.exp4, n * 4 + 8)
                            dve.scalar_tensor_tensor(out=kT[other][:, :], in0=ex[:, 1, :], scalar=1.0,
                                                     in1=re[:, 1, :], op0=ALU.min, op1=ALU.add).then_inc(L.qf, 1)
                        if pre and i == 5:
                            dve.wait_ge(L.ebeta, n + 2)
                            link_beta(dve.tensor_scalar(b2r[:, :], b1r[:, :], 1.0, None, ALU.add))
                            link_beta(dve.reciprocal(bE[:, :], b2r[:, :]))
                            link_beta(dve.tensor_scalar(bE[:, :], bE[:, :], wt("decay")[:, 0:1], 0.9999, ALU.mult,
                                                        ALU.min))
                            sk = STK[other]

                            def two(ap):
                                return ap.rearrange("p (b t) -> p b t", b=2)
                            m, l = BETA_ROWS[1], BETA_ROWS[2]
                            link_beta(dve.tensor_copy(sk[:, :, 0:T], two(bE[:, :])))
                            link_beta(dve.tensor_tensor(two(b1r[m:P, :]), two(bE[m:P, :]), sk[m:P, :, 0:T],
                                                        ALU.subtract))
                            link_beta(dve.tensor_copy(sk[m:P, :, 0:T], two(b1r[m:P, :])))
                            link_beta(dve.tensor_tensor(two(b2r[l:P, :]), two(b1r[l:P, :]), sk[l:P, :, 0:T],
                                                        ALU.subtract))
                            link_beta(dve.tensor_copy(sk[l:P, :, 0:T], two(b2r[l:P, :])))
                            link_beta(dve.tensor_copy(sk[:, :, T:T + P], sk[:, :, P:T]))
                            dve.memset(sk[:, :, 0:T + 1:T], 0.0).then_inc(L.stk, 1)
                            link_beta.close()
                        if post and i == 5:
                            dve.wait_ge(L.wo, n)
                            dve.wait_ge(L.yr, n)
                            dve.tensor_tensor(HR[:, :, :], tiles(7), YR0[:, :, :], ALU.add).then_inc(L.hr, 1)
                            dve.wait_ge(L.hr, n)
                            token_stats(dve, lambda t: HR[:, t, :], st2, mv2, ve2, link_out, L.var2)
                        if post and i == 6:
                            dve.wait_ge(L.rstd2, n)
                            token_norm(dve, lambda t: HR[:, t, :], lambda t: HN[:, t, :], mv2, rs2).then_inc(L.hn, 1)
                        if pre and i == 7:
                            dve.wait_ge(L.vmg, n + 2)
                            for h in range(2):
                                ps = bank[6 + h][:, :].rearrange("p (t c) -> p t c", t=2)[:, :, 128:152]
                                r = ROW["bmg"]
                                last = dve.tensor_tensor(MG[:, 2 * h:2 * h + 2, :], ps,
                                                         over(R[:, r:r + 1, 0:24], [P, 2, 24]), ALU.add)
                            link_gate(last)
                            mix = MG[:, :, 0:HJ].rearrange("p t (h j) -> p t h j", j=J0)
                            link_gate(dve.tensor_tensor(mx[:, :, :], mix[:, :, :, 0], mix[:, :, :, 1], ALU.max))
                            dve.tensor_tensor(E0[:, :, 0:HJ].rearrange("p t (h j) -> p t h j", j=J0), mix,
                                              over(mx[:, :, :].unsqueeze(3), [P, TP, H0, J0]), ALU.subtract)
                            dve.tensor_scalar(E0[:, :, HJ:24], MG[:, :, HJ:24], -1.0, None,
                                              ALU.mult).then_inc(L.e0, 1)
                            dve.wait_ge(L.e1, n + 2)
                            e = E1[:, :, 0:HJ].rearrange("p t (h j) -> p t h j", j=J0)
                            dve.tensor_tensor(SD[:, :, 0:H0], e[:, :, :, 0], e[:, :, :, 1], ALU.add)
                            link_gate(dve.tensor_scalar(SD[:, :, H0:16], E1[:, :, HJ:24], 1.0, None, ALU.add))
                            link_gate(dve.reciprocal(RD[:, :, :], SD[:, :, :]))
                            dve.tensor_tensor(WM[other][:, :, :].rearrange("p t (h j) -> p t h j", j=J0), e,
                                              over(RD[:, :, 0:H0].unsqueeze(3), [P, TP, H0, J0]), ALU.mult)
                            for h in range(2):
                                ps = bank[6 + h][:, :].rearrange("p (t c) -> p t c", t=2)[:, :, 0:P]
                                g = RD[:, 2 * h:2 * h + 2, H0:16]
                                dve.tensor_tensor(VG[other][:, 2 * h:2 * h + 2, :, 0:D0],
                                                  ps.rearrange("p t (h e) -> p t h e", e=D0),
                                                  over(g.unsqueeze(3), [P, 2, H0, D0]), ALU.mult)
                            dve.tensor_copy(VG[other][:, :, :, D0], RD[:, :, H0:16]).then_inc(L.v_used, 1)
                            link_gate.close()
                    if pre:
                        link_ln.close()
                    if post:
                        link_post.close()
                        link_out.close()
                        dve.wait_ge(L.xd, n)
                        at = bass.ds((n - 1) * TP, TP)
                        dve.tensor_tensor(X[:, at, :], X[:, at, :], HG[:, :, :], ALU.add).then_inc(x_done, 1)
                linear_steps(dve, step)

            def heads(run, xp):
                g8 = 8 * run
                SCALE = float(D1) ** -0.5

                def split_max(c, b):
                    index, evacuated, written, free = ((2 * c, A.m0ev, A.mwr0, c), (2 * c + 1, A.m1ev, A.mwr1, c))[b]
                    dve.wait_ge((A.m0T, A.m1T)[b], c + 1)
                    if later(free * 16):
                        dve.wait_ge(written, free * 16)
                    link = Link(dve, A.link_m, index, 1)
                    ps = bank[6 + b][0:H1, 0:T]
                    link(dve.tensor_copy(MH[b][:, 0, :], ps))
                    dve.tensor_tensor(MH[b][:, 1, :], ps, MH[b][:, 0, :], ALU.subtract).then_inc(evacuated, 1)

                def step(n, par, pre, mx, att, prev, post=False, tail=False):
                    c = n + g8
                    other = 1 - par
                    for i in range(32):
                        b, s = i // 16, i % 16
                        if pre and i == 0:
                            link = Link(dve, A.link_ln, c + 1, 2)
                            dve.wait_ge(x_done, n + (8 * xp - 6))
                            token_stats(dve, xs(n + 1), st, mv, ve, link, A.var)
                            link.close()
                        if mx:
                            qt, a, g = s // 8, s % 2, s % 8 // 2 * 2
                            dve.wait_ge(A.mx, c * 32 + (i + 1))
                            h = 2 * g + a
                            dve.tensor_reduce(NM[:, 2 * b + qt, h:h + 3:2],
                                              bank[2 + i % 2][:, :].rearrange("p (u t) -> p u t", u=2), AX_X,
                                              ALU.max, negate=True).then_inc(A.red, 1)
                        if prev and i == 1:
                            split_max(c - 1, 1)
                        if pre and i == 2:
                            dve.wait_ge(A.rstd, c + 2)
                            if later(c):
                                dve.wait_ge(A.yr, c)
                            token_norm(dve, xs(n + 1), lambda t: Y1[other][:, t, :], mv, rs).then_inc(A.norm, 1)
                        if post and 3 <= i < 7:
                            t = i - 3
                            if t == 0:
                                link_n = Link(dve, A.link_n, c - 2, 4)
                            ps = bank[6 + t % 2][:, :].rearrange("p (h e) -> p h e", e=32)
                            dve.wait_ge(A.pt, c * 4 + (t - 7))
                            link_n(dve.reciprocal(rec1[:, t, :], ps[:, :, D1]))
                            dve.tensor_tensor(AN[:, t, :].rearrange("p (h e) -> p h e", e=D1), ps[:, :, 0:D1],
                                              over(rec1[:, t, :].unsqueeze(2), [P, H1, D1]),
                                              ALU.mult).then_inc(A.norm1, 1)
                        if pre and i == 11:
                            dve.wait_ge(A.q, c + 2)
                            if later(c * 2 + 2):
                                dve.wait_ge(A.r1, c * 2 + 2)
                            dve.tensor_scalar(qk32[0][:, :], bank[6][:, :], wt("bq")[:, 0:1], SCALE, ALU.add,
                                              ALU.mult).then_inc(A.qev, 1)
                        if pre and i == 12:
                            dve.wait_ge(A.qev, c + 2)
                            if later(c * 192 + 192):
                                dve.wait_ge(A.scr, c * 192 + 192)
                            dve.tensor_copy(PQ[0][:, 0, :], qk32[0][:, :]).then_inc(A.hi, 1)
                        if post and i == 13:
                            dve.wait_ge(A.wo, c - 1)
                            dve.wait_ge(A.yr, c - 1)
                            dve.tensor_tensor(Z[:, :, :], tiles(7), YR1[par][:, :, :], ALU.add).then_inc(A.z, 1)
                            dve.wait_ge(A.z, c - 1)
                            link = Link(dve, A.link_z, c - 2, 2)
                            token_stats(dve, lambda t: Z[:, t, :], st2, mv2, ve2, link, A.var2)
                            link.close()
                        if pre and i == 14:
                            dve.wait_ge(A.kev, c + 2)
                            dve.tensor_copy(PQ[1][:, 0, :], qk32[1][:, :]).then_inc(A.hi, 1)
                        if pre and i in (16, 17):
                            h = i - 16
                            dve.wait_ge(A.r1, c * 2 + (3 + h))
                            dve.tensor_copy(PQ[h][:, 1, :], qkr[h][:, :]).then_inc(A.mid, 1)
                        if post and i == 18:
                            dve.wait_ge(A.rstd2, c - 1)
                            token_norm(dve, lambda t: Z[:, t, :], lambda t: ZN[:, t, :], mv2, rs2).then_inc(A.zn, 1)
                        if mx and i == 19:
                            split_max(c, 0)
                heads_steps(dve, step)

            def experts(run, xp):
                def gather(n, par, e):
                    c = n + 8 * run
                    if later(c * 4 + e):
                        dve.wait_ge(E.acc, c * 4 + e)
                    dve.wait_ge(E.y, c * 4 + (e + 1))
                    dve.tensor_tensor(YB[:, :, :], tiles(4 + e % 2), row4(f"b2_{e}"), ALU.add).then_inc(E.yused, 1)
                    dve.wait_ge(E.yused, c * 4 + (e + 1))
                    for t in range(TP):
                        last = dve.scalar_tensor_tensor(out=AC[:, t, :], in0=YB[:, t, :],
                                                        scalar=MK[par][:, e, t:t + 1],
                                                        in1=(AC if e else XS[par])[:, t, :], op0=ALU.mult,
                                                        op1=ALU.add)
                    last.then_inc(E.acc, 1)

                def masks(n, par):
                    c = n + 8 * run
                    link = Link(dve, E.link_key, c, 10)
                    dve.wait_ge(E.xs, c + 1)
                    if later(c * 4 - 1):
                        dve.wait_ge(E.acc, c * 4 - 1)
                    link(dve.tensor_tensor(KP[:, :, :], XS[par][:, :, :], row4("rw"), ALU.mult))
                    link(dve.tensor_reduce(key[0][:, :], KP[:, :, :], AX_X, ALU.add))
                    link(dve.tensor_scalar(key[0][:, :], key[0][:, :], row("rb")[:, 0:1], None, ALU.add))
                    link(dve.tensor_copy(kint[:, :], key[0][:, :]))
                    link(dve.tensor_copy(key[1][:, :], kint[:, :]))
                    link(dve.tensor_tensor(key[2][:, :], key[1][:, :], key[0][:, :], ALU.is_gt))
                    link(dve.tensor_tensor(key[1][:, :], key[1][:, :], key[2][:, :], ALU.subtract))
                    link(dve.tensor_copy(kint[:, :], key[1][:, :]))
                    link(dve.tensor_scalar(kint[:, :], kint[:, :], EXPERTS - 1, None, ALU.bitwise_and))
                    link(dve.tensor_copy(key[2][:, :], kint[:, :]))
                    for e in range(EXPERTS):
                        last = dve.tensor_scalar(MK[par][:, e, :], key[2][:, :], float(e), None, ALU.is_equal)
                    last.then_inc(E.mask, 1)
                    link.close()

                def step(n, par, pre, main, post):
                    c = n + 8 * run
                    other = 1 - par
                    if main:
                        masks(n, par)
                    if post:
                        gather(n - 1, other, EXPERTS - 1)
                        dve.wait_ge(E.acc, c * 4)
                        link = Link(dve, E.link_ln, c - 1, 2)
                        token_stats(dve, lambda t: AC[:, t, :], st, mv, ve, link, E.var)
                        link.close()
                        dve.wait_ge(E.rstd, c)
                        token_norm(dve, lambda t: AC[:, t, :], lambda t: EN[:, t, :], mv, rs).then_inc(E.norm, 1)
                    if main:
                        dve.wait_ge(E.mask, c + 1)
                        for e in range(EXPERTS - 1):
                            gather(n, par, e)
                    if post:
                        dve.wait_ge(E.b, c)
                        at = bass.ds((n - 1) * TP, TP)
                        dve.tensor_tensor(X[:, at, :], X[:, at, :], EG[:, :, :], ALU.add).then_inc(x_done, 1)
                linear_steps(dve, step)

            def attn(run, xp):
                def step(n, par, pre, main):
                    other = 1 - par
                    if pre:
                        link = Link(dve, V.link_ln, n + 1, 2)
                        dve.wait_ge(x_done, n + (8 * xp - 6))
                        token_stats(dve, xs(n + 1), st, mv, ve, link, V.var)
                        link.close()
                    if main:
                        for h in range(2):
                            dve.wait_ge(V.s, n * 2 + (1 + h))
                            dve.tensor_reduce(nmx[:, 2 * h:2 * h + 2],
                                              bank[5 + h][:, :].rearrange("p (u t) -> p u t", u=2), AX_X,
                                              ALU.max, negate=True).then_inc(V.nmx, 1)
                    if pre:
                        dve.wait_ge(V.rstd, n + 2)
                        if later(n):
                            dve.wait_ge(V.yx, n)
                        token_norm(dve, xs(n + 1), lambda t: YV[other][:, t, :], mv, rs).then_inc(V.norm, 1)
                        k = ROW["abk"]
                        w = KQV[other]
                        for t in range(TP):
                            dve.wait_ge(V.proj, n * 4 + (t + 5))
                            dve.tensor_tensor(w[:, t, :, :].rearrange("p k c -> p (k c)"), bank[1 + t % 2][:, 0:3 * P],
                                              R[:, k:k + 3, :].rearrange("p k c -> p (k c)"),
                                              ALU.add).then_inc(V.biased, 1)
                        dve.wait_ge(V.biased, n * 4 + 8)
                        link = Link(dve, V.link_b, n + 1, 3)
                        for u in range(12):
                            last = dve.bn_stats(st12[:, u, :], w[:, u // 3, u % 3, :])
                        link(last)
                        dve.tensor_tensor(dif12[:, :], st12[:, :, 1], st12[:, :, 4], ALU.subtract)
                        dve.tensor_tensor(mean12[:, :], st12[:, :, 1], st12[:, :, 4], ALU.add)
                        link(dve.tensor_tensor(var12[:, :], st12[:, :, 2], st12[:, :, 5], ALU.add))
                        dve.tensor_tensor(dif12[:, :], dif12[:, :], dif12[:, :], ALU.mult)
                        dve.tensor_scalar(mean12[:, :], mean12[:, :], 0.5, None, ALU.mult)
                        link(dve.tensor_scalar(var12[:, :], var12[:, :], 1.0 / P, LN_EPS, ALU.mult, ALU.add))
                        dve.scalar_tensor_tensor(out=ve12[:, :], in0=dif12[:, :], scalar=0.25, in1=var12[:, :],
                                                 op0=ALU.mult, op1=ALU.add).then_inc(V.var12, 1)
                        link.close()
                    if main:
                        dve.wait_ge(V.e, n * 4 + 4)
                        dve.reciprocal(rsum[:, :], esum[:, :]).then_inc(V.sumr, 1)
                        dve.wait_ge(V.sumr, n + 1)
                        dve.wait_ge(V.av, n + 1)
                        dve.wait_ge(V.yx, n + 1)
                        for t in range(TP):
                            at = X[:, bass.ds(n * TP + t, 1), :].rearrange("p o c -> p (o c)")
                            last = dve.scalar_tensor_tensor(out=at, in0=bank[7][:, t * P:(t + 1) * P],
                                                            scalar=rsum[:, t:t + 1], in1=YX[:, t, :],
                                                            op0=ALU.mult, op1=ALU.add)
                        last.then_inc(x_done, 1)
                    if pre:
                        dve.wait_ge(V.rstd12, n + 2)
                        for u in range(12):
                            a = w[:, u // 3, u % 3, :]
                            last = dve.tensor_scalar(a, a, mean12[:, u:u + 1], rs12[:, u:u + 1], ALU.subtract, ALU.mult)
                        last.then_inc(V.norm12, 1)
                attn_steps(dve, step)

            dve.wait_ge(w_loaded, 16 * LOADS)
            link = Link(dve, setup_link, 0, 2)
            dve.memset(I0[:, :], 0.0)
            link(dve.tensor_scalar(row("scb"), row("scb"), 0.5 / 127.0, None, ALU.mult))
            for t in (0, 2):
                dve.tensor_copy(I0[:, t * P:(t + 1) * P], wt("ident"))
            for t in range(TP):
                dve.tensor_copy(I1[:, t * P:(t + 1) * P], wt("ident"))
            dve.tensor_tensor(wt("cbt"), wt("cbt"), row("scb"), ALU.mult)
            for name in ("qbias", "ln2g", "ln2b"):
                dve.tensor_scalar(row(name), row(name), 0.5, None, ALU.mult)
            dve.tensor_scalar(nbb[:, :], wt("bbeta"), -1.0, None, ALU.mult)
            link(dve.tensor_copy(SEL[:, :, :].rearrange("p h c -> p (h c)"), selF))
            link.close()
            dve.tensor_copy(rs[:, :], I1[:, 0:TP]).then_inc(setup_done, 1)
            dve.wait_ge(x_loaded, 16 * PAIRS)
            dve.tensor_copy(rs2[:, :], I1[:, 0:TP]).then_inc(x_done, 8)
            run_phases(dve, {"ffn": ffn, "linear": linear, "heads": heads, "experts": experts, "attn": attn})


def _lay_out(a):
    f = np.float32
    g = lambda k: np.asarray(a[k], dtype=f)
    pack = np.zeros((P, PACKED), f)

    def put(name, value):
        at, n = PACK[name]
        pack[:, at:at + n] = np.asarray(value).reshape(P, n)

    put("cbt", g("L0_ffn_CB").T)
    put("q0", g("L0_attn_Wq").T)
    put("k0", g("L0_attn_Wk").T)
    put("vmg", np.concatenate([g("L0_attn_Wv"), g("L0_attn_Wmix"), g("L0_attn_Wgate")], 0).T)
    at = PACK["beta"][0]
    for r in BETA_ROWS:
        pack[:, at + r:at + r + HJ] = g("L0_attn_Wbeta").T
        pack[r:r + HJ, PACK["bbeta"][0]] = g("L0_attn_bbeta")
        slopes = np.array([2.0 ** (-8.0 * (h + 1) / H0) for h in range(H0)], f)
        pack[r:r + HJ, PACK["decay"][0]] = np.repeat(np.exp(-slopes), J0)
    put("out0", g("L0_attn_Wout").T)
    order = np.array([(2 * gg + aa) * D1 + d for aa in range(2) for d in range(D1) for gg in range(H1 // 2)])
    put("q1", g("L1_ffn_Wq")[:, order])
    put("k1", g("L1_ffn_Wk")[:, order])
    put("bq", g("L1_ffn_bq")[order])
    put("bk", g("L1_ffn_bk")[order])
    put("v1", g("L1_ffn_Wv"))
    put("o1", g("L1_ffn_Wo"))
    put("b1", g("L1_ffn_b1").reshape(EXPERTS * CH, P).T)
    put("kqv", np.concatenate([g("L1_attn_Wk"), g("L1_attn_Wq"), g("L1_attn_Wv")], 1))
    put("hmask", (np.arange(P)[:, None] // D0 == np.arange(H0)[None, :]).astype(f))
    put("ident", np.eye(P, dtype=f))
    sel = np.zeros((P, HJ, P), f)
    for r in BETA_ROWS:
        for h in range(HJ):
            sel[r + h, h, :] = 1.0
    put("sel", sel)
    vec = {"scb": "L0_ffn_SCB", "qbias": "L0_ffn_bias", "bout": "L0_attn_bout", "lng": "L0_attn_ln_g",
           "lnb": "L0_attn_ln_b", "bv": "L1_ffn_bv", "bo": "L1_ffn_bo", "ln1g": "L1_ffn_ln1_g",
           "ln1b": "L1_ffn_ln1_b", "ln2g": "L1_ffn_ln2_g", "ln2b": "L1_ffn_ln2_b", "abk": "L1_attn_bk",
           "abq": "L1_attn_bq", "abv": "L1_attn_bv", "agk": "L1_attn_gk", "agq": "L1_attn_gq", "agv": "L1_attn_gv",
           "aek": "L1_attn_betak", "aeq": "L1_attn_betaq", "aev": "L1_attn_betav"}
    rows = np.zeros((len(ROWS), P), f)
    for name, key in vec.items():
        rows[ROW[name]] = g(key)
    rows[ROW["bmg"], 0:16] = g("L0_attn_bmix")
    rows[ROW["bmg"], 16:24] = g("L0_attn_bgate")
    rows[ROW["rw"]] = g("L1_ffn_router_w")[:, 0]
    rows[ROW["rb"], 0] = g("L1_ffn_router_b")[0]
    for e in range(EXPERTS):
        rows[ROW[f"b2_{e}"]] = g("L1_ffn_b2")[e]
    return {"in_x": g("L0_attn_x").reshape(SEQS * T, P), "in_pack": pack, "in_rows": rows.reshape(-1),
            "in_w1": g("L1_ffn_W1"), "in_w2": g("L1_ffn_W2")}


def kernel(**inputs):
    import concourse.bacc as _bacc
    from concourse.bass_utils import run_bass_kernel_spmd as _run

    nc = _bacc.Bacc("TRN2", target_bir_lowering=False, num_devices=1)
    arrays = {k: np.ascontiguousarray(v) for k, v in _lay_out(inputs).items()}
    args = [nc.dram_tensor(k, v.shape, F32, kind="ExternalInput").ap() for k, v in arrays.items()]
    out = nc.dram_tensor("out_0", (SEQS * T, P), F32, kind="ExternalOutput").ap()
    program(nc, *args, out)
    r = _run(nc, [arrays], core_ids=[0])
    return np.asarray(r.results[0]["out_0"]).reshape(SEQS, T, P)
```

```python
from contextlib import ExitStack

import numpy as np

import concourse.bass as bass
from concourse import mybir

ALU = mybir.AluOpType
ACT = mybir.ActivationFunctionType
AX_X = mybir.AxisListType.X
F32 = mybir.dt.float32
BF16 = mybir.dt.bfloat16
I32 = mybir.dt.int32

P = 128
SEQS, T = 16, 256
TILES = SEQS * T // P
TP = 4
N = TP * P
PAIRS = TILES // TP
H0, J0, D0 = 8, 2, 16
HJ = H0 * J0
H1, D1 = 16, 8
FF, EXPERTS = 512, 4
CH = FF // P
SLOTS = 6
KROWS = SLOTS * D1 + 2
LN_EPS, DEN_EPS = 1e-5, 1e-6
PHASES = ("ffn", "linear", "ffn", "experts", "attn", "experts")

SLOTS_H = 32
UNITS = [None] * SLOTS_H
for _e in range(EXPERTS):
    for _k in range(CH):
        for _kind, _slot in (("W1", 8 * _e + 2 * _k - 2), ("W2", 8 * _e + 2 * _k + 7)):
            UNITS[_slot % SLOTS_H] = (3 + _slot // SLOTS_H, _kind, _e, _k)

ROWS = ("scb", "qbias", "bmg", "bout", "lng", "lnb", "bv", "bo", "ln1g", "ln1b", "ln2g", "ln2b", "rw", "rb",
        "b2_0", "b2_1", "b2_2", "b2_3", "abk", "abq", "abv", "agk", "agq", "agv", "aek", "aeq", "aev", "decay")
ROW = {name: i for i, name in enumerate(ROWS)}
PACK = {}
_at = 0
for _name, _n in (("cbt", 128), ("q0", 128), ("k0", 128), ("vmg", 168), ("out0", 128), ("q1", 128),
                  ("k1", 128), ("v1", 128), ("o1", 128), ("kqv", 384), ("bq", 1), ("bk", 1), ("b1", 16),
                  ("hmask", 8), ("ident", 128), ("sel", HJ * P)):
    PACK[_name] = (_at, _n)
    _at += _n
PACKED = _at
BETA_ROWS = (0, 64, 96)


def later(count):
    return not isinstance(count, int) or count > 0


class Link:

    def __init__(self, engine, sem, index, per):
        self.engine, self.sem, self.start, self.per, self.k = engine, sem, index * per, per, 0

    def __call__(self, instruction):
        instruction.then_inc(self.sem, 1)
        self.k += 1
        self.engine.wait_ge(self.sem, self.start + self.k)

    def close(self):
        assert self.k == self.per, (self.k, self.per)


def over(ap, shape):
    return ap.to_broadcast(shape)


def program(nc, x, pack, rows, w1, w2, out):
    with ExitStack() as ctx:
        def sb(name, shape, dt=F32, scope=ctx):
            return scope.enter_context(nc.sbuf_tensor(name, shape, dt))

        def sem(name):
            return ctx.enter_context(nc.semaphore(name))

        bank = [ctx.enter_context(nc.psum_tensor(f"bank{i}", [P, 512], F32)) for i in range(8)]

        def tiles(b):
            return bank[b][:, :].rearrange("p (t c) -> p t c", t=TP)

        X = sb("X", [P, TILES, P])
        W = sb("W", [P, PACKED - HJ * P])
        R = sb("R", [P, len(ROWS), P])
        W1 = sb("W1", [P, EXPERTS, FF])
        W2 = sb("W2", [P, EXPERTS, CH, P])
        half = sb("half", [P, TP])
        tick = sb("tick", [P, 1])
        half12 = sb("half12", [P, 12])
        st = sb("st", [P, TP, 6])
        mv = sb("mv", [P, TP, 2])
        ve = sb("ve", [P, TP])
        rs = sb("rs", [P, TP])
        st2 = sb("st2", [P, TP, 6])
        mv2 = sb("mv2", [P, TP, 2])
        ve2 = sb("ve2", [P, TP])
        rs2 = sb("rs2", [P, TP])
        st3 = sb("st3", [P, TP, 6])
        mv3 = sb("mv3", [P, TP, 2])
        ve3 = sb("ve3", [P, TP])
        rs3 = sb("rs3", [P, TP])

        scr_q = nc.dram_tensor("scr_q", (2, SLOTS, P, T), BF16, kind="Internal").ap()
        scr_k = nc.dram_tensor("scr_k", (2, SLOTS, P, T), BF16, kind="Internal").ap()
        scr_m = nc.dram_tensor("scr_m", (2, 2, H1, T), BF16, kind="Internal").ap()
        LOADS = 3 + 2 * EXPERTS

        def wt(name):
            a, n = PACK[name]
            return W[:, a:a + n]

        def row(name):
            return R[:, ROW[name], :]

        def row4(name):
            return over(R[:, ROW[name]:ROW[name] + 1, :], [P, TP, P])

        with ExitStack() as early:
            FY = [sb(f"FY{i}", [P, TP, P], scope=early) for i in range(2)]
            FYT = [sb(f"FYT{i}", [P, N], scope=early) for i in range(2)]
            XB = [sb(f"XB{i}", [P, TP, P], scope=early) for i in range(2)]
            SEL = sb("SEL", [P, HJ, P], BF16, scope=early)
            I0 = sb("I0", [P, 512], scope=early)
            I1 = sb("I1", [P, 512], scope=early)
            Y0 = [sb(f"Y0_{i}", [P, TP, P], scope=early) for i in range(2)]
            YR0 = sb("YR0", [P, TP, P], scope=early)
            YT0 = sb("YT0", [P, N], scope=early)
            ex = sb("ex", [P, 2, N], scope=early)
            re = sb("re", [P, 2, N], scope=early)
            qf = sb("qf", [P, N], scope=early)
            kT = [sb(f"kT{i}", [P, N], scope=early) for i in range(2)]
            QX = [sb(f"QX{i}", [P, 2, H0, T], scope=early) for i in range(2)]
            selF = QX[0][:, :, :, :].rearrange("p b h t -> p (b h t)")[:, 0:HJ * P]
            bE = sb("bE", [P, TP, HJ], scope=early)
            bR = sb("bR", [P, TP, HJ], scope=early)
            part = [sb(f"part{i}", [P, TP, HJ], BF16, scope=early) for i in range(3)]
            BT = sb("BT", [P, TP, P], scope=early)
            STK = [sb(f"STK{i}", [P, 2, 384], BF16, scope=early) for i in range(2)]
            MG = sb("MG", [P, TP, 40], scope=early)
            mx = sb("mx", [P, TP, H0], scope=early)
            E0 = sb("E0", [P, TP, 40], scope=early)
            E1 = sb("E1", [P, TP, 40], scope=early)
            SD = sb("SD", [P, TP, 32], scope=early)
            RD = sb("RD", [P, TP, 32], scope=early)
            WM = [sb(f"WM{i}", [P, TP, HJ], scope=early) for i in range(2)]
            VG = [sb(f"VG{i}", [P, TP, H0, 32], scope=early) for i in range(2)]
            DD0 = [sb(f"DD0_{i}", [P, 1024], scope=early) for i in range(2)]
            DD1 = [sb(f"DD1_{i}", [P, 512], scope=early) for i in range(2)]
            SS = [sb(f"SS{i}", [P, 768], scope=early) for i in range(2)]
            A0 = [sb(f"A0_{i}", [P, 4, T], scope=early) for i in range(2)]
            A1 = [sb(f"A1_{i}", [P, 4, P], scope=early) for i in range(2)]
            OT0 = [sb(f"OT0_{i}", [P, 4, T], scope=early) for i in range(2)]
            den = sb("den", [P, 2, HJ], scope=early)
            rec = sb("rec", [P, 2, HJ], scope=early)
            rw0 = sb("rw0", [P, 2, HJ], scope=early)
            PR = sb("PR", [P, 2, HJ, D0], scope=early)
            YO = sb("YO", [P, TP, P], scope=early)
            YOT = sb("YOT", [P, N], scope=early)
            HR = sb("HR", [P, TP, P], scope=early)
            HN = sb("HN", [P, TP, P], scope=early)
            HG = sb("HG", [P, TP, P], scope=early)

        late = ctx
        QS = [sb(f"QS{i}", [P, 2, H1 // 2, T], BF16, scope=late) for i in range(2)]
        KS = [sb(f"KS{i}", [P, 2, H1 // 2, T], BF16, scope=late) for i in range(2)]
        V1 = [sb(f"V1_{i}", [P, TP, H1, 32], scope=late) for i in range(2)]
        VS = sb("VS", [P, TP, P], scope=late)
        PB = [sb(f"PB{i}", [P, 2, T], scope=late) for i in range(4)]
        YT1 = sb("YT1", [P, N], scope=late)
        Y1 = [sb(f"Y1_{i}", [P, TP, P], scope=late) for i in range(2)]
        YR1 = [sb(f"YR1_{i}", [P, TP, P], scope=late) for i in range(2)]
        qk32 = [sb(f"qk32_{i}", [P, N], scope=late) for i in range(2)]
        qkr = [sb(f"qkr_{i}", [P, N], scope=late) for i in range(2)]
        PQ = [sb(f"PQ_{i}", [P, 3, N], BF16, scope=late) for i in range(2)]
        OT1 = [sb(f"OT1_{i}", [P, 4, T], scope=late) for i in range(2)]
        NM = sb("NM", [P, TP, H1], scope=late)
        MH = [sb(f"MH{i}", [H1, 2, T], BF16, scope=late) for i in range(2)]
        ones = sb("ones", [2, H1 // 2 * T * 2], BF16, scope=late)
        rec1 = sb("rec1", [P, TP, H1], scope=late)
        AN = sb("AN", [P, TP, P], scope=late)
        ANT = sb("ANT", [P, N], scope=late)
        Z = sb("Z", [P, TP, P], scope=late)
        ZN = sb("ZN", [P, TP, P], scope=late)
        ZG = sb("ZG", [P, TP, P], scope=late)
        with ExitStack() as shared:
            XS = [sb(f"XS{i}", [P, TP, P], scope=shared) for i in range(2)]
            XT = sb("XT", [P, N], scope=shared)
            HB = [sb(f"HB{i}", [P, CH, N], scope=shared) for i in range(2)]
            YB = sb("YB", [P, TP, P], scope=shared)
            AC = sb("AC", [P, TP, P], scope=shared)
            KP = YB
            key = [sb(f"key{i}", [P, TP], scope=shared) for i in range(3)]
            kint = sb("kint", [P, TP], I32, scope=shared)
            MK = [sb(f"MK{i}", [P, EXPERTS, TP], scope=shared) for i in range(2)]
            EN = sb("EN", [P, TP, P], scope=shared)
            EG = sb("EG", [P, TP, P], scope=shared)
        with ExitStack() as shared:
            YV, YVT, kqT, PAT, PA, YX = Y1, YT1, qk32, qkr, OT1[0], (VS, Z)
            KQV = [sb(f"KQV{i}", [P, TP, 3, P], scope=shared) for i in range(2)]
            RAW = sb("RAW", [P, TP, 3, P], scope=shared)
            st12 = sb("st12", [P, 12, 6], scope=shared)
            dif12, mean12, var12 = (sb(f"{k}12", [P, 12], scope=shared) for k in ("dif", "mean", "var"))
            ve12 = sb("ve12", [P, 12], scope=shared)
            rs12 = sb("rs12", [P, 12], scope=shared)
            nmx = sb("nmx", [P, TP], scope=shared)
            esum = sb("esum", [P, TP], scope=shared)
            rsum = sb("rsum", [P, TP], scope=shared)

        x_loaded, w_loaded, stored = sem("x_loaded"), sem("w_loaded"), sem("stored")
        setup_done = sem("setup_done")
        setup_link = sem("setup_link")
        consts_done = sem("consts_done")
        x_done = sem("x_done")

        class F:
            link = sem("ffn_link")
            var = sem("ffn_var")
            rstd = sem("ffn_rstd")
            norm = sem("ffn_norm")
            turned = sem("ffn_turned")
            copied = sem("ffn_copied")
            mm = sem("ffn_mm")
            xb = sem("ffn_xb")

        class L:
            link_ln = sem("lin_link_ln")
            link_beta = sem("lin_link_beta")
            link_gate = sem("lin_link_gate")
            link_post = sem("lin_link_post")
            link_out = sem("lin_link_out")
            var = sem("lin_var")
            rstd = sem("lin_rstd")
            norm = sem("lin_norm")
            turned = sem("lin_turned")
            copied = sem("lin_copied")
            qk = sem("lin_qk")
            exp4 = sem("lin_exp4")
            mg = sem("lin_mg")
            bt = sem("lin_bt")
            bT = sem("lin_bT")
            vmg = sem("lin_vmg")
            v_used = sem("lin_v_used")
            e0 = sem("lin_e0")
            e1 = sem("lin_e1")
            qf = sem("lin_qf")
            qx = sem("lin_qx")
            stk = sem("lin_stk")
            yr = sem("lin_yr")
            bc = sem("lin_bc")
            bcused = sem("lin_bcused")
            s = sem("lin_s")
            scopied = sem("lin_scopied")
            a0 = sem("lin_a0")
            a1 = sem("lin_a1")
            av = sem("lin_av")
            ocopied = sem("lin_ocopied")
            pt = sem("lin_pt")
            ptused = sem("lin_ptused")
            yo = sem("lin_yo")
            yoT = sem("lin_yoT")
            yoc = sem("lin_yoc")
            wo = sem("lin_wo")
            hr = sem("lin_hr")
            var2 = sem("lin_var2")
            rstd2 = sem("lin_rstd2")
            hn = sem("lin_hn")
            hg = sem("lin_hg")
            xd = sem("lin_xd")

        class A:
            ready = sem("heads_ready")
            vzero = sem("heads_vzero")
            ones = sem("heads_ones")
            link_ln = sem("heads_link_ln")
            link_m = sem("heads_link_m")
            link_n = sem("heads_link_n")
            link_z = sem("heads_link_z")
            var = sem("heads_var")
            rstd = sem("heads_rstd")
            norm = sem("heads_norm")
            turned = sem("heads_turned")
            copied = sem("heads_copied")
            q = sem("heads_q")
            k = sem("heads_k")
            v = sem("heads_v")
            qev = sem("heads_qev")
            kev = sem("heads_kev")
            vev = sem("heads_vev")
            vcopied = sem("heads_vcopied")
            hi = sem("heads_hi")
            r1 = sem("heads_r1")
            mid = sem("heads_mid")
            parts = sem("heads_parts")
            scr = sem("heads_scr")
            qkl0 = sem("heads_qkl0")
            qkl1 = sem("heads_qkl1")
            m0T = sem("heads_m0T")
            m1T = sem("heads_m1T")
            m0ev = sem("heads_m0ev")
            m1ev = sem("heads_m1ev")
            mwr0 = sem("heads_mwr0")
            mwr1 = sem("heads_mwr1")
            ml0 = sem("heads_ml0")
            ml1 = sem("heads_ml1")
            mx = sem("heads_mx")
            red = sem("heads_red")
            s = sem("heads_s")
            e = sem("heads_e")
            pv = sem("heads_pv")
            ocopied = sem("heads_ocopied")
            pt = sem("heads_pt")
            norm1 = sem("heads_norm1")
            anT = sem("heads_anT")
            anc = sem("heads_anc")
            wo = sem("heads_wo")
            yr = sem("heads_yr")
            z = sem("heads_z")
            var2 = sem("heads_var2")
            rstd2 = sem("heads_rstd2")
            zn = sem("heads_zn")
            zg = sem("heads_zg")
            x1 = sem("heads_x1")

        class E:
            link_key = sem("exp_link_key")
            link_ln = sem("exp_link_ln")
            turned = sem("exp_turned")
            xt = sem("exp_xt")
            h = sem("exp_h")
            relu = sem("exp_relu")
            y = sem("exp_y")
            yused = sem("exp_yused")
            mask = sem("exp_mask")
            acc = sem("exp_acc")
            var = sem("exp_var")
            rstd = sem("exp_rstd")
            norm = sem("exp_norm")
            g = sem("exp_g")
            b = sem("exp_b")

        class V:
            link_ln = sem("attn_link_ln")
            link_b = sem("attn_link_b")
            var = sem("attn_var")
            rstd = sem("attn_rstd")
            norm = sem("attn_norm")
            turned = sem("attn_turned")
            copied = sem("attn_copied")
            proj = sem("attn_proj")
            biased = sem("attn_biased")
            var12 = sem("attn_var12")
            rstd12 = sem("attn_rstd12")
            norm12 = sem("attn_norm12")
            g = sem("attn_g")
            kqv = sem("attn_kqv")
            kqT = sem("attn_kqT")
            kqc = sem("attn_kqc")
            s = sem("attn_s")
            nmx = sem("attn_nmx")
            e = sem("attn_e")
            pT = sem("attn_pT")
            pc = sem("attn_pc")
            av = sem("attn_av")
            yx = sem("attn_yx")
            sumr = sem("attn_sumr")

        schedule, runs, xp = [], {}, 1
        for name in PHASES:
            schedule.append((name, runs.get(name, 0), xp))
            runs[name] = runs.get(name, 0) + 1
            xp += 1

        def token_stats(dve, src, st_, mv_, ve_, link, var_sem):
            for t in range(TP):
                last = dve.bn_stats(st_[:, t, :], src(t))
            link(last)
            dve.memset(tick[:, :], 0.0)
            for t in range(TP):
                last = dve.bn_aggr(mv_[:, t, :], st_[:, t, :])
            link(last)
            dve.tensor_scalar(ve_[:, :], mv_[:, :, 1], LN_EPS, None, ALU.add).then_inc(var_sem, 1)

        def token_norm(dve, src, dst, mv_, rs_):
            for t in range(TP):
                last = dve.tensor_scalar(dst(t), src(t), mv_[:, t, 0:1], rs_[:, t:t + 1], ALU.subtract, ALU.mult)
            return last

        def pairs(engine, step):
            with engine.Fori(0, PAIRS // 2) as it:
                step(it)

        def linear_steps(engine, step):
            step(-1, 1, True, False, False)
            step(0, 0, True, True, False)
            with engine.Fori(0, PAIRS // 2 - 1) as it:
                step(it * 2 + 1, 1, True, True, True)
                step(it * 2 + 2, 0, True, True, True)
            step(PAIRS - 1, 1, False, True, True)
            step(PAIRS, 0, False, False, True)

        def experts_steps(engine, step):
            def stages(n):
                return [0 <= n - back < PAIRS for back in (-1, 0, 1, 2, 3, 4)]
            first, last = 4, PAIRS - 2
            for n in range(-1, first):
                step(n, n % 2, *stages(n))
            with engine.Fori(0, (last - first) // 2) as it:
                step(it * 2 + first, 0, *stages(first))
                step(it * 2 + (first + 1), 1, *stages(first))
            for n in range(last, PAIRS + 4):
                step(n, n % 2, *stages(n))

        def attn_steps(engine, step):
            step(-2, 0, True, False, False)
            step(-1, 1, True, True, False)
            with engine.Fori(0, PAIRS // 2 - 1) as it:
                step(it * 2, 0, True, True, True)
                step(it * 2 + 1, 1, True, True, True)
            step(PAIRS - 2, 0, False, True, True)
            step(PAIRS - 1, 1, False, False, True)

        def run_phases(engine, phases):
            for name, run, xp in schedule:
                phases[name](run, xp)

        block = ctx.enter_context(nc.Block())

        @block.sync
        def _(sp):
            for n in range(PAIRS):
                sp.dma_start(X[:, TP * n:TP * n + TP, :],
                             x[N * n:N * n + N, :].rearrange("(t p) c -> p t c", p=P)).then_inc(x_loaded, 16)
            sp.dma_start(W[:, :], pack[:, 0:PACKED - HJ * P]).then_inc(w_loaded, 16)
            sp.dma_start(selF, pack[:, PACKED - HJ * P:PACKED]).then_inc(w_loaded, 16)
            sp.dma_start(R[:, :, :].rearrange("p r c -> p (r c)"),
                         rows.partition_broadcast(P)).then_inc(w_loaded, 16)
            for e in range(EXPERTS):
                sp.dma_start(W1[:, e, :], w1[e]).then_inc(w_loaded, 16)
                sp.dma_start(W2[:, e, :, :], w2[e].rearrange("(k p) c -> p k c", p=P)).then_inc(w_loaded, 16)

            def experts(run, xp):
                g8 = 8 * run

                def move_max(n, b, par):
                    written, loaded = (A.mwr0, A.mwr1)[b], (A.ml0, A.ml1)[b]
                    sp.wait_ge((A.m0ev, A.m1ev)[b], n + (g8 + 1))
                    sp.dma_start(scr_m[b].rearrange("s h t -> h s t"), MH[b][:, :, :]).then_inc(written, 16)
                    sp.wait_ge(written, n * 16 + (16 * g8 + 16))
                    for a in range(2):
                        r = 64 * a + SLOTS * D1
                        sp.dma_start(QS[par][r:r + 2, b, :, :],
                                     scr_m[b].rearrange("s (g a) t -> a s g t", a=2)[a]).then_inc(loaded, 16)

                def load_parts(n, b, par):
                    for a in range(2):
                        for scr, dst in ((scr_q, QS), (scr_k, KS)):
                            sp.dma_start(dst[par][64 * a:64 * a + SLOTS * D1, b, :, :].rearrange("p g t -> p (g t)"),
                                         scr[b, :, 64 * a:64 * a + 64, :].rearrange("s (d g) t -> s d (g t)", d=D1)
                                         ).then_inc((A.qkl0, A.qkl1)[b], 16)

                def step(n, par, pre, mx, att, post, exp, fin):
                    other = 1 - par
                    if att:
                        move_max(n - 1, 1, other)
                    if pre:
                        sp.wait_ge(A.parts, n * 2 + (2 * g8 + 4))
                        if later(n * 64 + 64 * (g8 + 1)):
                            sp.wait_ge(A.qkl0, n * 64 + 64 * (g8 + 1))
                        if later(n * 64 + 64 * (g8 + 1)):
                            sp.wait_ge(A.qkl1, n * 64 + 64 * (g8 + 1))
                        for b in range(2):
                            h = slice(T * b, T * b + T)
                            for scr, pt, at, src in ((scr_q, PQ[0], 0, (0, 3)), (scr_q, PQ[0], 3, (0, 2)),
                                                     (scr_q, PQ[0], 5, (0, 1)), (scr_k, PQ[1], 0, (0, 0)),
                                                     (scr_k, PQ[1], 3, (1, 1)), (scr_k, PQ[1], 5, (2, 3))):
                                k = SLOTS - at if at == 5 else (3, 2)[at == 3]
                                if src[1] > src[0]:
                                    s = pt[:, src[0]:src[1], h]
                                else:
                                    s = over(pt[:, src[0]:src[0] + 1, h], [P, k, T])
                                sp.dma_start(scr[b, at:at + k].rearrange("s r t -> r s t"), s).then_inc(A.scr, 16)
                        sp.wait_ge(A.scr, n * 192 + 192 * (g8 + 2))
                        if att:
                            sp.wait_ge(A.s, n * 32 + (32 * g8 - 16))
                        load_parts(n + 1, 0, other)
                    if mx:
                        move_max(n, 0, par)
                    if pre:
                        if att:
                            sp.wait_ge(A.s, n * 32 + 32 * g8)
                        load_parts(n + 1, 1, other)

                if run == 0:
                    sp.wait_ge(A.ones, 1)
                    for b in range(2):
                        for a in range(2):
                            r = 64 * a + SLOTS * D1
                            sp.dma_start(KS[b][r:r + 2, :, :, :].rearrange("p b g t -> p (b g t)"),
                                         ones[:, :]).then_inc(A.ready, 16)
                experts_steps(sp, step)

            for name, run, xp in schedule:
                if name == "experts":
                    experts(run, xp)
            with sp.Fori(0, PAIRS) as n:
                sp.wait_ge(x_done, n + (8 * schedule[-1][2] + 1))
                sp.dma_start(out[bass.ds(n * N, N), :].rearrange("(t p) c -> p t c", p=P),
                             X[:, bass.ds(n * TP, TP), :]).then_inc(stored, 16)
            sp.wait_ge(stored, 16 * PAIRS)

        @block.gpsimd
        def _(pool):
            def power(var_sem, rstd_sem, count, ve_, rs_):
                pool.wait_ge(var_sem, count)
                pool.tensor_tensor(rs_[:, :], ve_[:, :], half[:, 0:ve_.shape[1]], ALU.pow).then_inc(rstd_sem, 1)

            def ffn(run, xp):
                def step(it):
                    n0 = it * 2
                    for b in range(2):
                        power(F.var, F.rstd, n0 + (8 * run + 1 + b), (ve, ve2)[b], (rs, rs2)[b])
                    for b in range(2):
                        pool.wait_ge(x_done, n0 + (8 * xp - 1 + b))
                        pool.tensor_tensor(XB[b][:, :, :], X[:, bass.ds((n0 + b) * TP, TP), :], row4("qbias"),
                                           ALU.add).then_inc(F.xb, 1)
                pairs(pool, step)

            def linear(run, xp):
                def step(n, par, pre, main, post):
                    if pre:
                        power(L.var, L.rstd, n + 2, ve, rs)
                    for i in range(8):
                        if post and i == 6:
                            power(L.var2, L.rstd2, n, ve2, rs2)
                        if post and i == 7:
                            pool.wait_ge(L.hn, n)
                            pool.tensor_tensor(HG[:, :, :], HN[:, :, :], row4("lng"), ALU.mult).then_inc(L.hg, 1)
                            pool.wait_ge(L.hg, n)
                            pool.tensor_tensor(HG[:, :, :], HG[:, :, :], row4("lnb"), ALU.add).then_inc(L.xd, 1)
                        if main:
                            j = n * 8 + i
                            pool.wait_ge(L.bcused, j * 3 + 3)
                            pool.wait_ge(L.scopied, j * 2 + 2)
                            if later(j - 1):
                                pool.wait_ge(L.av, j - 1)
                            s = SS[i % 2][:, 512:768].rearrange("p (h o t) -> p h o t", h=2, o=1)
                            pool.tensor_tensor(A1[i % 2][:, :, :].rearrange("p (h j) t -> p h j t", h=2),
                                               DD1[i % 2][:, :].rearrange("p (h j t) -> p h j t", h=2, j=2),
                                               over(s, [P, 2, 2, P]), ALU.mult).then_inc(L.a1, 1)
                    if main:
                        pool.wait_ge(L.norm, n + 1)
                        if later(n):
                            pool.wait_ge(L.hr, n)
                        pool.tensor_tensor(YR0[:, :, :], Y0[par][:, :, :], row4("bout"), ALU.add).then_inc(L.yr, 1)
                linear_steps(pool, step)

            def experts(run, xp):
                g8 = 8 * run

                def step(n, par, pre, mx, att, post, exp, fin):
                    c = n + g8
                    if pre:
                        power(A.var, A.rstd, c + 2, ve, rs)
                    if mx:
                        pool.wait_ge(A.vev, c + 1)
                        if later(c * 32 - 32):
                            pool.wait_ge(A.pv, c * 32 - 32)
                        bv = over(row("bv").rearrange("p (o h d) -> p o h d", o=1, h=H1), [P, TP, H1, D1])
                        pool.tensor_tensor(V1[par][:, :, :, 0:D1],
                                           VS[:, :, :].rearrange("p t (h d) -> p t h d", h=H1), bv,
                                           ALU.add).then_inc(A.vcopied, 1)
                    if pre:
                        for h in range(2):
                            pool.wait_ge(A.hi, c * 2 + (3 + h))
                            pool.tensor_tensor(qkr[h][:, :], qk32[h][:, :], PQ[h][:, 0, :],
                                               ALU.subtract).then_inc(A.r1, 1)
                    if fin:
                        power(E.var, E.rstd, c - 3, ve3, rs3)
                    if pre:
                        for h in range(2):
                            pool.wait_ge(A.mid, c * 2 + (3 + h))
                            pool.tensor_tensor(PQ[h][:, 2, :], qkr[h][:, :], PQ[h][:, 1, :],
                                               ALU.subtract).then_inc(A.parts, 1)
                    if post:
                        power(A.var2, A.rstd2, c - 1, ve2, rs2)
                    if fin:
                        pool.wait_ge(E.norm, c - 3)
                        pool.tensor_tensor(EG[:, :, :], EN[:, :, :], row4("ln2g"), ALU.mult).then_inc(E.g, 1)
                        pool.wait_ge(E.g, c - 3)
                        pool.tensor_tensor(EG[:, :, :], EG[:, :, :], row4("ln2b"), ALU.add).then_inc(E.b, 1)
                    if post:
                        pool.wait_ge(A.zn, c - 1)
                        pool.tensor_tensor(ZG[:, :, :], ZN[:, :, :], row4("ln1g"), ALU.mult).then_inc(A.zg, 1)
                        pool.wait_ge(A.zg, c - 1)
                        if later(c * 4 - 15):
                            pool.wait_ge(E.acc, c * 4 - 15)
                        pool.tensor_tensor(XS[par][:, :, :], ZG[:, :, :], row4("ln1b"), ALU.add).then_inc(A.x1, 1)
                    if mx:
                        pool.wait_ge(A.norm, c + 1)
                        if later(c - 1):
                            pool.wait_ge(A.z, c - 1)
                        pool.tensor_tensor(YR1[par][:, :, :], Y1[par][:, :, :], row4("bo"), ALU.add).then_inc(A.yr, 1)

                if run == 0:
                    pool.wait_ge(x_done, 8 * xp)
                    pool.memset(ones[:, :], 1.0).then_inc(A.ones, 1)
                    for b in range(2):
                        pool.memset(V1[b][:, :, :, :], 0.0).then_inc(A.vzero, 1)
                    pool.wait_ge(A.vzero, 2)
                    for b in range(2):
                        pool.memset(V1[b][:, :, :, D1:D1 + 1], 1.0).then_inc(A.vzero, 1)
                    pool.wait_ge(A.vzero, 4)
                experts_steps(pool, step)

            def attn(run, xp):
                def rows3(name):
                    k = ROW[name]
                    return over(R[:, k:k + 3, :].rearrange("p (o k) c -> p o (k c)", o=1), [P, TP, 3 * P])

                def step(n, par, pre, mid, main):
                    other = 1 - par
                    if pre:
                        power(V.var, V.rstd, n + 3, ve, rs)
                    if mid:
                        pool.wait_ge(V.norm12, n + 2)
                        w = KQV[other][:, :, :, :].rearrange("p t k c -> p t (k c)")
                        pool.tensor_tensor(w, w, rows3("agk"), ALU.mult).then_inc(V.g, 1)
                        pool.wait_ge(V.g, n + 2)
                        pool.tensor_tensor(w, w, rows3("aek"), ALU.add).then_inc(V.kqv, 1)
                        pool.wait_ge(V.norm, n + 2)
                        pool.wait_ge(x_done, n + 8 * xp)
                        pool.tensor_tensor(YX[other][:, :, :], YV[other][:, :, :], X[:, bass.ds((n + 1) * TP, TP), :],
                                           ALU.add).then_inc(V.yx, 1)
                    if pre:
                        pool.wait_ge(V.var12, n + 3)
                        pool.tensor_tensor(rs12[:, :], ve12[:, :], half12[:, :], ALU.pow).then_inc(V.rstd12, 1)
                attn_steps(pool, step)

            pool.memset(half12[:, :], -0.5).then_inc(consts_done, 1)
            pool.memset(half[:, :], -0.5).then_inc(consts_done, 1)
            for b in range(2):
                pool.memset(VG[b][:, :, :, :], 0.0).then_inc(consts_done, 1)
                pool.memset(STK[b][:, :, :], 0.0).then_inc(consts_done, 1)
            pool.memset(BT[:, :, :], 0.0).then_inc(consts_done, 1)
            pool.wait_ge(consts_done, 7)
            pool.wait_ge(w_loaded, 16 * LOADS)
            pool.wait_ge(setup_done, 1)
            run_phases(pool, {"ffn": ffn, "linear": linear, "experts": experts, "attn": attn})

        @block.scalar
        def _(act):
            def ffn(run, xp):
                def step(it):
                    n0 = it * 2
                    for b in range(2):
                        act.wait_ge(F.turned, n0 + (8 * run + 1 + b))
                        act.activation(FYT[b][:, :], bank[b][:, :], ACT.Copy).then_inc(F.copied, 1)
                pairs(act, step)

            def linear(run, xp):
                hmask = wt("hmask")

                def step(n, par, pre, main, post):
                    other = 1 - par
                    for i in range(8):
                        if (main, pre)[i == 7]:
                            if later(n * 8 + i):
                                act.wait_ge(L.a0, n * 8 + i)
                            if later(n * 8 + i):
                                act.wait_ge(L.a1, n * 8 + i)
                            ss = SS[(i + 1) % 2]
                            act.wait_ge(L.s, n * 16 + (2 * i + 3))
                            act.activation(ss[:, 0:512], bank[2][:, :], ACT.Copy).then_inc(L.scopied, 1)
                            act.wait_ge(L.s, n * 16 + (2 * i + 4))
                            act.activation(ss[:, 512:768], bank[3][:, 0:T], ACT.Copy).then_inc(L.scopied, 1)
                        if (i == 0 and post) or (i == 4 and main):
                            done = n * 2 + i // 4 - 1
                            act.wait_ge(L.av, done * 4 + 4)
                            if i == 4:
                                if later(done * 2 - 2):
                                    act.wait_ge(L.pt, done * 2 - 2)
                            for h in range(2):
                                act.activation(OT0[1 - i // 4][:, 2 * h:2 * h + 2, :],
                                               bank[4 + h][:, :].rearrange("p (r t) -> p r t", r=2),
                                               ACT.Copy).then_inc(L.ocopied, 1)
                        if pre and i == 2:
                            act.wait_ge(L.turned, n + 2)
                            if later(n + 1):
                                act.wait_ge(L.vmg, n + 1)
                            act.activation(YT0[:, :], bank[6][:, :], ACT.Copy).then_inc(L.copied, 1)
                        if post and i == 2:
                            act.wait_ge(L.yoT, n)
                            act.activation(YOT[:, :], bank[7][:, :], ACT.Copy).then_inc(L.yoc, 1)
                        if pre and i == 3:
                            if later(n + 1):
                                act.wait_ge(L.qf, n + 1)
                            for h, b in ((0, 7), (1, 6)):
                                act.wait_ge(L.qk, n * 2 + (3 + h))
                                act.activation(ex[:, h, :], bank[b][:, :], ACT.Exp).then_inc(L.exp4, 1)
                                act.activation(re[:, h, :], bank[b][:, :], ACT.Relu).then_inc(L.exp4, 1)
                        if pre and i == 4:
                            act.wait_ge(L.e0, n + 2)
                            act.activation(E1[:, :, :], E0[:, :, :], ACT.Exp).then_inc(L.e1, 1)
                        if pre and i in (5, 6):
                            act.wait_ge(L.qf, n + 2)
                            for h in range(4 * (i - 5), 4 * (i - 5) + 4):
                                act.activation(QX[other][:, :, h, :], qf[:, :].rearrange("p (b t) -> p b t", b=2),
                                               ACT.Copy, scale=hmask[:, h:h + 1]).then_inc(L.qx, 1)
                        if pre and i == 6:
                            act.wait_ge(L.bT, n + 2)
                            bt = bank[7][:, :].rearrange("p (b t) -> p b t", b=2)
                            act.activation(STK[other][:, :, 1:T], bt[:, :, 1:T], ACT.Copy).then_inc(L.stk, 1)
                            act.activation(STK[other][:, :, T + 1:T + P], bt[:, :, P + 1:T],
                                           ACT.Copy).then_inc(L.stk, 1)
                linear_steps(act, step)

            def experts(run, xp):
                g8 = 8 * run

                def relu(p, e, k):
                    c = p + g8
                    act.wait_ge(E.h, c * 16 + (4 * e + k + 1))
                    if later(c * 4 + (e - 1)):
                        act.wait_ge(E.y, c * 4 + (e - 1))
                    b0 = PACK["b1"][0] + CH * e + k
                    act.activation(HB[e % 2][:, k, :], bank[5][:, :], ACT.Relu,
                                   bias=W[:, b0:b0 + 1]).then_inc(E.relu, 1)

                def step(n, par, pre, mx, att, post, exp, fin):
                    c = n + g8

                    def copy_sums(i):
                        h, back = {9: (0, 2), 17: (1, 2), 25: (2, 2), 1: (3, 3)}[i]
                        if i != 1:
                            if later((c - 1) * 4 + (2 * (h // 2) - 2)):
                                act.wait_ge(A.pt, (c - 1) * 4 + (2 * (h // 2) - 2))
                        act.wait_ge(A.pv, c * 32 + (8 * h + 8 - (32, 64)[i == 1]))
                        r = 2 * (h % 2)
                        act.activation(OT1[h // 2][:, r:r + 2, :], bank[4][:, :].rearrange("p (r t) -> p r t", r=2),
                                       ACT.Copy).then_inc(A.ocopied, 1)

                    for i in range(SLOTS_H):
                        if pre and i == 7:
                            act.wait_ge(A.turned, c + 2)
                            if later(c + 1):
                                act.wait_ge(A.v, c + 1)
                            act.activation(YT1[:, :], bank[6][:, :], ACT.Copy).then_inc(A.copied, 1)
                        if att:
                            q = c * 32 + (i - 32)
                            act.wait_ge(A.s, q + 1)
                            if later(q - 3):
                                act.wait_ge(A.pv, q - 3)
                            act.activation(PB[i % 4][:, :, :], bank[i % 2][:, :].rearrange("p (k t) -> p k t", k=2),
                                           ACT.Exp).then_inc(A.e, 1)
                        if pre and i == 11:
                            act.wait_ge(A.k, c + 2)
                            if later(c * 2 + 2):
                                act.wait_ge(A.parts, c * 2 + 2)
                            act.activation(qk32[1][:, :], bank[6][:, :], ACT.Identity,
                                           bias=wt("bk")[:, 0:1]).then_inc(A.kev, 1)
                        if post and i == 12:
                            act.wait_ge(A.anT, c - 1)
                            act.activation(ANT[:, :], bank[6][:, :], ACT.Copy).then_inc(A.anc, 1)
                        if post and i == 29:
                            act.wait_ge(E.turned, c - 1)
                            if later((c - 2) * 16):
                                act.wait_ge(E.h, (c - 2) * 16)
                            act.activation(XT[:, :], bank[6][:, :], ACT.Copy).then_inc(E.xt, 1)
                        lag, kind, e, k = UNITS[i]
                        if kind == "W1" and (post, exp, fin)[lag - 2]:
                            relu(n - lag, e, k)
                        if (i == 1 and post) or (i in (9, 17, 25) and att):
                            copy_sums(i)
                        if pre and i == 16:
                            act.wait_ge(A.v, c + 2)
                            if later(c + 1):
                                act.wait_ge(A.vcopied, c + 1)
                            act.activation(VS[:, :, :], tiles(6), ACT.Copy).then_inc(A.vev, 1)
                experts_steps(act, step)

            def attn(run, xp):
                def step(n, par, pre, mid, main):
                    if pre:
                        act.wait_ge(V.turned, n + 3)
                        if later(n * 4 + 8):
                            act.wait_ge(V.proj, n * 4 + 8)
                        act.activation(YVT[:, :], bank[0][:, :], ACT.Copy).then_inc(V.copied, 1)
                    if main:
                        for t in range(TP):
                            act.wait_ge(V.nmx, n * 2 + (1 + t // 2))
                            act.activation(PA[:, t, :], bank[5 + t // 2][:, (t % 2) * T:(t % 2) * T + T], ACT.Exp,
                                           bias=nmx[:, t:t + 1], accum_out=esum[:, t:t + 1]).then_inc(V.e, 1)
                        for u in range(2):
                            act.wait_ge(V.pT, n * 2 + (1 + u))
                            act.activation(PAT[u][:, :], bank[3 + u][:, :], ACT.Copy).then_inc(V.pc, 1)
                    if mid:
                        for h in range(2):
                            act.wait_ge(V.kqT, n * 2 + (3 + h))
                            if later(n * 2 + 2):
                                act.wait_ge(V.s, n * 2 + 2)
                            act.activation(kqT[h][:, :], bank[3 + h][:, :], ACT.Copy).then_inc(V.kqc, 1)
                attn_steps(act, step)

            act.wait_ge(w_loaded, 16 * LOADS)
            act.wait_ge(setup_done, 1)
            run_phases(act, {"ffn": ffn, "linear": linear, "experts": experts, "attn": attn})

        @block.tensor
        def _(pe):
            ident = wt("ident")

            def ffn(run, xp):
                def step(it):
                    n0 = it * 2
                    for b in range(2):
                        pe.wait_ge(F.norm, n0 + (8 * run + 1 + b))
                        for t in range(TP):
                            last = pe.transpose(bank[b][:, t * P:(t + 1) * P], FY[b][:, t, :], ident)
                        last.then_inc(F.turned, 1)
                    for b in range(2):
                        pe.wait_ge(F.copied, n0 + (8 * run + 1 + b))
                        pe.wait_ge(x_done, n0 + (8 * xp - 1 + b))
                        for t in range(TP):
                            last = pe.matmul(bank[2 + b][:, t * P:(t + 1) * P], FYT[b][:, t * P:(t + 1) * P],
                                             wt("cbt"), start=True, stop=True)
                        last.then_inc(F.mm, 1)
                pairs(pe, step)

            def linear(run, xp):
                vm0 = PACK["vmg"][0]

                def sums(j, seq, par, s):
                    b = s // 4
                    s %= 4
                    pe.wait_ge(L.a0, j + 1)
                    pe.wait_ge(L.a1, j + 1)
                    if s % 2 == 0:
                        if later(seq * 2 + (s // 2 - 1)):
                            pe.wait_ge(L.ocopied, seq * 2 + (s // 2 - 1))
                    for c in range(4):
                        o = bank[4 + s // 2][32 * c:32 * c + 32, (s % 2) * T:(s % 2) * T + T]
                        v = VG[par]
                        pe.matmul(o, v[:, 2 * b, 2 * s + c // 2, :], A0[s % 2][:, c, :], start=True, stop=False)
                        last = pe.matmul(o[:, P:T], v[:, 2 * b + 1, 2 * s + c // 2, :], A1[s % 2][:, c, :],
                                         start=False, stop=True)
                    last.then_inc(L.av, 1)

                def decays(n, i, par, c):
                    b, s = i // 4, i % 4
                    if later(n * 24 + (3 * i + c - 1)):
                        pe.wait_ge(L.bcused, n * 24 + (3 * i + c - 1))
                    for k in range(2 if c < 2 else 4):
                        hj = 4 * s + 2 * c + k if c < 2 else 4 * s + k
                        o, w = (k * T, T) if c < 2 else (k * P, P)
                        last = pe.matmul(bank[(3 * i + c) % 2][:, o:o + w], SEL[:, hj, :],
                                         STK[par][:, b, 0:T] if c < 2 else STK[par][:, b, T:T + P],
                                         start=True, stop=True)
                    last.then_inc(L.bc, 1)

                def scores(n, i, par, u):
                    b, s = i // 4, i % 4
                    if later(n * 16 + (2 * i + u - 1)):
                        pe.wait_ge(L.scopied, n * 16 + (2 * i + u - 1))
                    q = QX[par][:, b, 2 * s:2 * s + 2, :]
                    k = b * T + u * P
                    pe.matmul(bank[2 + u][:, 0:(T if u else 2 * T)], kT[par][:, k:k + P], q[:, :, P:T] if u else q,
                              start=True, stop=True).then_inc(L.s, 1)

                def turn_sums(n, main, b):
                    for t in (2 * b, 2 * b + 1):
                        pe.wait_ge(L.ocopied, n * 4 + (2 * b - 2))
                        if t >= 2:
                            pe.wait_ge(L.ptused, n * 4 + (t - 5))
                        elif main:
                            pe.wait_ge(L.v_used, n + 1)
                            pe.wait_ge(L.stk, n * 2 + 2)
                        else:
                            pe.wait_ge(L.hr, n - 1)
                        for r in range(4):
                            last = pe.transpose(bank[6 + t % 2][:, r * P:(r + 1) * P],
                                                OT0[b][:, r, (t % 2) * P:(t % 2) * P + P], ident)
                        last.then_inc(L.pt, 1)

                def step(n, par, pre, main, post):
                    other = 1 - par
                    for i in range(8):
                        j = n * 8 + i
                        after = (n, i + 1, par) if i < 7 else (n + 1, 0, other)
                        after = after if (pre if i == 7 else main) else None
                        if post and i == 0:
                            turn_sums(n, main, 0)
                        if main:
                            decays(n, i, par, 2)
                        if after:
                            if i == 7:
                                pe.wait_ge(L.qx, n * 8 + 16)
                                pe.wait_ge(L.stk, n * 2 + 4)
                            scores(*after, 0)
                            decays(*after, 0)
                            scores(*after, 1)
                        if (i == 0 and post) or (i > 0 and main):
                            if i == 1:
                                pe.wait_ge(L.v_used, n + 1)
                            sums(j - 1, n * 2 + ((i - 1) // 4), par if i else other, (i - 1) % 8)
                        if after:
                            decays(*after, 1)
                        if post and i == 1:
                            turn_sums(n, main, 1)
                        if pre and i == 2:
                            pe.wait_ge(L.norm, n + 2)
                            if later(n + 1):
                                pe.wait_ge(L.v_used, n + 1)
                            if later(n * 4 - 1):
                                pe.wait_ge(L.ptused, n * 4 - 1)
                            for t in range(TP):
                                last = pe.transpose(bank[6][:, t * P:(t + 1) * P], Y0[other][:, t, :], ident)
                            last.then_inc(L.turned, 1)
                        if post and i == 2:
                            pe.wait_ge(L.yo, n * 2)
                            for t in range(TP):
                                last = pe.transpose(bank[7][:, t * P:(t + 1) * P], YO[:, t, :], ident)
                            last.then_inc(L.yoT, 1)
                        if pre and i == 3:
                            pe.wait_ge(L.copied, n + 2)
                            if later(n):
                                pe.wait_ge(L.yoc, n)
                            if later(n * 4):
                                pe.wait_ge(L.ptused, n * 4)
                            pe.matmul(bank[7][:, :], wt("q0"), YT0[:, :], start=True, stop=True).then_inc(L.qk, 1)
                            pe.matmul(bank[6][:, :], wt("k0"), YT0[:, :], start=True, stop=True).then_inc(L.qk, 1)
                            pe.wait_ge(L.exp4, n * 4 + 6)
                            for t in range(TP):
                                last = pe.matmul(bank[7][:, 40 * t:40 * t + 40], YT0[:, t * P:(t + 1) * P],
                                                 W[:, vm0 + P:vm0 + 168], start=True, stop=True)
                            last.then_inc(L.mg, 1)
                        if post and i == 4:
                            if pre:
                                pe.wait_ge(L.exp4, n * 4 + 8)
                            pe.wait_ge(L.yoc, n)
                            for t in range(TP):
                                last = pe.matmul(bank[6][:, t * P:(t + 1) * P], YOT[:, t * P:(t + 1) * P],
                                                 wt("out0"), start=True, stop=True)
                            last.then_inc(L.wo, 1)
                        if pre and i == 6:
                            if not post:
                                pe.wait_ge(L.exp4, n * 4 + 8)
                            if later(n):
                                pe.wait_ge(L.hr, n)
                            pe.wait_ge(L.e0, n + 2)
                            pe.wait_ge(L.bt, n + 2)
                            for t in range(TP):
                                last = pe.transpose(bank[7][:, t * P:(t + 1) * P], BT[:, t, :], ident)
                            last.then_inc(L.bT, 1)
                            for t in range(TP):
                                last = pe.matmul(bank[6][:, t * P:(t + 1) * P], YT0[:, t * P:(t + 1) * P],
                                                 W[:, vm0:vm0 + P], start=True, stop=True)
                            last.then_inc(L.vmg, 1)

                linear_steps(pe, step)

            def experts(run, xp):
                g8 = 8 * run

                def unit(p, kind, e, k):
                    c = p + g8
                    if kind == "W1":
                        if (e, k) == (0, 0):
                            pe.wait_ge(E.xt, c + 1)
                        if later(c * 16 + (4 * e + k)):
                            pe.wait_ge(E.relu, c * 16 + (4 * e + k))
                        pe.matmul(bank[5][:, :], W1[:, e, k * P:(k + 1) * P], XT[:, :], start=True,
                                  stop=True).then_inc(E.h, 1)
                        return
                    if k == 0:
                        pe.wait_ge(E.relu, c * 16 + (4 * e + 4))
                        if later(c * 4 + e):
                            pe.wait_ge(E.yused, c * 4 + e)
                    for q in range(CH):
                        last = pe.matmul(bank[7][:, k * P:(k + 1) * P], HB[e % 2][:, q, k * P:(k + 1) * P],
                                         W2[:, e, q, :], start=(q == 0), stop=(q == CH - 1))
                    if k == TP - 1:
                        last.then_inc(E.y, 1)

                def weigh(q, par, seq, b, s):
                    pe.wait_ge(A.e, q + 1)
                    if s % 8 == 0:
                        if later(seq * 2 + s // 8):
                            pe.wait_ge(A.ocopied, seq * 2 + s // 8)
                    o = bank[4][32 * (s % 4):32 * (s % 4) + 32, (s // 4 % 2) * T:(s // 4 % 2) * T + T]
                    for kt in range(2):
                        last = pe.matmul(o, V1[par][:, 2 * b + kt, s, :], PB[s % 4][:, kt, :],
                                         start=(kt == 0), stop=(kt == 1))
                    last.then_inc(A.pv, 1)

                def turn_sums(c, t):
                    pe.wait_ge(A.ocopied, c * 4 + (2 * (t // 2) - 6))
                    for r in range(4):
                        last = pe.transpose(bank[6][:, r * P:(r + 1) * P],
                                            OT1[t // 2][:, r, (t % 2) * P:(t % 2) * P + P], ident)
                    last.then_inc(A.pt, 1)

                def turn(src, done):
                    for t in range(TP):
                        last = pe.transpose(bank[6][:, t * P:(t + 1) * P], src[:, t, :], ident)
                    last.then_inc(done, 1)

                def project(src, weight, done):
                    for t in range(TP):
                        last = pe.matmul(bank[6][:, t * P:(t + 1) * P], src[:, t * P:(t + 1) * P], weight,
                                         start=True, stop=True)
                    last.then_inc(done, 1)

                def step(n, par, pre, mx, att, post, exp, fin):
                    c = n + g8
                    other = 1 - par

                    def upto(lag):
                        return n + (1 - lag + g8) if not isinstance(n, int) else min(max(n - lag + 1, 0), PAIRS) + g8

                    for i in range(SLOTS_H):
                        b, s = i // 16, i % 16
                        q = c * 32 + (i - 32)
                        if att:
                            a, g = s % 2, s // 2
                            if later(q - 1):
                                pe.wait_ge(A.e, q - 1)
                            if s == 0:
                                pe.wait_ge((A.ml0, A.ml1)[b], c * 32)
                                pe.wait_ge(A.vcopied, c)
                            for kt in range(2):
                                last = pe.matmul(bank[i % 2][:, kt * T:(kt + 1) * T],
                                                 KS[other][64 * a:64 * a + KROWS, b, g, kt * P:(kt + 1) * P],
                                                 QS[other][64 * a:64 * a + KROWS, b, g, :], start=True, stop=True)
                            last.then_inc(A.s, 1)
                        if mx:
                            qt, a, g = s // 8, s % 2, s % 8 // 2 * 2
                            if later(c * 32 + (i - 1)):
                                pe.wait_ge(A.red, c * 32 + (i - 1))
                            if s == 0:
                                pe.wait_ge((A.qkl0, A.qkl1)[b], c * 64 + 64)
                            for u in range(2):
                                r = slice(64 * a, 64 * a + SLOTS * D1)
                                last = pe.matmul(bank[2 + i % 2][:, u * T:(u + 1) * T],
                                                 QS[par][r, b, g + u, qt * P:(qt + 1) * P],
                                                 KS[par][r, b, g + u, :], start=True, stop=True)
                            last.then_inc(A.mx, 1)
                        lag, kind, e, k = UNITS[i]
                        if (post, exp, fin)[lag - 2]:
                            unit(n - lag, kind, e, k)
                        if i < 2 and post:
                            weigh(q - 2, par, c * 2 - 3, 1, i + 14)
                        if i >= 2 and att:
                            weigh(q - 2, other, c * 2 + ((i - 2) // 16 - 2), (i - 2) // 16, (i - 2) % 16)
                        if att and i == 1:
                            pe.wait_ge(A.red, c * 32)
                            pe.wait_ge(A.m0ev, upto(1))
                            if later(upto(3)):
                                pe.wait_ge(E.xt, upto(3))
                            for t in range(2):
                                last = pe.transpose(bank[6][0:H1, t * P:(t + 1) * P], NM[:, 2 + t, :], ident)
                            last.then_inc(A.m1T, 1)
                        if post and i == 3:
                            pe.wait_ge(A.m1ev, upto(1))
                            if later(upto(3)):
                                pe.wait_ge(E.xt, upto(3))
                            turn_sums(c, 0)
                        if post and i == 5:
                            pe.wait_ge(A.norm1, c * 4 - 7)
                            turn_sums(c, 1)
                        if pre and i == 6:
                            pe.wait_ge(A.norm, c + 2)
                            if post:
                                pe.wait_ge(A.norm1, c * 4 - 6)
                            else:
                                if later(upto(1)):
                                    pe.wait_ge(A.m1ev, upto(1))
                                if later(upto(1)):
                                    pe.wait_ge(A.m0ev, upto(1))
                                if later(upto(0)):
                                    pe.wait_ge(A.vev, upto(0))
                            turn(Y1[other], A.turned)
                        if post and i == 7:
                            pe.wait_ge(A.norm1, c * 4 - 6)
                            pe.wait_ge(A.copied, upto(-1))
                            turn_sums(c, 2)
                        if pre and i == 8:
                            pe.wait_ge(A.copied, c + 2)
                            if post:
                                pe.wait_ge(A.norm1, c * 4 - 5)
                            pe.matmul(bank[6][:, :], wt("q1"), YT1[:, :], start=True, stop=True).then_inc(A.q, 1)
                        if post and i == 9:
                            pe.wait_ge(A.norm1, c * 4 - 5)
                            pe.wait_ge(A.qev, upto(-1))
                            turn_sums(c, 3)
                        if pre and i == 10:
                            pe.wait_ge(A.qev, c + 2)
                            if post:
                                pe.wait_ge(A.norm1, c * 4 - 4)
                            pe.matmul(bank[6][:, :], wt("k1"), YT1[:, :], start=True, stop=True).then_inc(A.k, 1)
                        if post and i == 11:
                            pe.wait_ge(A.norm1, c * 4 - 4)
                            pe.wait_ge(A.kev, upto(-1))
                            turn(AN, A.anT)
                        if post and i == 13:
                            pe.wait_ge(A.anc, c - 1)
                            project(ANT, wt("o1"), A.wo)
                        if pre and i == 15:
                            pe.wait_ge(A.kev, c + 2)
                            if later(upto(2)):
                                pe.wait_ge(A.z, upto(2))
                            project(YT1, wt("v1"), A.v)
                        if mx and i == 20:
                            pe.wait_ge(A.red, c * 32 + 16)
                            pe.wait_ge(A.vev, upto(-1))
                            if later(upto(2)):
                                pe.wait_ge(A.z, upto(2))
                            for t in range(2):
                                last = pe.transpose(bank[6][0:H1, t * P:(t + 1) * P], NM[:, t, :], ident)
                            last.then_inc(A.m0T, 1)
                        if post and i == 26:
                            pe.wait_ge(A.m0ev, upto(0))
                            pe.wait_ge(A.z, c - 1)
                            pe.wait_ge(A.x1, c - 1)
                            turn(XS[par], E.turned)

                pe.wait_ge(x_done, 8 * xp)
                if run == 0:
                    pe.wait_ge(A.ready, 64)
                experts_steps(pe, step)

            def attn(run, xp):
                def step(n, par, pre, mid, main):
                    other = 1 - par
                    if main:
                        pe.wait_ge(V.kqc, n * 2 + 2)
                        for t in range(TP):
                            last = pe.matmul(bank[5 + t // 2][:, (t % 2) * T:(t % 2) * T + T],
                                             kqT[0][:, t * P:(t + 1) * P],
                                             kqT[1][:, (t // 2) * T:(t // 2) * T + T], start=True, stop=True)
                            if t % 2:
                                last.then_inc(V.s, 1)
                    if pre:
                        pe.wait_ge(V.norm, n + 3)
                        for t in range(TP):
                            last = pe.transpose(bank[0][:, t * P:(t + 1) * P], YV[par][:, t, :], ident)
                        last.then_inc(V.turned, 1)
                        pe.wait_ge(V.copied, n + 3)
                        a0 = PACK["kqv"][0]
                        for t in range(TP):
                            if later(n * 4 + (t + 7)):
                                pe.wait_ge(V.biased, n * 4 + (t + 7))
                            pe.matmul(bank[1 + t % 2][:, 0:3 * P], YVT[:, t * P:(t + 1) * P], W[:, a0:a0 + 3 * P],
                                      start=True, stop=True).then_inc(V.proj, 1)
                    if main:
                        pe.wait_ge(V.e, n * 4 + 4)
                        for u in range(2):
                            for t in range(TP):
                                last = pe.transpose(bank[3 + u][:, t * P:(t + 1) * P], PA[:, t, u * P:(u + 1) * P],
                                                    ident)
                            last.then_inc(V.pT, 1)
                        pe.wait_ge(V.pc, n * 2 + 2)
                        pe.wait_ge(x_done, n + 8 * xp)
                        for t in range(TP):
                            for u in range(2):
                                last = pe.matmul(bank[7][:, t * P:(t + 1) * P], PAT[u][:, t * P:(t + 1) * P],
                                                 KQV[par][:, 2 * (t // 2) + u, 2, :], start=(u == 0), stop=(u == 1))
                        last.then_inc(V.av, 1)
                    if mid:
                        pe.wait_ge(V.kqv, n + 2)
                        for h in range(2):
                            for t in range(TP):
                                last = pe.transpose(bank[3 + h][:, t * P:(t + 1) * P], KQV[other][:, t, h, :], ident)
                            last.then_inc(V.kqT, 1)
                pe.wait_ge(x_done, 8 * xp)
                attn_steps(pe, step)

            pe.wait_ge(w_loaded, 16 * LOADS)
            pe.wait_ge(setup_done, 1)
            run_phases(pe, {"ffn": ffn, "linear": linear, "experts": experts, "attn": attn})

        @block.vector
        def _(dve):
            def xs(n):
                return lambda t: X[:, bass.ds(n * TP + t, 1), :].rearrange("p o c -> p (o c)")

            def ffn(run, xp):
                def step(it):
                    n0 = it * 2
                    link = Link(dve, F.link, it + 4 * run, 4)
                    for b in range(2):
                        dve.wait_ge(x_done, n0 + (8 * xp - 7 + b))
                        token_stats(dve, xs(n0 + b), (st, st2)[b], (mv, mv2)[b], (ve, ve2)[b], link, F.var)
                    for b in range(2):
                        dve.wait_ge(F.rstd, n0 + (8 * run + 1 + b))
                        token_norm(dve, xs(n0 + b), lambda t, b=b: FY[b][:, t, :], (mv, mv2)[b],
                                   (rs, rs2)[b]).then_inc(F.norm, 1)
                    for b in range(2):
                        dve.wait_ge(F.mm, n0 + (8 * run + 1 + b))
                        dve.wait_ge(F.xb, n0 + (8 * run + 1 + b))
                        dve.tensor_tensor(X[:, bass.ds((n0 + b) * TP, TP), :], tiles(2 + b), XB[b][:, :, :],
                                          ALU.add).then_inc(x_done, 1)
                    link.close()
                pairs(dve, step)

            def linear(run, xp):
                def finish_tiles(link, n, b, other):
                    ps = [bank[6 + u][:, :].rearrange("p (h e) -> p h e", e=32) for u in range(2)]
                    for u in range(2):
                        dve.wait_ge(L.pt, n * 4 + (2 * b + u - 3))
                        last = dve.tensor_scalar(den[:, u, :], ps[u][:, :, D0], DEN_EPS, None, ALU.add)
                    link(last)
                    link(dve.reciprocal(rec[:, :, :], den[:, :, :]))
                    link(dve.tensor_tensor(rw0[:, :, :], rec[:, :, :], WM[other][:, 2 * b:2 * b + 2, :], ALU.mult))
                    for u in range(2):
                        dve.tensor_tensor(PR[:, u, :, :], ps[u][:, :, 0:D0],
                                          over(rw0[:, u, :].unsqueeze(2), [P, HJ, D0]),
                                          ALU.mult).then_inc(L.ptused, 1)
                    dve.wait_ge(L.ptused, n * 4 + (2 * b - 2))
                    pr = PR[:, :, :, :].rearrange("p u (h j) e -> p (u h) j e", j=J0)
                    dve.tensor_tensor(YO[:, 2 * b:2 * b + 2, :].rearrange("p u (h e) -> p (u h) e", e=D0),
                                      pr[:, :, 0, :], pr[:, :, 1, :], ALU.add).then_inc(L.yo, 1)

                def slot(n, i):
                    j = n * 8 + i
                    if later(j - 1):
                        dve.wait_ge(L.a0, j - 1)
                    for c in range(3):
                        if c == 2:
                            dve.wait_ge(L.bcused, j * 3 + 2)
                            dve.wait_ge(L.scopied, j * 2 + 1)
                            if later(j - 1):
                                dve.wait_ge(L.av, j - 1)
                            s = SS[i % 2][:, 0:512].rearrange("p (h o t) -> p h o t", h=2, o=1)
                            dve.tensor_tensor(A0[i % 2][:, :, :].rearrange("p (h j) t -> p h j t", h=2),
                                              DD0[i % 2][:, :].rearrange("p (h j t) -> p h j t", h=2, j=2),
                                              over(s, [P, 2, 2, T]), ALU.mult).then_inc(L.a0, 1)
                            if later(j - 1):
                                dve.wait_ge(L.a1, j - 1)
                        dve.wait_ge(L.bc, j * 3 + (c + 1))
                        dst = DD0[i % 2][:, 512 * c:512 * c + 512] if c < 2 else DD1[i % 2][:, :]
                        dve.tensor_tensor_scan(dst, bank[(3 * i + c) % 2][:, :], (I0 if c < 2 else I1)[:, :], 0.0,
                                               ALU.mult, ALU.add).then_inc(L.bcused, 1)

                def step(n, par, pre, main, post):
                    other = 1 - par
                    if pre:
                        link_ln, link_beta = Link(dve, L.link_ln, n + 1, 2), Link(dve, L.link_beta, n + 1, 7)
                        link_gate = Link(dve, L.link_gate, n + 1, 4)
                    if post:
                        link_post, link_out = Link(dve, L.link_post, n - 1, 6), Link(dve, L.link_out, n - 1, 2)
                    for i in range(8):
                        if pre and i == 0:
                            dve.wait_ge(x_done, n + (8 * xp - 6))
                            token_stats(dve, xs(n + 1), st, mv, ve, link_ln, L.var)
                        if main:
                            slot(n, i)
                        if pre and i == 1:
                            dve.wait_ge(L.rstd, n + 2)
                            if later(n):
                                dve.wait_ge(L.yr, n)
                            token_norm(dve, xs(n + 1), lambda t: Y0[other][:, t, :], mv, rs).then_inc(L.norm, 1)
                        if post and i in (0, 1):
                            finish_tiles(link_post, n, i, other)
                        if pre and i == 4:
                            dve.wait_ge(L.mg, n + 2)
                            r = ROW["bmg"]
                            link_gate(dve.tensor_tensor(MG[:, :, :],
                                                        bank[7][:, 0:TP * 40].rearrange("p (t c) -> p t c", t=TP),
                                                        over(R[:, r:r + 1, 0:40], [P, TP, 40]), ALU.add))
                            mix = MG[:, :, 0:HJ].rearrange("p t (h j) -> p t h j", j=J0)
                            link_gate(dve.tensor_tensor(mx[:, :, :], mix[:, :, :, 0], mix[:, :, :, 1], ALU.max))
                            dve.tensor_tensor(E0[:, :, 0:HJ].rearrange("p t (h j) -> p t h j", j=J0), mix,
                                              over(mx[:, :, :].unsqueeze(3), [P, TP, H0, J0]), ALU.subtract)
                            dve.tensor_scalar(E0[:, :, HJ:40], MG[:, :, HJ:40], -1.0, None,
                                              ALU.mult).then_inc(L.e0, 1)
                        if pre and i == 4:
                            if later(n * 8 + 8):
                                dve.wait_ge(L.qx, n * 8 + 8)
                            dve.wait_ge(L.exp4, n * 4 + 6)
                            dve.scalar_tensor_tensor(out=qf[:, :], in0=ex[:, 0, :], scalar=1.0, in1=re[:, 0, :],
                                                     op0=ALU.min, op1=ALU.add)
                            dve.wait_ge(L.exp4, n * 4 + 8)
                            dve.scalar_tensor_tensor(out=kT[other][:, :], in0=ex[:, 1, :], scalar=1.0,
                                                     in1=re[:, 1, :], op0=ALU.min, op1=ALU.add).then_inc(L.qf, 1)
                        if pre and i == 4:
                            dve.wait_ge(L.e1, n + 2)
                            e = E1[:, :, 0:HJ].rearrange("p t (h j) -> p t h j", j=J0)
                            dve.tensor_tensor(SD[:, :, 0:H0], e[:, :, :, 0], e[:, :, :, 1], ALU.add)
                            link_gate(dve.tensor_scalar(SD[:, :, H0:32], E1[:, :, HJ:40], 1.0, None, ALU.add))
                            link_gate(dve.reciprocal(RD[:, :, :], SD[:, :, :]))
                            dve.tensor_tensor(WM[other][:, :, :].rearrange("p t (h j) -> p t h j", j=J0), e,
                                              over(RD[:, :, 0:H0].unsqueeze(3), [P, TP, H0, J0]), ALU.mult)
                            r = ROW["decay"]
                            link_beta(dve.tensor_tensor(bE[:, :, :], RD[:, :, HJ:32],
                                                        over(R[:, r:r + 1, 0:HJ], [P, TP, HJ]), ALU.mult))
                            link_beta(dve.tensor_scalar(bE[:, :, :], bE[:, :, :], 0.9999, None, ALU.min))
                            link_beta(dve.tensor_copy(part[0][:, :, :], bE[:, :, :]))
                        if pre and i == 5:
                            link_beta(dve.tensor_tensor(bR[:, :, :], bE[:, :, :], part[0][:, :, :], ALU.subtract))
                            link_beta(dve.tensor_copy(part[1][:, :, :], bR[:, :, :]))
                            link_beta(dve.tensor_tensor(bE[:, :, :], bR[:, :, :], part[1][:, :, :], ALU.subtract))
                            link_beta(dve.tensor_copy(part[2][:, :, :], bE[:, :, :]))
                            for k, c in enumerate(BETA_ROWS):
                                last = dve.tensor_copy(BT[:, :, c:c + HJ], part[k][:, :, :])
                            last.then_inc(L.bt, 1)
                            link_beta.close()
                        if post and i == 5:
                            dve.wait_ge(L.wo, n)
                            dve.wait_ge(L.yr, n)
                            dve.tensor_tensor(HR[:, :, :], tiles(6), YR0[:, :, :], ALU.add).then_inc(L.hr, 1)
                            dve.wait_ge(L.hr, n)
                            token_stats(dve, lambda t: HR[:, t, :], st2, mv2, ve2, link_out, L.var2)
                        if post and i == 6:
                            dve.wait_ge(L.rstd2, n)
                            token_norm(dve, lambda t: HR[:, t, :], lambda t: HN[:, t, :], mv2, rs2).then_inc(L.hn, 1)
                        if pre and i == 7:
                            dve.wait_ge(L.vmg, n + 2)
                            dve.tensor_tensor(VG[other][:, :, :, 0:D0],
                                              tiles(6).rearrange("p t (h e) -> p t h e", e=D0),
                                              over(RD[:, :, H0:HJ].unsqueeze(3), [P, TP, H0, D0]), ALU.mult)
                            dve.tensor_copy(VG[other][:, :, :, D0], RD[:, :, H0:HJ]).then_inc(L.v_used, 1)
                            link_gate.close()
                    if pre:
                        link_ln.close()
                    if post:
                        link_post.close()
                        link_out.close()
                        dve.wait_ge(L.xd, n)
                        at = bass.ds((n - 1) * TP, TP)
                        dve.tensor_tensor(X[:, at, :], X[:, at, :], HG[:, :, :], ALU.add).then_inc(x_done, 1)
                linear_steps(dve, step)

            def experts(run, xp):
                g8 = 8 * run
                SCALE = float(D1) ** -0.5

                def split_max(c, b):
                    index, evacuated, written, free = ((2 * c, A.m0ev, A.mwr0, c), (2 * c + 1, A.m1ev, A.mwr1, c))[b]
                    dve.wait_ge((A.m0T, A.m1T)[b], c + 1)
                    if later(free * 16):
                        dve.wait_ge(written, free * 16)
                    link = Link(dve, A.link_m, index, 1)
                    ps = bank[6][0:H1, 0:T]
                    link(dve.tensor_copy(MH[b][:, 0, :], ps))
                    dve.tensor_tensor(MH[b][:, 1, :], ps, MH[b][:, 0, :], ALU.subtract).then_inc(evacuated, 1)

                def take(n, e):
                    c = n + g8
                    if later(c * 4 + e):
                        dve.wait_ge(E.acc, c * 4 + e)
                    dve.wait_ge(E.y, c * 4 + (e + 1))
                    dve.tensor_tensor(YB[:, :, :], tiles(7), row4(f"b2_{e}"), ALU.add).then_inc(E.yused, 1)

                def gather(n, par, e):
                    c = n + g8
                    dve.wait_ge(E.yused, c * 4 + (e + 1))
                    if e == 0:
                        dve.wait_ge(E.mask, c + 1)
                        if later(c):
                            dve.wait_ge(E.norm, c)
                    for t in range(TP):
                        last = dve.scalar_tensor_tensor(out=AC[:, t, :], in0=YB[:, t, :],
                                                        scalar=MK[par][:, e, t:t + 1],
                                                        in1=(AC if e else XS[par])[:, t, :], op0=ALU.mult,
                                                        op1=ALU.add)
                    last.then_inc(E.acc, 1)

                def stats(src, st_, link):
                    for t in range(TP):
                        last = dve.bn_stats(st_[:, t, :], src(t))
                    link(last)

                def moments(st_, mv_, ve_, link, var_sem):
                    dve.memset(tick[:, :], 0.0)
                    for t in range(TP):
                        last = dve.bn_aggr(mv_[:, t, :], st_[:, t, :])
                    link(last)
                    dve.tensor_scalar(ve_[:, :], mv_[:, :, 1], LN_EPS, None, ALU.add).then_inc(var_sem, 1)

                def scale(src, dst, mv_, rs_, tt):
                    for t in tt:
                        last = dve.tensor_scalar(dst(t), src(t), mv_[:, t, 0:1], rs_[:, t:t + 1], ALU.subtract,
                                                 ALU.mult)
                    return last

                def masks(n, par, acc):
                    c = n + g8
                    link = Link(dve, E.link_key, c, 10)
                    dve.wait_ge(A.x1, c + 1)
                    if later(acc):
                        dve.wait_ge(E.acc, acc)
                    link(dve.tensor_tensor(KP[:, :, :], XS[par][:, :, :], row4("rw"), ALU.mult))
                    link(dve.tensor_reduce(key[0][:, :], KP[:, :, :], AX_X, ALU.add))
                    link(dve.tensor_scalar(key[0][:, :], key[0][:, :], row("rb")[:, 0:1], None, ALU.add))
                    link(dve.tensor_copy(kint[:, :], key[0][:, :]))
                    link(dve.tensor_copy(key[1][:, :], kint[:, :]))
                    link(dve.tensor_tensor(key[2][:, :], key[1][:, :], key[0][:, :], ALU.is_gt))
                    link(dve.tensor_tensor(key[1][:, :], key[1][:, :], key[2][:, :], ALU.subtract))
                    link(dve.tensor_copy(kint[:, :], key[1][:, :]))
                    link(dve.tensor_scalar(kint[:, :], kint[:, :], EXPERTS - 1, None, ALU.bitwise_and))
                    link(dve.tensor_copy(key[2][:, :], kint[:, :]))
                    for e in range(EXPERTS):
                        last = dve.tensor_scalar(MK[par][:, e, :], key[2][:, :], float(e), None, ALU.is_equal)
                    last.then_inc(E.mask, 1)
                    link.close()

                def step(n, par, pre, mx, att, post, exp, fin):
                    c = n + g8
                    other = 1 - par
                    if pre:
                        link_x = Link(dve, A.link_ln, c + 1, 2)
                    if post:
                        link_n, link_z = Link(dve, A.link_n, c - 2, 4), Link(dve, A.link_z, c - 2, 2)
                    if fin:
                        link_e = Link(dve, E.link_ln, c - 4, 2)

                    def divide(t):
                        ps = bank[6][:, :].rearrange("p (h e) -> p h e", e=32)
                        dve.wait_ge(A.pt, c * 4 + (t - 7))
                        link_n(dve.reciprocal(rec1[:, t, :], ps[:, :, D1]))
                        dve.tensor_tensor(AN[:, t, :].rearrange("p (h e) -> p h e", e=D1), ps[:, :, 0:D1],
                                          over(rec1[:, t, :].unsqueeze(2), [P, H1, D1]),
                                          ALU.mult).then_inc(A.norm1, 1)

                    def y(t):
                        return Y1[other][:, t, :]

                    for i in range(SLOTS_H):
                        b, s = i // 16, i % 16
                        if mx:
                            qt, a, g = s // 8, s % 2, s % 8 // 2 * 2
                            dve.wait_ge(A.mx, c * 32 + (i + 1))
                            h = 2 * g + a
                            dve.tensor_reduce(NM[:, 2 * b + qt, h:h + 3:2],
                                              bank[2 + i % 2][:, :].rearrange("p (u t) -> p u t", u=2), AX_X,
                                              ALU.max, negate=True).then_inc(A.red, 1)
                        if pre and i == 0:
                            dve.wait_ge(x_done, n + (8 * xp - 6))
                            stats(xs(n + 1), st, link_x)
                        if pre and i == 1:
                            moments(st, mv, ve, link_x, A.var)
                        if pre and i == 3:
                            dve.wait_ge(A.rstd, c + 2)
                            if later(c):
                                dve.wait_ge(A.yr, c)
                            scale(xs(n + 1), y, mv, rs, (0, 1))
                        if pre and i == 9:
                            dve.wait_ge(A.q, c + 2)
                            if later(c * 2 + 2):
                                dve.wait_ge(A.r1, c * 2 + 2)
                            dve.tensor_scalar(qk32[0][:, :], bank[6][:, :], wt("bq")[:, 0:1], SCALE, ALU.add,
                                              ALU.mult).then_inc(A.qev, 1)
                        if att and i == 2:
                            split_max(c - 1, 1)
                        if post and i in (4, 6, 8, 10):
                            divide(i // 2 - 2)
                        if pre and i == 4:
                            scale(xs(n + 1), y, mv, rs, (2, 3)).then_inc(A.norm, 1)
                        if pre and i == 10:
                            dve.wait_ge(A.qev, c + 2)
                            if later(c * 192 + 192):
                                dve.wait_ge(A.scr, c * 192 + 192)
                            dve.tensor_copy(PQ[0][:, 0, :], qk32[0][:, :]).then_inc(A.hi, 1)
                        if pre and i == 11:
                            dve.wait_ge(A.kev, c + 2)
                            dve.tensor_copy(PQ[1][:, 0, :], qk32[1][:, :]).then_inc(A.hi, 1)
                        if pre and i in (12, 13):
                            h = i - 12
                            dve.wait_ge(A.r1, c * 2 + (3 + h))
                            dve.tensor_copy(PQ[h][:, 1, :], qkr[h][:, :]).then_inc(A.mid, 1)
                        if post and i == 14:
                            dve.wait_ge(A.wo, c - 1)
                            dve.wait_ge(A.yr, c - 1)
                            dve.tensor_tensor(Z[:, :, :], tiles(6), YR1[par][:, :, :], ALU.add).then_inc(A.z, 1)
                        if post and i == 16:
                            dve.wait_ge(A.z, c - 1)
                            stats(lambda t: Z[:, t, :], st2, link_z)
                        if post and i == 17:
                            moments(st2, mv2, ve2, link_z, A.var2)
                        if post and i == 20:
                            dve.wait_ge(A.rstd2, c - 1)
                            scale(lambda t: Z[:, t, :], lambda t: ZN[:, t, :], mv2, rs2, (0, 1))
                        if mx and i == 21:
                            split_max(c, 0)
                        if post and i == 21:
                            scale(lambda t: Z[:, t, :], lambda t: ZN[:, t, :], mv2, rs2, (2, 3)).then_inc(A.zn, 1)
                        if fin and i == 6:
                            take(n - 4, 3)
                        if fin and i == 7:
                            gather(n - 4, par, 3)
                        if fin and i == 11:
                            dve.wait_ge(E.acc, c * 4 - 12)
                            stats(lambda t: AC[:, t, :], st3, link_e)
                        if fin and i == 12:
                            moments(st3, mv3, ve3, link_e, E.var)
                        if exp and i == 14:
                            take(n - 3, 0)
                        if fin and i == 15:
                            dve.wait_ge(E.rstd, c - 3)
                            scale(lambda t: AC[:, t, :], lambda t: EN[:, t, :], mv3, rs3,
                                  range(TP)).then_inc(E.norm, 1)
                        if exp and i == 17:
                            gather(n - 3, other, 0)
                        if exp and i == 22:
                            take(n - 3, 1)
                        if exp and i == 23:
                            gather(n - 3, other, 1)
                        if fin and i == 25:
                            dve.wait_ge(E.b, c - 3)
                            at = bass.ds((n - 4) * TP, TP)
                            dve.tensor_tensor(X[:, at, :], X[:, at, :], EG[:, :, :], ALU.add).then_inc(x_done, 1)
                        if post and i == 27:
                            masks(n - 2, par, (c - 2) * 4 - 2)
                        if exp and i == 30:
                            take(n - 3, 2)
                        if exp and i == 31:
                            gather(n - 3, other, 2)
                experts_steps(dve, step)

            def attn(run, xp):
                def step(n, par, pre, mid, main):
                    other = 1 - par
                    if pre:
                        link = Link(dve, V.link_ln, n + 2, 2)
                        dve.wait_ge(x_done, n + (8 * xp - 5))
                        token_stats(dve, xs(n + 2), st, mv, ve, link, V.var)
                        link.close()
                    if mid:
                        dve.wait_ge(V.rstd12, n + 2)
                        for u in range(12):
                            last = dve.tensor_scalar(KQV[other][:, u // 3, u % 3, :], RAW[:, u // 3, u % 3, :],
                                                     mean12[:, u:u + 1], rs12[:, u:u + 1], ALU.subtract, ALU.mult)
                        last.then_inc(V.norm12, 1)
                    if pre:
                        dve.wait_ge(V.rstd, n + 3)
                        if later(n + 1):
                            dve.wait_ge(V.yx, n + 1)
                        token_norm(dve, xs(n + 2), lambda t: YV[par][:, t, :], mv, rs).then_inc(V.norm, 1)
                    if main:
                        for h in range(2):
                            dve.wait_ge(V.s, n * 2 + (1 + h))
                            dve.tensor_reduce(nmx[:, 2 * h:2 * h + 2],
                                              bank[5 + h][:, :].rearrange("p (u t) -> p u t", u=2), AX_X,
                                              ALU.max, negate=True).then_inc(V.nmx, 1)
                    if pre:
                        k = ROW["abk"]
                        if later(n + 2):
                            dve.wait_ge(V.norm12, n + 2)
                        for t in range(TP):
                            dve.wait_ge(V.proj, n * 4 + (t + 9))
                            dve.tensor_tensor(RAW[:, t, :, :].rearrange("p k c -> p (k c)"), bank[1 + t % 2][:, 0:3 * P],
                                              R[:, k:k + 3, :].rearrange("p k c -> p (k c)"),
                                              ALU.add).then_inc(V.biased, 1)
                        dve.wait_ge(V.biased, n * 4 + 12)
                        link = Link(dve, V.link_b, n + 2, 3)
                        for u in range(12):
                            last = dve.bn_stats(st12[:, u, :], RAW[:, u // 3, u % 3, :])
                        link(last)
                        dve.tensor_tensor(dif12[:, :], st12[:, :, 1], st12[:, :, 4], ALU.subtract)
                        dve.tensor_tensor(mean12[:, :], st12[:, :, 1], st12[:, :, 4], ALU.add)
                        link(dve.tensor_tensor(var12[:, :], st12[:, :, 2], st12[:, :, 5], ALU.add))
                        dve.tensor_tensor(dif12[:, :], dif12[:, :], dif12[:, :], ALU.mult)
                        dve.tensor_scalar(mean12[:, :], mean12[:, :], 0.5, None, ALU.mult)
                        link(dve.tensor_scalar(var12[:, :], var12[:, :], 1.0 / P, LN_EPS, ALU.mult, ALU.add))
                        dve.scalar_tensor_tensor(out=ve12[:, :], in0=dif12[:, :], scalar=0.25, in1=var12[:, :],
                                                 op0=ALU.mult, op1=ALU.add).then_inc(V.var12, 1)
                        link.close()
                    if main:
                        dve.wait_ge(V.e, n * 4 + 4)
                        dve.wait_ge(x_done, n + 8 * xp)
                        dve.reciprocal(rsum[:, :], esum[:, :]).then_inc(V.sumr, 1)
                        dve.wait_ge(V.sumr, n + 1)
                        dve.wait_ge(V.av, n + 1)
                        dve.wait_ge(V.yx, n + 1)
                        for t in range(TP):
                            at = X[:, bass.ds(n * TP + t, 1), :].rearrange("p o c -> p (o c)")
                            last = dve.scalar_tensor_tensor(out=at, in0=bank[7][:, t * P:(t + 1) * P],
                                                            scalar=rsum[:, t:t + 1], in1=YX[par][:, t, :],
                                                            op0=ALU.mult, op1=ALU.add)
                        last.then_inc(x_done, 1)
                attn_steps(dve, step)

            dve.wait_ge(w_loaded, 16 * LOADS)
            link = Link(dve, setup_link, 0, 2)
            dve.memset(I0[:, :], 0.0)
            link(dve.tensor_scalar(row("scb"), row("scb"), 0.5 / 127.0, None, ALU.mult))
            for t in (0, 2):
                dve.tensor_copy(I0[:, t * P:(t + 1) * P], wt("ident"))
            for t in range(TP):
                dve.tensor_copy(I1[:, t * P:(t + 1) * P], wt("ident"))
            dve.tensor_tensor(wt("cbt"), wt("cbt"), row("scb"), ALU.mult)
            for name in ("qbias", "ln2g", "ln2b"):
                dve.tensor_scalar(row(name), row(name), 0.5, None, ALU.mult)
            link(dve.tensor_copy(SEL[:, :, :].rearrange("p h c -> p (h c)"), selF))
            link.close()
            dve.tensor_copy(rs[:, :], I1[:, 0:TP]).then_inc(setup_done, 1)
            dve.wait_ge(x_loaded, 16 * PAIRS)
            dve.tensor_copy(rs2[:, :], I1[:, 0:TP]).then_inc(x_done, 8)
            run_phases(dve, {"ffn": ffn, "linear": linear, "experts": experts, "attn": attn})


def _lay_out(a):
    f = np.float32
    g = lambda k: np.asarray(a[k], dtype=f)
    pack = np.zeros((P, PACKED), f)

    def put(name, value):
        at, n = PACK[name]
        pack[:, at:at + n] = np.asarray(value).reshape(P, n)

    put("cbt", g("L0_ffn_CB").T)
    put("q0", g("L0_attn_Wq").T)
    put("k0", g("L0_attn_Wk").T)
    put("vmg", np.concatenate([g("L0_attn_Wv"), g("L0_attn_Wmix"), g("L0_attn_Wgate"),
                               g("L0_attn_Wbeta")], 0).T)
    put("out0", g("L0_attn_Wout").T)
    order = np.array([(2 * gg + aa) * D1 + d for aa in range(2) for d in range(D1) for gg in range(H1 // 2)])
    put("q1", g("L1_ffn_Wq")[:, order])
    put("k1", g("L1_ffn_Wk")[:, order])
    put("bq", g("L1_ffn_bq")[order])
    put("bk", g("L1_ffn_bk")[order])
    put("v1", g("L1_ffn_Wv"))
    put("o1", g("L1_ffn_Wo"))
    put("b1", g("L1_ffn_b1").reshape(EXPERTS * CH, P).T)
    put("kqv", np.concatenate([g("L1_attn_Wk"), g("L1_attn_Wq"), g("L1_attn_Wv")], 1))
    put("hmask", (np.arange(P)[:, None] // D0 == np.arange(H0)[None, :]).astype(f))
    put("ident", np.eye(P, dtype=f))
    sel = np.zeros((P, HJ, P), f)
    for r in BETA_ROWS:
        for h in range(HJ):
            sel[r + h, h, :] = 1.0
    put("sel", sel)
    vec = {"scb": "L0_ffn_SCB", "qbias": "L0_ffn_bias", "bout": "L0_attn_bout", "lng": "L0_attn_ln_g",
           "lnb": "L0_attn_ln_b", "bv": "L1_ffn_bv", "bo": "L1_ffn_bo", "ln1g": "L1_ffn_ln1_g",
           "ln1b": "L1_ffn_ln1_b", "ln2g": "L1_ffn_ln2_g", "ln2b": "L1_ffn_ln2_b", "abk": "L1_attn_bk",
           "abq": "L1_attn_bq", "abv": "L1_attn_bv", "agk": "L1_attn_gk", "agq": "L1_attn_gq", "agv": "L1_attn_gv",
           "aek": "L1_attn_betak", "aeq": "L1_attn_betaq", "aev": "L1_attn_betav"}
    rows = np.zeros((len(ROWS), P), f)
    for name, key in vec.items():
        rows[ROW[name]] = g(key)
    rows[ROW["bmg"], 0:16] = g("L0_attn_bmix")
    rows[ROW["bmg"], 16:24] = g("L0_attn_bgate")
    rows[ROW["bmg"], 24:40] = g("L0_attn_bbeta")
    slopes = np.array([2.0 ** (-8.0 * (h + 1) / H0) for h in range(H0)], f)
    rows[ROW["decay"], 0:HJ] = np.repeat(np.exp(-slopes), J0)
    rows[ROW["rw"]] = g("L1_ffn_router_w")[:, 0]
    rows[ROW["rb"], 0] = g("L1_ffn_router_b")[0]
    for e in range(EXPERTS):
        rows[ROW[f"b2_{e}"]] = g("L1_ffn_b2")[e]
    return {"in_x": g("L0_attn_x").reshape(SEQS * T, P), "in_pack": pack, "in_rows": rows.reshape(-1),
            "in_w1": g("L1_ffn_W1"), "in_w2": g("L1_ffn_W2")}


def kernel(**inputs):
    import concourse.bacc as _bacc
    from concourse.bass_utils import run_bass_kernel_spmd as _run

    nc = _bacc.Bacc("TRN2", target_bir_lowering=False, num_devices=1)
    arrays = {k: np.ascontiguousarray(v) for k, v in _lay_out(inputs).items()}
    args = [nc.dram_tensor(k, v.shape, F32, kind="ExternalInput").ap() for k, v in arrays.items()]
    out = nc.dram_tensor("out_0", (SEQS * T, P), F32, kind="ExternalOutput").ap()
    program(nc, *args, out)
    r = _run(nc, [arrays], core_ids=[0])
    return np.asarray(r.results[0]["out_0"]).reshape(SEQS, T, P)
```

```python
from contextlib import ExitStack

import numpy as np

import concourse.bass as bass
from concourse import mybir

ALU = mybir.AluOpType
ACT = mybir.ActivationFunctionType
AX_X = mybir.AxisListType.X
F32 = mybir.dt.float32
BF16 = mybir.dt.bfloat16
I32 = mybir.dt.int32

P = 128
SEQS, T = 16, 256
TILES = SEQS * T // P
TP = 4
N = TP * P
PAIRS = TILES // TP
H0, J0, D0 = 8, 2, 16
HJ = H0 * J0
H1, D1 = 16, 8
FF, EXPERTS = 512, 4
CH = FF // P
SLOTS = 6
KROWS = SLOTS * D1 + 2
LN_EPS, DEN_EPS = 1e-5, 1e-6
PHASES = ("ffn", "linear", "ffn", "experts", "attn", "experts")

SLOTS_H = 32
UNITS = [None] * SLOTS_H
for _e in range(EXPERTS):
    for _k in range(CH):
        for _kind, _slot in (("W1", 8 * _e + 2 * _k - 2), ("W2", 8 * _e + 2 * _k + 7)):
            UNITS[_slot % SLOTS_H] = (3 + _slot // SLOTS_H, _kind, _e, _k)

ROWS = ("scb", "qbias", "bmg", "bout", "lng", "lnb", "bv", "bo", "ln1g", "ln1b", "ln2g", "ln2b", "rw", "rb",
        "b2_0", "b2_1", "b2_2", "b2_3", "abk", "abq", "abv", "agk", "agq", "agv", "aek", "aeq", "aev", "decay")
ROW = {name: i for i, name in enumerate(ROWS)}
PACK = {}
_at = 0
for _name, _n in (("cbt", 128), ("q0", 128), ("k0", 128), ("vmg", 168), ("out0", 128), ("q1", 128),
                  ("k1", 128), ("v1", 128), ("o1", 128), ("kqv", 384), ("bq", 1), ("bk", 1), ("b1", 16),
                  ("hmask", 8), ("ident", 128)):
    PACK[_name] = (_at, _n)
    _at += _n
PACKED = _at
BETA_ROWS = (0, 64, 96)


def later(count):
    return not isinstance(count, int) or count > 0


class Link:

    def __init__(self, engine, sem, index, per):
        self.engine, self.sem, self.start, self.per, self.k = engine, sem, index * per, per, 0

    def __call__(self, instruction):
        instruction.then_inc(self.sem, 1)
        self.k += 1
        self.engine.wait_ge(self.sem, self.start + self.k)

    def close(self):
        assert self.k == self.per, (self.k, self.per)


def over(ap, shape):
    return ap.to_broadcast(shape)


def program(nc, x, pack, rows, w1, w2, out):
    with ExitStack() as ctx:
        def sb(name, shape, dt=F32, scope=ctx):
            return scope.enter_context(nc.sbuf_tensor(name, shape, dt))

        def sem(name):
            return ctx.enter_context(nc.semaphore(name))

        bank = [ctx.enter_context(nc.psum_tensor(f"bank{i}", [P, 512], F32)) for i in range(8)]

        def tiles(b):
            return bank[b][:, :].rearrange("p (t c) -> p t c", t=TP)

        X = sb("X", [P, TILES, P])
        W = sb("W", [P, PACKED])
        R = sb("R", [P, len(ROWS), P])
        W1 = sb("W1", [P, EXPERTS, FF])
        W2 = sb("W2", [P, EXPERTS, CH, P])
        half = sb("half", [P, TP])
        tick = sb("tick", [P, 1])
        half12 = sb("half12", [P, 12])
        st = sb("st", [P, TP, 6])
        mv = sb("mv", [P, TP, 2])
        ve = sb("ve", [P, TP])
        rs = sb("rs", [P, TP])
        st2 = sb("st2", [P, TP, 6])
        mv2 = sb("mv2", [P, TP, 2])
        ve2 = sb("ve2", [P, TP])
        rs2 = sb("rs2", [P, TP])
        st3 = sb("st3", [P, TP, 6])
        mv3 = sb("mv3", [P, TP, 2])
        ve3 = sb("ve3", [P, TP])
        rs3 = sb("rs3", [P, TP])

        scr_q = nc.dram_tensor("scr_q", (2, SLOTS, P, T), BF16, kind="Internal").ap()
        scr_k = nc.dram_tensor("scr_k", (2, SLOTS, P, T), BF16, kind="Internal").ap()
        scr_m = nc.dram_tensor("scr_m", (2, 2, H1, T), BF16, kind="Internal").ap()
        REST = 1 + 2 * EXPERTS

        def wt(name):
            a, n = PACK[name]
            return W[:, a:a + n]

        def row(name):
            return R[:, ROW[name], :]

        def row4(name):
            return over(R[:, ROW[name]:ROW[name] + 1, :], [P, TP, P])

        with ExitStack() as early:
            FY = [sb(f"FY{i}", [P, TP, P], scope=early) for i in range(2)]
            FYT = [sb(f"FYT{i}", [P, N], scope=early) for i in range(2)]
            XB = [sb(f"XB{i}", [P, TP, P], scope=early) for i in range(2)]
            SEL = sb("SEL", [P, HJ, P], BF16, scope=early)
            rowsel = sb("rowsel", [P, HJ], scope=early)
            I0 = sb("I0", [P, 512], scope=early)
            I1 = sb("I1", [P, 512], scope=early)
            Y0 = [sb(f"Y0_{i}", [P, TP, P], scope=early) for i in range(2)]
            YR0 = sb("YR0", [P, TP, P], scope=early)
            YT0 = sb("YT0", [P, N], scope=early)
            ex = sb("ex", [P, 2, N], scope=early)
            re = sb("re", [P, 2, N], scope=early)
            qf = sb("qf", [P, N], scope=early)
            kT = [sb(f"kT{i}", [P, N], scope=early) for i in range(2)]
            QX = [sb(f"QX{i}", [P, 2, H0, T], scope=early) for i in range(2)]
            bE = sb("bE", [P, TP, HJ], scope=early)
            bR = sb("bR", [P, TP, HJ], scope=early)
            part = [sb(f"part{i}", [P, TP, HJ], BF16, scope=early) for i in range(3)]
            BT = sb("BT", [P, TP, P], scope=early)
            STK = [sb(f"STK{i}", [P, 2, 384], BF16, scope=early) for i in range(2)]
            MG = sb("MG", [P, TP, 40], scope=early)
            mx = sb("mx", [P, TP, H0], scope=early)
            E0 = sb("E0", [P, TP, 40], scope=early)
            E1 = sb("E1", [P, TP, 40], scope=early)
            SD = sb("SD", [P, TP, 32], scope=early)
            RD = sb("RD", [P, TP, 32], scope=early)
            WM = [sb(f"WM{i}", [P, TP, HJ], scope=early) for i in range(2)]
            VG = [sb(f"VG{i}", [P, TP, H0, 32], scope=early) for i in range(2)]
            DD0 = [sb(f"DD0_{i}", [P, 1024], scope=early) for i in range(2)]
            DD1 = [sb(f"DD1_{i}", [P, 512], scope=early) for i in range(2)]
            SS = [sb(f"SS{i}", [P, 768], scope=early) for i in range(2)]
            A0 = [sb(f"A0_{i}", [P, 4, T], scope=early) for i in range(2)]
            A1 = [sb(f"A1_{i}", [P, 4, P], scope=early) for i in range(2)]
            OT0 = [sb(f"OT0_{i}", [P, 4, T], scope=early) for i in range(2)]
            den = sb("den", [P, 2, HJ], scope=early)
            rec = sb("rec", [P, 2, HJ], scope=early)
            rw0 = sb("rw0", [P, 2, HJ], scope=early)
            PR = sb("PR", [P, 2, HJ, D0], scope=early)
            YO = sb("YO", [P, TP, P], scope=early)
            YOT = sb("YOT", [P, N], scope=early)
            HR = sb("HR", [P, TP, P], scope=early)
            HN = sb("HN", [P, TP, P], scope=early)
            HG = sb("HG", [P, TP, P], scope=early)

        late = ctx
        PB = [sb(f"PB{i}", [P, 2, T], scope=late) for i in range(4)]
        OT1 = [sb(f"OT1_{i}", [P, 4, T], scope=late) for i in range(2)]
        QS = [sb(f"QS{i}", [P, 2, H1 // 2, T], BF16, scope=late) for i in range(2)]
        KS = [sb(f"KS{i}", [P, 2, H1 // 2, T], BF16, scope=late) for i in range(2)]
        V1 = [sb(f"V1_{i}", [P, TP, H1, 32], scope=late) for i in range(2)]
        VS = sb("VS", [P, TP, P], scope=late)
        YT1 = sb("YT1", [P, N], scope=late)
        Y1 = [sb(f"Y1_{i}", [P, TP, P], scope=late) for i in range(2)]
        YR1 = [sb(f"YR1_{i}", [P, TP, P], scope=late) for i in range(2)]
        qk32 = [sb(f"qk32_{i}", [P, N], scope=late) for i in range(2)]
        qkr = [sb(f"qkr_{i}", [P, N], scope=late) for i in range(2)]
        PQ = [sb(f"PQ_{i}", [P, 3, N], BF16, scope=late) for i in range(2)]
        NM = sb("NM", [P, TP, H1], scope=late)
        MH = [sb(f"MH{i}", [H1, 2, T], BF16, scope=late) for i in range(2)]
        rec1 = sb("rec1", [P, TP, H1], scope=late)
        AN = sb("AN", [P, TP, P], scope=late)
        ANT = sb("ANT", [P, N], scope=late)
        Z = sb("Z", [P, TP, P], scope=late)
        ZN = sb("ZN", [P, TP, P], scope=late)
        ZG = sb("ZG", [P, TP, P], scope=late)
        with ExitStack() as shared:
            ones = sb("ones", [2, H1 // 2 * T * 2], BF16, scope=shared)
        XS = [sb(f"XS{i}", [P, TP, P]) for i in range(2)]
        XT = sb("XT", [P, N])
        HB = [sb(f"HB{i}", [P, CH, N]) for i in range(2)]
        YB = sb("YB", [P, TP, P])
        AC = sb("AC", [P, TP, P])
        KP = YB
        key = [sb(f"key{i}", [P, TP]) for i in range(3)]
        kint = sb("kint", [P, TP], I32)
        MK = [sb(f"MK{i}", [P, EXPERTS, TP]) for i in range(2)]
        EN = sb("EN", [P, TP, P])
        EG = sb("EG", [P, TP, P])
        YV, YVT, PA, YX = Y1, YT1, OT1[0], (VS, Z)
        kqT = [z[:, :, :].rearrange("p t c -> p (t c)") for z in (ZN, ZG)]
        PAT = (AN[:, :, :].rearrange("p t c -> p (t c)"), ANT[:, :])
        KQV = [sb(f"KQV{i}", [P, TP, 3, P]) for i in range(2)]
        RAW = sb("RAW", [P, TP, 3, P])
        st12 = sb("st12", [P, 12, 6])
        dif12, mean12, var12 = (sb(f"{k}12", [P, 12]) for k in ("dif", "mean", "var"))
        ve12 = sb("ve12", [P, 12])
        rs12 = sb("rs12", [P, 12])
        nmx = sb("nmx", [P, TP])
        esum = sb("esum", [P, TP])
        rsum = sb("rsum", [P, TP])

        x_loaded, w_loaded, rest_loaded, stored = sem("x_loaded"), sem("w_loaded"), sem("rest_loaded"), sem("stored")
        setup_done = sem("setup_done")
        setup_link = sem("setup_link")
        halved = sem("halved")
        consts_done = sem("consts_done")
        x_even, x_odd = sem("x_even"), sem("x_odd")
        x_of = [(x_even, x_odd)[k % 2] for k in range(len(PHASES) + 1)]
        base = [(k + 1) // 2 * PAIRS for k in range(len(PHASES) + 1)]

        class F:
            link = sem("ffn_link")
            var = sem("ffn_var")
            rstd = sem("ffn_rstd")
            norm = sem("ffn_norm")
            turned = sem("ffn_turned")
            copied = sem("ffn_copied")
            mm = sem("ffn_mm")
            xb = sem("ffn_xb")

        class L:
            link_ln = sem("lin_link_ln")
            link_beta = sem("lin_link_beta")
            link_gate = sem("lin_link_gate")
            link_post = sem("lin_link_post")
            link_out = sem("lin_link_out")
            var = sem("lin_var")
            rstd = sem("lin_rstd")
            norm = sem("lin_norm")
            turned = sem("lin_turned")
            copied = sem("lin_copied")
            qk = sem("lin_qk")
            exp4 = sem("lin_exp4")
            mg = sem("lin_mg")
            bt = sem("lin_bt")
            bT = sem("lin_bT")
            vmg = sem("lin_vmg")
            v_used = sem("lin_v_used")
            e0 = sem("lin_e0")
            e1 = sem("lin_e1")
            qf = sem("lin_qf")
            qx = sem("lin_qx")
            stk = sem("lin_stk")
            yr = sem("lin_yr")
            bc = sem("lin_bc")
            bcused = sem("lin_bcused")
            s = sem("lin_s")
            scopied = sem("lin_scopied")
            a0 = sem("lin_a0")
            a1 = sem("lin_a1")
            av = sem("lin_av")
            ocopied = sem("lin_ocopied")
            pt = sem("lin_pt")
            ptused = sem("lin_ptused")
            yo = sem("lin_yo")
            yoT = sem("lin_yoT")
            yoc = sem("lin_yoc")
            wo = sem("lin_wo")
            hr = sem("lin_hr")
            var2 = sem("lin_var2")
            rstd2 = sem("lin_rstd2")
            hn = sem("lin_hn")
            hg = sem("lin_hg")
            xd = sem("lin_xd")

        class A:
            ready = sem("heads_ready")
            vzero = sem("heads_vzero")
            ones = sem("heads_ones")
            link_ln = sem("heads_link_ln")
            link_m = sem("heads_link_m")
            link_n = sem("heads_link_n")
            link_z = sem("heads_link_z")
            var = sem("heads_var")
            rstd = sem("heads_rstd")
            norm = sem("heads_norm")
            turned = sem("heads_turned")
            copied = sem("heads_copied")
            q = sem("heads_q")
            k = sem("heads_k")
            v = sem("heads_v")
            qev = sem("heads_qev")
            kev = sem("heads_kev")
            vev = sem("heads_vev")
            vcopied = sem("heads_vcopied")
            hi = sem("heads_hi")
            r1 = sem("heads_r1")
            mid = sem("heads_mid")
            parts = sem("heads_parts")
            scr = sem("heads_scr")
            qkl0 = sem("heads_qkl0")
            qkl1 = sem("heads_qkl1")
            m0T = sem("heads_m0T")
            m1T = sem("heads_m1T")
            m0ev = sem("heads_m0ev")
            m1ev = sem("heads_m1ev")
            mwr0 = sem("heads_mwr0")
            mwr1 = sem("heads_mwr1")
            ml0 = sem("heads_ml0")
            ml1 = sem("heads_ml1")
            mx = sem("heads_mx")
            red = sem("heads_red")
            s = sem("heads_s")
            e = sem("heads_e")
            pv = sem("heads_pv")
            ocopied = sem("heads_ocopied")
            pt = sem("heads_pt")
            norm1 = sem("heads_norm1")
            anT = sem("heads_anT")
            anc = sem("heads_anc")
            wo = sem("heads_wo")
            yr = sem("heads_yr")
            z = sem("heads_z")
            var2 = sem("heads_var2")
            rstd2 = sem("heads_rstd2")
            zn = sem("heads_zn")
            zg = sem("heads_zg")
            x1 = sem("heads_x1")

        class E:
            link_key = sem("exp_link_key")
            link_ln = sem("exp_link_ln")
            turned = sem("exp_turned")
            xt = sem("exp_xt")
            h = sem("exp_h")
            relu = sem("exp_relu")
            y = sem("exp_y")
            yused = sem("exp_yused")
            mask = sem("exp_mask")
            acc = sem("exp_acc")
            var = sem("exp_var")
            rstd = sem("exp_rstd")
            norm = sem("exp_norm")
            g = sem("exp_g")
            b = sem("exp_b")

        class V:
            link_ln = sem("attn_link_ln")
            link_b = sem("attn_link_b")
            var = sem("attn_var")
            rstd = sem("attn_rstd")
            norm = sem("attn_norm")
            turned = sem("attn_turned")
            copied = sem("attn_copied")
            proj = sem("attn_proj")
            biased = sem("attn_biased")
            var12 = sem("attn_var12")
            rstd12 = sem("attn_rstd12")
            norm12 = sem("attn_norm12")
            g = sem("attn_g")
            kqv = sem("attn_kqv")
            kqT = sem("attn_kqT")
            kqc = sem("attn_kqc")
            s = sem("attn_s")
            nmx = sem("attn_nmx")
            e = sem("attn_e")
            pT = sem("attn_pT")
            pc = sem("attn_pc")
            av = sem("attn_av")
            yx = sem("attn_yx")
            sumr = sem("attn_sumr")

        schedule, runs, xp = [], {}, 1
        for name in PHASES:
            schedule.append((name, runs.get(name, 0), xp))
            runs[name] = runs.get(name, 0) + 1
            xp += 1

        def token_stats(dve, src, st_, mv_, ve_, link, var_sem):
            for t in range(TP):
                last = dve.bn_stats(st_[:, t, :], src(t))
            link(last)
            dve.memset(tick[:, :], 0.0)
            for t in range(TP):
                last = dve.bn_aggr(mv_[:, t, :], st_[:, t, :])
            link(last)
            dve.tensor_scalar(ve_[:, :], mv_[:, :, 1], LN_EPS, None, ALU.add).then_inc(var_sem, 1)

        def token_norm(dve, src, dst, mv_, rs_):
            for t in range(TP):
                last = dve.tensor_scalar(dst(t), src(t), mv_[:, t, 0:1], rs_[:, t:t + 1], ALU.subtract, ALU.mult)
            return last

        LEADS = {"linear": {(PAIRS, i): i - 2 for i in range(PAIRS - 1)},
                 "experts": {(PAIRS + 2, 26): -2, (PAIRS + 3, 8): -1}}

        def nothing(n, i):
            pass

        def linear_steps(engine, step, between):
            step(-1, 1, True, False, False)
            step(0, 0, True, True, False)
            with engine.Fori(0, PAIRS // 2 - 1) as it:
                step(it * 2 + 1, 1, True, True, True)
                step(it * 2 + 2, 0, True, True, True)
            step(PAIRS - 1, 1, False, True, True)
            step(PAIRS, 0, False, False, True, between)

        def experts_steps(engine, step, between, start=-1):
            def stages(n):
                return [0 <= n - back < PAIRS for back in (-1, 0, 1, 2, 3, 4)]
            first, last = 4, PAIRS - 2
            for n in range(start, first):
                step(n, n % 2, *stages(n))
            with engine.Fori(0, (last - first) // 2) as it:
                step(it * 2 + first, 0, *stages(first))
                step(it * 2 + (first + 1), 1, *stages(first))
            for n in range(last, PAIRS + 4):
                step(n, n % 2, *stages(n), between if n > last + 3 else nothing)

        def short_step(step, n):
            step(n, n % 2, n + 2 < PAIRS, 0 <= n + 1 < PAIRS, 0 <= n)

        def short_steps(engine, step, first, start_next):
            for n in range(first, 0):
                short_step(step, n)
            if first <= 0:
                with engine.Fori(0, PAIRS // 2 - 1) as it:
                    step(it * 2, 0, True, True, True)
                    step(it * 2 + 1, 1, True, True, True)
            for n in range(first if first > 0 else PAIRS - 2, PAIRS):
                if n == PAIRS - 1:
                    start_next()
                short_step(step, n)

        def run_phases(engine, phases):
            step, first = phases[schedule[0][0]](*schedule[0][1:]), -2
            for (name, run, xp), after in zip(schedule, schedule[1:] + [None]):
                follower = phases[after[0]](*after[1:]) if after else None
                lead = LEADS.get(name, {}) if after else {}

                def between(n, i):
                    if (n, i) in lead:
                        short_step(follower, lead[n, i])

                def start_next():
                    if after and after[0] == "experts":
                        follower(-1, 1, True, False, False, False, False, False)

                if name == "linear":
                    linear_steps(engine, step, between)
                elif name == "experts":
                    experts_steps(engine, step, between, 0)
                else:
                    short_steps(engine, step, first, start_next)
                step, first = follower, max(lead.values()) + 1 if lead else -2

        block = ctx.enter_context(nc.Block())

        @block.sync
        def _(sp):
            sp.dma_start(W[:, :], pack).then_inc(w_loaded, 16)
            sp.dma_start(R[:, 0:2, :].rearrange("p r c -> p (r c)"),
                         rows[0:2 * P].partition_broadcast(P)).then_inc(w_loaded, 16)
            for n in range(PAIRS):
                sp.dma_start(X[:, TP * n:TP * n + TP, :],
                             x[N * n:N * n + N, :].rearrange("(t p) c -> p t c", p=P)).then_inc(x_loaded, 16)
            sp.dma_start(R[:, 2:, :].rearrange("p r c -> p (r c)"),
                         rows[2 * P:].partition_broadcast(P)).then_inc(rest_loaded, 16)
            for e in range(EXPERTS):
                sp.dma_start(W1[:, e, :], w1[e]).then_inc(rest_loaded, 16)
                sp.dma_start(W2[:, e, :, :], w2[e].rearrange("(k p) c -> p k c", p=P)).then_inc(rest_loaded, 16)

            def experts(run, xp):
                g8 = 8 * run

                def move_max(n, b, par):
                    written, loaded = (A.mwr0, A.mwr1)[b], (A.ml0, A.ml1)[b]
                    sp.wait_ge((A.m0ev, A.m1ev)[b], n + (g8 + 1))
                    sp.dma_start(scr_m[b].rearrange("s h t -> h s t"), MH[b][:, :, :]).then_inc(written, 16)
                    sp.wait_ge(written, n * 16 + (16 * g8 + 16))
                    for a in range(2):
                        r = 64 * a + SLOTS * D1
                        sp.dma_start(QS[par][r:r + 2, b, :, :],
                                     scr_m[b].rearrange("s (g a) t -> a s g t", a=2)[a]).then_inc(loaded, 16)

                def load_parts(n, b, par):
                    for a in range(2):
                        for scr, dst in ((scr_q, QS), (scr_k, KS)):
                            sp.dma_start(dst[par][64 * a:64 * a + SLOTS * D1, b, :, :].rearrange("p g t -> p (g t)"),
                                         scr[b, :, 64 * a:64 * a + 64, :].rearrange("s (d g) t -> s d (g t)", d=D1)
                                         ).then_inc((A.qkl0, A.qkl1)[b], 16)

                def step(n, par, pre, mx, att, post, exp, fin, between=nothing):
                    other = 1 - par
                    if att:
                        move_max(n - 1, 1, other)
                    if pre:
                        sp.wait_ge(A.parts, n * 2 + (2 * g8 + 4))
                        if later(n * 64 + 64 * (g8 + 1)):
                            sp.wait_ge(A.qkl0, n * 64 + 64 * (g8 + 1))
                        if later(n * 64 + 64 * (g8 + 1)):
                            sp.wait_ge(A.qkl1, n * 64 + 64 * (g8 + 1))
                        for b in range(2):
                            h = slice(T * b, T * b + T)
                            for scr, pt, at, src in ((scr_q, PQ[0], 0, (0, 3)), (scr_q, PQ[0], 3, (0, 2)),
                                                     (scr_q, PQ[0], 5, (0, 1)), (scr_k, PQ[1], 0, (0, 0)),
                                                     (scr_k, PQ[1], 3, (1, 1)), (scr_k, PQ[1], 5, (2, 3))):
                                k = SLOTS - at if at == 5 else (3, 2)[at == 3]
                                if src[1] > src[0]:
                                    s = pt[:, src[0]:src[1], h]
                                else:
                                    s = over(pt[:, src[0]:src[0] + 1, h], [P, k, T])
                                sp.dma_start(scr[b, at:at + k].rearrange("s r t -> r s t"), s).then_inc(A.scr, 16)
                        sp.wait_ge(A.scr, n * 192 + 192 * (g8 + 2))
                        if att:
                            sp.wait_ge(A.s, n * 32 + (32 * g8 - 16))
                        load_parts(n + 1, 0, other)
                    if mx:
                        move_max(n, 0, par)
                    if pre:
                        if att:
                            sp.wait_ge(A.s, n * 32 + 32 * g8)
                        load_parts(n + 1, 1, other)

                if run == 0:
                    sp.wait_ge(A.ones, 1)
                    for b in range(2):
                        for a in range(2):
                            r = 64 * a + SLOTS * D1
                            sp.dma_start(KS[b][r:r + 2, :, :, :].rearrange("p b g t -> p (b g t)"),
                                         ones[:, :]).then_inc(A.ready, 16)
                experts_steps(sp, step, nothing)

            for name, run, xp in schedule:
                if name == "experts":
                    experts(run, xp)
            with sp.Fori(0, PAIRS) as n:
                sp.wait_ge(x_of[-1], n + (base[-1] + 1))
                sp.dma_start(out[bass.ds(n * N, N), :].rearrange("(t p) c -> p t c", p=P),
                             X[:, bass.ds(n * TP, TP), :]).then_inc(stored, 16)
            sp.wait_ge(stored, 16 * PAIRS)

        @block.gpsimd
        def _(pool):
            def power(var_sem, rstd_sem, count, ve_, rs_):
                pool.wait_ge(var_sem, count)
                pool.tensor_tensor(rs_[:, :], ve_[:, :], half[:, 0:ve_.shape[1]], ALU.pow).then_inc(rstd_sem, 1)

            def ffn(run, xp):
                def step(n, par, pre, mid, main):
                    if pre:
                        power(F.var, F.rstd, n + (8 * run + 3), ve, rs)
                    if mid:
                        pool.wait_ge(x_of[xp - 1], n + (base[xp - 1] + 2))
                        pool.wait_ge(x_of[xp], n + base[xp])
                        pool.tensor_tensor(XB[1 - par][:, :, :], X[:, bass.ds((n + 1) * TP, TP), :], row4("qbias"),
                                           ALU.add).then_inc(F.xb, 1)
                return step

            def linear(run, xp):
                def step(n, par, pre, main, post, between=nothing):
                    if isinstance(n, int) and n == -1:
                        pool.wait_ge(rest_loaded, 16 * REST)
                    if pre:
                        power(L.var, L.rstd, n + 2, ve, rs)
                    for i in range(8):
                        if post and i == 6:
                            power(L.var2, L.rstd2, n, ve2, rs2)
                        if post and i == 7:
                            pool.wait_ge(L.hn, n)
                            pool.tensor_tensor(HG[:, :, :], HN[:, :, :], row4("lng"), ALU.mult).then_inc(L.hg, 1)
                            pool.wait_ge(L.hg, n)
                            pool.tensor_tensor(HG[:, :, :], HG[:, :, :], row4("lnb"), ALU.add).then_inc(L.xd, 1)
                        if main:
                            j = n * 8 + i
                            pool.wait_ge(L.bcused, j * 3 + 2)
                            pool.wait_ge(L.scopied, j * 2 + 1)
                            if later(j - 1):
                                pool.wait_ge(L.av, j - 1)
                            s = SS[i % 2][:, 256:512].rearrange("p (o t) -> p o t", o=1)
                            pool.tensor_tensor(A0[i % 2][:, 2:4, :],
                                               DD0[i % 2][:, 512:1024].rearrange("p (j t) -> p j t", j=2),
                                               over(s, [P, 2, T]), ALU.mult).then_inc(L.a1, 1)
                            pool.wait_ge(L.bcused, j * 3 + 3)
                            pool.wait_ge(L.scopied, j * 2 + 2)
                            s = SS[i % 2][:, 512:768].rearrange("p (h o t) -> p h o t", h=2, o=1)
                            pool.tensor_tensor(A1[i % 2][:, :, :].rearrange("p (h j) t -> p h j t", h=2),
                                               DD1[i % 2][:, :].rearrange("p (h j t) -> p h j t", h=2, j=2),
                                               over(s, [P, 2, 2, P]), ALU.mult).then_inc(L.a1, 1)
                        between(n, i)
                    if main:
                        pool.wait_ge(L.norm, n + 1)
                        if later(n):
                            pool.wait_ge(L.hr, n)
                        pool.tensor_tensor(YR0[:, :, :], Y0[par][:, :, :], row4("bout"), ALU.add).then_inc(L.yr, 1)
                return step

            def experts(run, xp):
                g8 = 8 * run

                def step(n, par, pre, mx, att, post, exp, fin, between=nothing):
                    c = n + g8
                    between(n, 4)
                    between(n, 8)
                    if pre:
                        power(A.var, A.rstd, c + 2, ve, rs)
                    if mx:
                        pool.wait_ge(A.vev, c + 1)
                        if later(c * 32 - 32):
                            pool.wait_ge(A.pv, c * 32 - 32)
                        bv = over(row("bv").rearrange("p (o h d) -> p o h d", o=1, h=H1), [P, TP, H1, D1])
                        pool.tensor_tensor(V1[par][:, :, :, 0:D1],
                                           VS[:, :, :].rearrange("p t (h d) -> p t h d", h=H1), bv,
                                           ALU.add).then_inc(A.vcopied, 1)
                    if pre:
                        for h in range(2):
                            pool.wait_ge(A.hi, c * 2 + (3 + h))
                            pool.tensor_tensor(qkr[h][:, :], qk32[h][:, :], PQ[h][:, 0, :],
                                               ALU.subtract).then_inc(A.r1, 1)
                    if fin:
                        power(E.var, E.rstd, c - 3, ve3, rs3)
                    if pre:
                        for h in range(2):
                            pool.wait_ge(A.mid, c * 2 + (3 + h))
                            pool.tensor_tensor(PQ[h][:, 2, :], qkr[h][:, :], PQ[h][:, 1, :],
                                               ALU.subtract).then_inc(A.parts, 1)
                    if post:
                        power(A.var2, A.rstd2, c - 1, ve2, rs2)
                    if fin:
                        pool.wait_ge(E.norm, c - 3)
                        pool.tensor_tensor(EG[:, :, :], EN[:, :, :], row4("ln2g"), ALU.mult).then_inc(E.g, 1)
                        pool.wait_ge(E.g, c - 3)
                        pool.tensor_tensor(EG[:, :, :], EG[:, :, :], row4("ln2b"), ALU.add).then_inc(E.b, 1)
                    between(n, 26)
                    if post:
                        pool.wait_ge(A.zn, c - 1)
                        pool.tensor_tensor(ZG[:, :, :], ZN[:, :, :], row4("ln1g"), ALU.mult).then_inc(A.zg, 1)
                        pool.wait_ge(A.zg, c - 1)
                        if later(c * 4 - 15):
                            pool.wait_ge(E.acc, c * 4 - 15)
                        pool.tensor_tensor(XS[par][:, :, :], ZG[:, :, :], row4("ln1b"), ALU.add).then_inc(A.x1, 1)
                    if mx:
                        pool.wait_ge(A.norm, c + 1)
                        if later(c - 1):
                            pool.wait_ge(A.z, c - 1)
                        pool.tensor_tensor(YR1[par][:, :, :], Y1[par][:, :, :], row4("bo"), ALU.add).then_inc(A.yr, 1)

                if run == 0:
                    pool.wait_ge(x_of[xp - 2], base[xp - 2] + PAIRS)
                    pool.wait_ge(halved, 1)
                    pool.memset(ones[:, :], 1.0).then_inc(A.ones, 1)
                    for b in range(2):
                        pool.memset(V1[b][:, :, :, :], 0.0).then_inc(A.vzero, 1)
                    pool.wait_ge(A.vzero, 2)
                    for b in range(2):
                        pool.memset(V1[b][:, :, :, D1:D1 + 1], 1.0).then_inc(A.vzero, 1)
                    pool.wait_ge(A.vzero, 4)
                return step

            def attn(run, xp):
                def rows3(name):
                    k = ROW[name]
                    return over(R[:, k:k + 3, :].rearrange("p (o k) c -> p o (k c)", o=1), [P, TP, 3 * P])

                def step(n, par, pre, mid, main):
                    other = 1 - par
                    if pre:
                        power(V.var, V.rstd, n + 3, ve, rs)
                    if mid:
                        pool.wait_ge(V.norm12, n + 2)
                        w = KQV[other][:, :, :, :].rearrange("p t k c -> p t (k c)")
                        pool.tensor_tensor(w, w, rows3("agk"), ALU.mult).then_inc(V.g, 1)
                        pool.wait_ge(V.g, n + 2)
                        pool.tensor_tensor(w, w, rows3("aek"), ALU.add).then_inc(V.kqv, 1)
                        pool.wait_ge(V.norm, n + 2)
                        pool.wait_ge(x_of[xp], n + base[xp])
                        pool.tensor_tensor(YX[other][:, :, :], YV[other][:, :, :], X[:, bass.ds((n + 1) * TP, TP), :],
                                           ALU.add).then_inc(V.yx, 1)
                    if pre:
                        pool.wait_ge(V.var12, n + 3)
                        pool.tensor_tensor(rs12[:, :], ve12[:, :], half12[:, :], ALU.pow).then_inc(V.rstd12, 1)
                return step

            pool.memset(half12[:, :], -0.5).then_inc(consts_done, 1)
            pool.memset(half[:, :], -0.5).then_inc(consts_done, 1)
            for b in range(2):
                pool.memset(VG[b][:, :, :, :], 0.0).then_inc(consts_done, 1)
                pool.memset(STK[b][:, :, :], 0.0).then_inc(consts_done, 1)
            pool.memset(BT[:, :, :], 0.0).then_inc(consts_done, 1)
            pool.wait_ge(consts_done, 7)
            pool.wait_ge(w_loaded, 32)
            pool.wait_ge(setup_done, 1)
            run_phases(pool, {"ffn": ffn, "linear": linear, "experts": experts, "attn": attn})

        @block.scalar
        def _(act):
            def ffn(run, xp):
                def step(n, par, pre, mid, main):
                    if mid:
                        act.wait_ge(F.turned, n + (8 * run + 2))
                        act.activation(FYT[1 - par][:, :], bank[1][:, :], ACT.Copy).then_inc(F.copied, 1)
                return step

            def linear(run, xp):
                hmask = wt("hmask")

                def step(n, par, pre, main, post, between=nothing):
                    other = 1 - par
                    for i in range(8):
                        if pre and i == 4:
                            act.wait_ge(L.e0, n + 2)
                            act.activation(E1[:, :, :], E0[:, :, :], ACT.Exp).then_inc(L.e1, 1)
                        if (main, pre)[i == 7]:
                            if later(n * 8 + i):
                                act.wait_ge(L.a0, n * 8 + i)
                            if later(n * 16 + 2 * i):
                                act.wait_ge(L.a1, n * 16 + 2 * i)
                            ss = SS[(i + 1) % 2]
                            act.wait_ge(L.s, n * 16 + (2 * i + 3))
                            act.activation(ss[:, 0:512], bank[2][:, :], ACT.Copy).then_inc(L.scopied, 1)
                            act.wait_ge(L.s, n * 16 + (2 * i + 4))
                            act.activation(ss[:, 512:768], bank[3][:, 0:T], ACT.Copy).then_inc(L.scopied, 1)
                        if (i == 0 and post) or (i == 4 and main):
                            done = n * 2 + i // 4 - 1
                            act.wait_ge(L.av, done * 4 + 4)
                            if i == 4:
                                if later(done * 2 - 2):
                                    act.wait_ge(L.pt, done * 2 - 2)
                            for h in range(2):
                                act.activation(OT0[1 - i // 4][:, 2 * h:2 * h + 2, :],
                                               bank[4 + h][:, :].rearrange("p (r t) -> p r t", r=2),
                                               ACT.Copy).then_inc(L.ocopied, 1)
                        if pre and i == 2:
                            act.wait_ge(L.turned, n + 2)
                            if later(n + 1):
                                act.wait_ge(L.vmg, n + 1)
                            act.activation(YT0[:, :], bank[6][:, :], ACT.Copy).then_inc(L.copied, 1)
                        if post and i == 2:
                            act.wait_ge(L.yoT, n)
                            act.activation(YOT[:, :], bank[7][:, :], ACT.Copy).then_inc(L.yoc, 1)
                        if pre and i in (3, 4):
                            h, b = ((0, 6), (1, 7))[i - 3]
                            if later(n * 2 + 2):
                                act.wait_ge(L.qf, n * 2 + 2)
                            act.wait_ge(L.qk, n * 2 + (3 + h))
                            act.activation(ex[:, h, :], bank[b][:, :], ACT.Exp).then_inc(L.exp4, 1)
                            act.activation(re[:, h, :], bank[b][:, :], ACT.Relu).then_inc(L.exp4, 1)
                        if pre and i in (5, 6):
                            act.wait_ge(L.qf, n * 2 + 3)
                            for h in range(4 * (i - 5), 4 * (i - 5) + 4):
                                act.activation(QX[other][:, :, h, :], qf[:, :].rearrange("p (b t) -> p b t", b=2),
                                               ACT.Copy, scale=hmask[:, h:h + 1]).then_inc(L.qx, 1)
                        if pre and i == 6:
                            act.wait_ge(L.bT, n + 2)
                            bt = bank[7][:, :].rearrange("p (b t) -> p b t", b=2)
                            act.activation(STK[other][:, :, 1:T], bt[:, :, 1:T], ACT.Copy).then_inc(L.stk, 1)
                            act.activation(STK[other][:, :, T + 1:T + P], bt[:, :, P + 1:T],
                                           ACT.Copy).then_inc(L.stk, 1)
                        between(n, i)
                return step

            def experts(run, xp):
                g8 = 8 * run

                def relu(p, e, k):
                    c = p + g8
                    act.wait_ge(E.h, c * 16 + (4 * e + k + 1))
                    if later(c * 4 + (e - 1)):
                        act.wait_ge(E.y, c * 4 + (e - 1))
                    b0 = PACK["b1"][0] + CH * e + k
                    act.activation(HB[e % 2][:, k, :], bank[6][:, :], ACT.Relu,
                                   bias=W[:, b0:b0 + 1]).then_inc(E.relu, 1)

                def step(n, par, pre, mx, att, post, exp, fin, between=nothing):
                    c = n + g8

                    def copy_sums(i):
                        h, back = {9: (0, 2), 17: (1, 2), 25: (2, 2), 1: (3, 3)}[i]
                        if i != 1:
                            if later((c - 1) * 4 + (2 * (h // 2) - 2)):
                                act.wait_ge(A.pt, (c - 1) * 4 + (2 * (h // 2) - 2))
                        act.wait_ge(A.pv, c * 32 + (8 * h + 8 - (32, 64)[i == 1]))
                        r = 2 * (h % 2)
                        act.activation(OT1[h // 2][:, r:r + 2, :], bank[5][:, :].rearrange("p (r t) -> p r t", r=2),
                                       ACT.Copy).then_inc(A.ocopied, 1)

                    for i in range(SLOTS_H):
                        if pre and i == 7:
                            act.wait_ge(A.turned, c + 2)
                            if later(c + 1):
                                act.wait_ge(A.v, c + 1)
                            act.activation(YT1[:, :], bank[0][:, :], ACT.Copy).then_inc(A.copied, 1)
                        if att:
                            q = c * 32 + (i - 32)
                            act.wait_ge(A.s, q + 1)
                            if later(q - 3):
                                act.wait_ge(A.pv, q - 3)
                            act.activation(PB[i % 4][:, :, :], bank[1 + i % 2][:, :].rearrange("p (k t) -> p k t", k=2),
                                           ACT.Exp).then_inc(A.e, 1)
                        if pre and i == 11:
                            act.wait_ge(A.k, c + 2)
                            if later(c * 2 + 2):
                                act.wait_ge(A.parts, c * 2 + 2)
                            act.activation(qk32[1][:, :], bank[0][:, :], ACT.Identity,
                                           bias=wt("bk")[:, 0:1]).then_inc(A.kev, 1)
                        if post and i == 12:
                            act.wait_ge(A.anT, c - 1)
                            act.activation(ANT[:, :], bank[0][:, :], ACT.Copy).then_inc(A.anc, 1)
                        if post and i == 29:
                            act.wait_ge(E.turned, c - 1)
                            if later((c - 2) * 16):
                                act.wait_ge(E.h, (c - 2) * 16)
                            act.activation(XT[:, :], bank[0][:, :], ACT.Copy).then_inc(E.xt, 1)
                        lag, kind, e, k = UNITS[i]
                        if kind == "W1" and (post, exp, fin)[lag - 2]:
                            relu(n - lag, e, k)
                        if (i == 1 and post) or (i in (9, 17, 25) and att):
                            copy_sums(i)
                        if pre and i == 16:
                            act.wait_ge(A.v, c + 2)
                            if later(c + 1):
                                act.wait_ge(A.vcopied, c + 1)
                            act.activation(VS[:, :, :], tiles(0), ACT.Copy).then_inc(A.vev, 1)
                        between(n, i)
                return step

            def attn(run, xp):
                def step(n, par, pre, mid, main):
                    if pre:
                        act.wait_ge(V.turned, n + 3)
                        if later(n * 4 + 8):
                            act.wait_ge(V.proj, n * 4 + 8)
                        act.activation(YVT[:, :], bank[0][:, :], ACT.Copy).then_inc(V.copied, 1)
                    if main:
                        for t in range(TP):
                            act.wait_ge(V.nmx, n * 2 + (1 + t // 2))
                            act.activation(PA[:, t, :], bank[5 + t // 2][:, (t % 2) * T:(t % 2) * T + T], ACT.Exp,
                                           bias=nmx[:, t:t + 1], accum_out=esum[:, t:t + 1]).then_inc(V.e, 1)
                        for u in range(2):
                            act.wait_ge(V.pT, n * 2 + (1 + u))
                            act.activation(PAT[u][:, :], bank[3 + u][:, :], ACT.Copy).then_inc(V.pc, 1)
                    if mid:
                        for h in range(2):
                            act.wait_ge(V.kqT, n * 2 + (3 + h))
                            if later(n * 2 + 2):
                                act.wait_ge(V.s, n * 2 + 2)
                            act.activation(kqT[h][:, :], bank[3 + h][:, :], ACT.Copy).then_inc(V.kqc, 1)
                return step

            act.wait_ge(w_loaded, 32)
            act.wait_ge(setup_done, 1)
            run_phases(act, {"ffn": ffn, "linear": linear, "experts": experts, "attn": attn})

        @block.tensor
        def _(pe):
            ident = wt("ident")

            def ffn(run, xp):
                def step(n, par, pre, mid, main):
                    if main:
                        pe.wait_ge(F.copied, n + (8 * run + 1))
                        pe.wait_ge(x_of[xp], n + (base[xp] - 1))
                        for t in range(TP):
                            last = pe.matmul(bank[2 + par][:, t * P:(t + 1) * P], FYT[par][:, t * P:(t + 1) * P],
                                             wt("cbt"), start=True, stop=True)
                        last.then_inc(F.mm, 1)
                    if mid:
                        pe.wait_ge(F.norm, n + (8 * run + 2))
                        if later(n + (8 * run + 1)):
                            pe.wait_ge(F.copied, n + (8 * run + 1))
                        for t in range(TP):
                            last = pe.transpose(bank[1][:, t * P:(t + 1) * P], FY[1 - par][:, t, :], ident)
                        last.then_inc(F.turned, 1)
                return step

            def linear(run, xp):
                vm0 = PACK["vmg"][0]

                def sums(j, seq, par, s):
                    b = s // 4
                    s %= 4
                    pe.wait_ge(L.a0, j + 1)
                    pe.wait_ge(L.a1, j * 2 + 2)
                    if s % 2 == 0:
                        if later(seq * 2 + (s // 2 - 1)):
                            pe.wait_ge(L.ocopied, seq * 2 + (s // 2 - 1))
                    for c in range(4):
                        o = bank[4 + s // 2][32 * c:32 * c + 32, (s % 2) * T:(s % 2) * T + T]
                        v = VG[par]
                        pe.matmul(o, v[:, 2 * b, 2 * s + c // 2, :], A0[s % 2][:, c, :], start=True, stop=False)
                        last = pe.matmul(o[:, P:T], v[:, 2 * b + 1, 2 * s + c // 2, :], A1[s % 2][:, c, :],
                                         start=False, stop=True)
                    last.then_inc(L.av, 1)

                def decays(n, i, par, c):
                    b, s = i // 4, i % 4
                    if later(n * 24 + (3 * i + c - 1)):
                        pe.wait_ge(L.bcused, n * 24 + (3 * i + c - 1))
                    for k in range(2 if c < 2 else 4):
                        hj = 4 * s + 2 * c + k if c < 2 else 4 * s + k
                        o, w = (k * T, T) if c < 2 else (k * P, P)
                        last = pe.matmul(bank[(3 * i + c) % 2][:, o:o + w], SEL[:, hj, :],
                                         STK[par][:, b, 0:T] if c < 2 else STK[par][:, b, T:T + P],
                                         start=True, stop=True)
                    last.then_inc(L.bc, 1)

                def scores(n, i, par, u):
                    b, s = i // 4, i % 4
                    if later(n * 16 + (2 * i + u - 1)):
                        pe.wait_ge(L.scopied, n * 16 + (2 * i + u - 1))
                    q = QX[par][:, b, 2 * s:2 * s + 2, :]
                    k = b * T + u * P
                    pe.matmul(bank[2 + u][:, 0:(T if u else 2 * T)], kT[par][:, k:k + P], q[:, :, P:T] if u else q,
                              start=True, stop=True).then_inc(L.s, 1)

                def turn_sums(n, main, b):
                    for t in (2 * b, 2 * b + 1):
                        pe.wait_ge(L.ocopied, n * 4 + (2 * b - 2))
                        if t >= 2:
                            pe.wait_ge(L.ptused, n * 4 + (t - 5))
                        elif main:
                            pe.wait_ge(L.v_used, n + 1)
                            pe.wait_ge(L.stk, n * 2 + 2)
                        else:
                            pe.wait_ge(L.hr, n - 1)
                        for r in range(4):
                            last = pe.transpose(bank[6 + t % 2][:, r * P:(r + 1) * P],
                                                OT0[b][:, r, (t % 2) * P:(t % 2) * P + P], ident)
                        last.then_inc(L.pt, 1)

                def step(n, par, pre, main, post, between=nothing):
                    other = 1 - par
                    for i in range(8):
                        j = n * 8 + i
                        after = (n, i + 1, par) if i < 7 else (n + 1, 0, other)
                        after = after if (pre if i == 7 else main) else None
                        if post and i == 0:
                            turn_sums(n, main, 0)
                        if main:
                            decays(n, i, par, 2)
                        if after:
                            if i == 7:
                                pe.wait_ge(L.qx, n * 8 + 16)
                                pe.wait_ge(L.stk, n * 2 + 4)
                                pe.wait_ge(L.qf, n * 2 + 4)
                            scores(*after, 0)
                            decays(*after, 0)
                            scores(*after, 1)
                        if (i == 0 and post) or (i > 0 and main):
                            if i == 1:
                                pe.wait_ge(L.v_used, n + 1)
                            sums(j - 1, n * 2 + ((i - 1) // 4), par if i else other, (i - 1) % 8)
                        if after:
                            decays(*after, 1)
                        if post and i == 1:
                            turn_sums(n, main, 1)
                        if pre and i == 2:
                            pe.wait_ge(L.norm, n + 2)
                            if later(n + 1):
                                pe.wait_ge(L.v_used, n + 1)
                            if later(n * 4 - 1):
                                pe.wait_ge(L.ptused, n * 4 - 1)
                            for t in range(TP):
                                last = pe.transpose(bank[6][:, t * P:(t + 1) * P], Y0[other][:, t, :], ident)
                            last.then_inc(L.turned, 1)
                        if post and i == 2:
                            pe.wait_ge(L.yo, n * 2)
                            for t in range(TP):
                                last = pe.transpose(bank[7][:, t * P:(t + 1) * P], YO[:, t, :], ident)
                            last.then_inc(L.yoT, 1)
                        if pre and i == 3:
                            pe.wait_ge(L.copied, n + 2)
                            if later(n):
                                pe.wait_ge(L.yoc, n)
                            if later(n * 4):
                                pe.wait_ge(L.ptused, n * 4)
                            for t in range(TP):
                                last = pe.matmul(bank[7][:, 40 * t:40 * t + 40], YT0[:, t * P:(t + 1) * P],
                                                 W[:, vm0 + P:vm0 + 168], start=True, stop=True)
                            last.then_inc(L.mg, 1)
                            pe.matmul(bank[6][:, :], wt("q0"), YT0[:, :], start=True, stop=True).then_inc(L.qk, 1)
                        if pre and i == 4:
                            pe.wait_ge(L.e0, n + 2)
                            pe.matmul(bank[7][:, :], wt("k0"), YT0[:, :], start=True, stop=True).then_inc(L.qk, 1)
                        if post and i == 4:
                            if pre:
                                pe.wait_ge(L.exp4, n * 4 + 6)
                            pe.wait_ge(L.yoc, n)
                            for t in range(TP):
                                last = pe.matmul(bank[6][:, t * P:(t + 1) * P], YOT[:, t * P:(t + 1) * P],
                                                 wt("out0"), start=True, stop=True)
                            last.then_inc(L.wo, 1)
                        if pre and i == 6:
                            pe.wait_ge(L.exp4, n * 4 + 8)
                            if later(n):
                                pe.wait_ge(L.hr, n)
                            pe.wait_ge(L.e0, n + 2)
                            pe.wait_ge(L.bt, n + 2)
                            for t in range(TP):
                                last = pe.transpose(bank[7][:, t * P:(t + 1) * P], BT[:, t, :], ident)
                            last.then_inc(L.bT, 1)
                            for t in range(TP):
                                last = pe.matmul(bank[6][:, t * P:(t + 1) * P], YT0[:, t * P:(t + 1) * P],
                                                 W[:, vm0:vm0 + P], start=True, stop=True)
                            last.then_inc(L.vmg, 1)
                        between(n, i)

                return step

            def experts(run, xp):
                g8 = 8 * run

                def unit(p, kind, e, k):
                    c = p + g8
                    if kind == "W1":
                        if (e, k) == (0, 0):
                            pe.wait_ge(E.xt, c + 1)
                        if later(c * 16 + (4 * e + k)):
                            pe.wait_ge(E.relu, c * 16 + (4 * e + k))
                        pe.matmul(bank[6][:, :], W1[:, e, k * P:(k + 1) * P], XT[:, :], start=True,
                                  stop=True).then_inc(E.h, 1)
                        return
                    if k == 0:
                        pe.wait_ge(E.relu, c * 16 + (4 * e + 4))
                        if later(c * 4 + e):
                            pe.wait_ge(E.yused, c * 4 + e)
                    for q in range(CH):
                        last = pe.matmul(bank[7][:, k * P:(k + 1) * P], HB[e % 2][:, q, k * P:(k + 1) * P],
                                         W2[:, e, q, :], start=(q == 0), stop=(q == CH - 1))
                    if k == TP - 1:
                        last.then_inc(E.y, 1)

                def weigh(q, par, seq, b, s):
                    pe.wait_ge(A.e, q + 1)
                    if s % 8 == 0:
                        if later(seq * 2 + s // 8):
                            pe.wait_ge(A.ocopied, seq * 2 + s // 8)
                    o = bank[5][32 * (s % 4):32 * (s % 4) + 32, (s // 4 % 2) * T:(s // 4 % 2) * T + T]
                    for kt in range(2):
                        last = pe.matmul(o, V1[par][:, 2 * b + kt, s, :], PB[s % 4][:, kt, :],
                                         start=(kt == 0), stop=(kt == 1))
                    last.then_inc(A.pv, 1)

                def turn_sums(c, t):
                    pe.wait_ge(A.ocopied, c * 4 + (2 * (t // 2) - 6))
                    for r in range(4):
                        last = pe.transpose(bank[0][:, r * P:(r + 1) * P],
                                            OT1[t // 2][:, r, (t % 2) * P:(t % 2) * P + P], ident)
                    last.then_inc(A.pt, 1)

                def turn(src, done):
                    for t in range(TP):
                        last = pe.transpose(bank[0][:, t * P:(t + 1) * P], src[:, t, :], ident)
                    last.then_inc(done, 1)

                def project(src, weight, done):
                    for t in range(TP):
                        last = pe.matmul(bank[0][:, t * P:(t + 1) * P], src[:, t * P:(t + 1) * P], weight,
                                         start=True, stop=True)
                    last.then_inc(done, 1)

                def step(n, par, pre, mx, att, post, exp, fin, between=nothing):
                    c = n + g8
                    other = 1 - par

                    def upto(lag):
                        return n + (1 - lag + g8) if not isinstance(n, int) else min(max(n - lag + 1, 0), PAIRS) + g8

                    if isinstance(n, int) and n == 0:
                        pe.wait_ge(x_of[xp - 1], base[xp - 1] + PAIRS)
                        if run == 0:
                            pe.wait_ge(A.ready, 64)
                            pe.wait_ge(rest_loaded, 16 * REST)
                    for i in range(SLOTS_H):
                        b, s = i // 16, i % 16
                        q = c * 32 + (i - 32)
                        if att:
                            a, g = s % 2, s // 2
                            if later(q - 1):
                                pe.wait_ge(A.e, q - 1)
                            if s == 0:
                                pe.wait_ge((A.ml0, A.ml1)[b], c * 32)
                                pe.wait_ge(A.vcopied, c)
                            for kt in range(2):
                                last = pe.matmul(bank[1 + i % 2][:, kt * T:(kt + 1) * T],
                                                 KS[other][64 * a:64 * a + KROWS, b, g, kt * P:(kt + 1) * P],
                                                 QS[other][64 * a:64 * a + KROWS, b, g, :], start=True, stop=True)
                            last.then_inc(A.s, 1)
                        if mx:
                            qt, a, g = s // 8, s % 2, s % 8 // 2 * 2
                            if later(c * 32 + (i - 1)):
                                pe.wait_ge(A.red, c * 32 + (i - 1))
                            if s == 0:
                                pe.wait_ge((A.qkl0, A.qkl1)[b], c * 64 + 64)
                            for u in range(2):
                                r = slice(64 * a, 64 * a + SLOTS * D1)
                                last = pe.matmul(bank[3 + i % 2][:, u * T:(u + 1) * T],
                                                 QS[par][r, b, g + u, qt * P:(qt + 1) * P],
                                                 KS[par][r, b, g + u, :], start=True, stop=True)
                            last.then_inc(A.mx, 1)
                        lag, kind, e, k = UNITS[i]
                        if (post, exp, fin)[lag - 2]:
                            unit(n - lag, kind, e, k)
                        if i < 2 and post:
                            weigh(q - 2, par, c * 2 - 3, 1, i + 14)
                        if i >= 2 and att:
                            weigh(q - 2, other, c * 2 + ((i - 2) // 16 - 2), (i - 2) // 16, (i - 2) % 16)
                        if att and i == 1:
                            pe.wait_ge(A.red, c * 32)
                            pe.wait_ge(A.m0ev, upto(1))
                            if later(upto(3)):
                                pe.wait_ge(E.xt, upto(3))
                            for t in range(2):
                                last = pe.transpose(bank[0][0:H1, t * P:(t + 1) * P], NM[:, 2 + t, :], ident)
                            last.then_inc(A.m1T, 1)
                        if post and i == 3:
                            pe.wait_ge(A.m1ev, upto(1))
                            if later(upto(3)):
                                pe.wait_ge(E.xt, upto(3))
                            turn_sums(c, 0)
                        if post and i == 5:
                            pe.wait_ge(A.norm1, c * 4 - 7)
                            turn_sums(c, 1)
                        if pre and i == 6:
                            pe.wait_ge(A.norm, c + 2)
                            if post:
                                pe.wait_ge(A.norm1, c * 4 - 6)
                            else:
                                if later(upto(1)):
                                    pe.wait_ge(A.m1ev, upto(1))
                                if later(upto(1)):
                                    pe.wait_ge(A.m0ev, upto(1))
                                if later(upto(0)):
                                    pe.wait_ge(A.vev, upto(0))
                            turn(Y1[other], A.turned)
                        if post and i == 7:
                            pe.wait_ge(A.norm1, c * 4 - 6)
                            pe.wait_ge(A.copied, upto(-1))
                            turn_sums(c, 2)
                        if pre and i == 8:
                            pe.wait_ge(A.copied, c + 2)
                            if post:
                                pe.wait_ge(A.norm1, c * 4 - 5)
                            pe.matmul(bank[0][:, :], wt("q1"), YT1[:, :], start=True, stop=True).then_inc(A.q, 1)
                        if post and i == 9:
                            pe.wait_ge(A.norm1, c * 4 - 5)
                            pe.wait_ge(A.qev, upto(-1))
                            turn_sums(c, 3)
                        if pre and i == 10:
                            pe.wait_ge(A.qev, c + 2)
                            if post:
                                pe.wait_ge(A.norm1, c * 4 - 4)
                            pe.matmul(bank[0][:, :], wt("k1"), YT1[:, :], start=True, stop=True).then_inc(A.k, 1)
                        if post and i == 11:
                            pe.wait_ge(A.norm1, c * 4 - 4)
                            pe.wait_ge(A.kev, upto(-1))
                            turn(AN, A.anT)
                        if post and i == 13:
                            pe.wait_ge(A.anc, c - 1)
                            project(ANT, wt("o1"), A.wo)
                        if pre and i == 15:
                            pe.wait_ge(A.kev, c + 2)
                            if later(upto(2)):
                                pe.wait_ge(A.z, upto(2))
                            project(YT1, wt("v1"), A.v)
                        if mx and i == 20:
                            pe.wait_ge(A.red, c * 32 + 16)
                            pe.wait_ge(A.vev, upto(-1))
                            if later(upto(2)):
                                pe.wait_ge(A.z, upto(2))
                            for t in range(2):
                                last = pe.transpose(bank[0][0:H1, t * P:(t + 1) * P], NM[:, t, :], ident)
                            last.then_inc(A.m0T, 1)
                        if post and i == 26:
                            pe.wait_ge(A.m0ev, upto(0))
                            pe.wait_ge(A.z, c - 1)
                            pe.wait_ge(A.x1, c - 1)
                            turn(XS[par], E.turned)
                        between(n, i)

                return step

            def attn(run, xp):
                def step(n, par, pre, mid, main):
                    other = 1 - par
                    if main:
                        pe.wait_ge(V.kqc, n * 2 + 2)
                        for t in range(TP):
                            last = pe.matmul(bank[5 + t // 2][:, (t % 2) * T:(t % 2) * T + T],
                                             kqT[0][:, t * P:(t + 1) * P],
                                             kqT[1][:, (t // 2) * T:(t // 2) * T + T], start=True, stop=True)
                            if t % 2:
                                last.then_inc(V.s, 1)
                    if pre:
                        pe.wait_ge(V.norm, n + 3)
                        for t in range(TP):
                            last = pe.transpose(bank[0][:, t * P:(t + 1) * P], YV[par][:, t, :], ident)
                        last.then_inc(V.turned, 1)
                        pe.wait_ge(V.copied, n + 3)
                        a0 = PACK["kqv"][0]
                        for t in range(TP):
                            if later(n * 4 + (t + 7)):
                                pe.wait_ge(V.biased, n * 4 + (t + 7))
                            pe.matmul(bank[1 + t % 2][:, 0:3 * P], YVT[:, t * P:(t + 1) * P], W[:, a0:a0 + 3 * P],
                                      start=True, stop=True).then_inc(V.proj, 1)
                    if main:
                        pe.wait_ge(V.e, n * 4 + 4)
                        for u in range(2):
                            for t in range(TP):
                                last = pe.transpose(bank[3 + u][:, t * P:(t + 1) * P], PA[:, t, u * P:(u + 1) * P],
                                                    ident)
                            last.then_inc(V.pT, 1)
                        pe.wait_ge(V.pc, n * 2 + 2)
                        if isinstance(n, int) and n == 0:
                            pe.wait_ge(E.yused, 4 * PAIRS)
                        pe.wait_ge(x_of[xp], n + base[xp])
                        for t in range(TP):
                            for u in range(2):
                                last = pe.matmul(bank[7][:, t * P:(t + 1) * P], PAT[u][:, t * P:(t + 1) * P],
                                                 KQV[par][:, 2 * (t // 2) + u, 2, :], start=(u == 0), stop=(u == 1))
                        last.then_inc(V.av, 1)
                    if mid:
                        pe.wait_ge(V.kqv, n + 2)
                        for h in range(2):
                            for t in range(TP):
                                last = pe.transpose(bank[3 + h][:, t * P:(t + 1) * P], KQV[other][:, t, h, :], ident)
                            last.then_inc(V.kqT, 1)
                return step

            pe.wait_ge(w_loaded, 32)
            pe.wait_ge(setup_done, 1)
            run_phases(pe, {"ffn": ffn, "linear": linear, "experts": experts, "attn": attn})

        @block.vector
        def _(dve):
            def xs(n):
                return lambda t: X[:, bass.ds(n * TP + t, 1), :].rearrange("p o c -> p (o c)")

            def ffn(run, xp):
                def step(n, par, pre, mid, main):
                    if mid:
                        dve.wait_ge(F.rstd, n + (8 * run + 2))
                        token_norm(dve, xs(n + 1), lambda t: FY[1 - par][:, t, :], mv, rs).then_inc(F.norm, 1)
                    if pre:
                        link = Link(dve, F.link, n + (8 * run + 2), 2)
                        dve.wait_ge(x_of[xp - 1], n + (base[xp - 1] + 3))
                        if later(n + (8 * run + 2)):
                            dve.wait_ge(F.norm, n + (8 * run + 2))
                        token_stats(dve, xs(n + 2), st, mv, ve, link, F.var)
                        link.close()
                    if main:
                        dve.wait_ge(F.mm, n + (8 * run + 1))
                        dve.wait_ge(F.xb, n + (8 * run + 1))
                        dve.tensor_tensor(X[:, bass.ds(n * TP, TP), :], tiles(2 + par), XB[par][:, :, :],
                                          ALU.add).then_inc(x_of[xp], 1)
                return step


            def linear(run, xp):
                def finish_tiles(link, n, b, other):
                    ps = [bank[6 + u][:, :].rearrange("p (h e) -> p h e", e=32) for u in range(2)]
                    for u in range(2):
                        dve.wait_ge(L.pt, n * 4 + (2 * b + u - 3))
                        last = dve.tensor_scalar(den[:, u, :], ps[u][:, :, D0], DEN_EPS, None, ALU.add)
                    link(last)
                    link(dve.reciprocal(rec[:, :, :], den[:, :, :]))
                    link(dve.tensor_tensor(rw0[:, :, :], rec[:, :, :], WM[other][:, 2 * b:2 * b + 2, :], ALU.mult))
                    for u in range(2):
                        dve.tensor_tensor(PR[:, u, :, :], ps[u][:, :, 0:D0],
                                          over(rw0[:, u, :].unsqueeze(2), [P, HJ, D0]),
                                          ALU.mult).then_inc(L.ptused, 1)
                    dve.wait_ge(L.ptused, n * 4 + (2 * b - 2))
                    pr = PR[:, :, :, :].rearrange("p u (h j) e -> p (u h) j e", j=J0)
                    dve.tensor_tensor(YO[:, 2 * b:2 * b + 2, :].rearrange("p u (h e) -> p (u h) e", e=D0),
                                      pr[:, :, 0, :], pr[:, :, 1, :], ALU.add).then_inc(L.yo, 1)

                def scan(n, i, c):
                    j = n * 8 + i
                    if c == 0:
                        if later(j - 1):
                            dve.wait_ge(L.a0, j - 1)
                        if later(j * 2 - 2):
                            dve.wait_ge(L.a1, j * 2 - 2)
                    dve.wait_ge(L.bc, j * 3 + (c + 1))
                    dst = DD0[i % 2][:, 512 * c:512 * c + 512] if c < 2 else DD1[i % 2][:, :]
                    dve.tensor_tensor_scan(dst, bank[(3 * i + c) % 2][:, :], (I0 if c < 2 else I1)[:, :], 0.0,
                                           ALU.mult, ALU.add).then_inc(L.bcused, 1)

                def weigh(n, i):
                    j = n * 8 + i
                    dve.wait_ge(L.bcused, j * 3 + 1)
                    dve.wait_ge(L.scopied, j * 2 + 1)
                    if later(j - 1):
                        dve.wait_ge(L.av, j - 1)
                    s = SS[i % 2][:, 0:256].rearrange("p (o t) -> p o t", o=1)
                    dve.tensor_tensor(A0[i % 2][:, 0:2, :], DD0[i % 2][:, 0:512].rearrange("p (j t) -> p j t", j=2),
                                      over(s, [P, 2, T]), ALU.mult).then_inc(L.a0, 1)

                def step(n, par, pre, main, post, between=nothing):
                    if isinstance(n, int) and n == -1:
                        dve.wait_ge(rest_loaded, 16 * REST)
                        for name in ("ln2g", "ln2b"):
                            last = dve.tensor_scalar(row(name), row(name), 0.5, None, ALU.mult)
                        last.then_inc(halved, 1)
                    other = 1 - par
                    if pre:
                        link_ln, link_beta = Link(dve, L.link_ln, n + 1, 2), Link(dve, L.link_beta, n + 1, 7)
                        link_gate = Link(dve, L.link_gate, n + 1, 4)
                    if post:
                        link_post, link_out = Link(dve, L.link_post, n - 1, 6), Link(dve, L.link_out, n - 1, 2)
                    for i in range(8):
                        if pre and i == 0:
                            dve.wait_ge(x_of[xp - 1], n + (base[xp - 1] + 2))
                            token_stats(dve, xs(n + 1), st, mv, ve, link_ln, L.var)
                        if pre and i == 4:
                            dve.wait_ge(L.mg, n + 2)
                            r = ROW["bmg"]
                            link_gate(dve.tensor_tensor(MG[:, :, :],
                                                        bank[7][:, 0:TP * 40].rearrange("p (t c) -> p t c", t=TP),
                                                        over(R[:, r:r + 1, 0:40], [P, TP, 40]), ALU.add))
                            mix = MG[:, :, 0:HJ].rearrange("p t (h j) -> p t h j", j=J0)
                            link_gate(dve.tensor_tensor(mx[:, :, :], mix[:, :, :, 0], mix[:, :, :, 1], ALU.max))
                            dve.tensor_tensor(E0[:, :, 0:HJ].rearrange("p t (h j) -> p t h j", j=J0), mix,
                                              over(mx[:, :, :].unsqueeze(3), [P, TP, H0, J0]), ALU.subtract)
                            dve.tensor_scalar(E0[:, :, HJ:40], MG[:, :, HJ:40], -1.0, None,
                                              ALU.mult).then_inc(L.e0, 1)
                        if main:
                            scan(n, i, 0)
                            scan(n, i, 1)
                            weigh(n, i)
                            if i < 7:
                                scan(n, i, 2)
                        if pre and i == 1:
                            dve.wait_ge(L.rstd, n + 2)
                            if later(n):
                                dve.wait_ge(L.yr, n)
                            token_norm(dve, xs(n + 1), lambda t: Y0[other][:, t, :], mv, rs).then_inc(L.norm, 1)
                        if post and i == 0:
                            finish_tiles(link_post, n, 0, other)
                        if pre and i == 4:
                            if later(n * 8 + 8):
                                dve.wait_ge(L.qx, n * 8 + 8)
                            dve.wait_ge(L.exp4, n * 4 + 6)
                            dve.scalar_tensor_tensor(out=qf[:, :], in0=ex[:, 0, :], scalar=1.0, in1=re[:, 0, :],
                                                     op0=ALU.min, op1=ALU.add).then_inc(L.qf, 1)
                        if pre and i == 4:
                            dve.wait_ge(L.e1, n + 2)
                            e = E1[:, :, 0:HJ].rearrange("p t (h j) -> p t h j", j=J0)
                            dve.tensor_tensor(SD[:, :, 0:H0], e[:, :, :, 0], e[:, :, :, 1], ALU.add)
                            link_gate(dve.tensor_scalar(SD[:, :, H0:32], E1[:, :, HJ:40], 1.0, None, ALU.add))
                            link_gate(dve.reciprocal(RD[:, :, :], SD[:, :, :]))
                            dve.tensor_tensor(WM[other][:, :, :].rearrange("p t (h j) -> p t h j", j=J0), e,
                                              over(RD[:, :, 0:H0].unsqueeze(3), [P, TP, H0, J0]), ALU.mult)
                            r = ROW["decay"]
                            link_beta(dve.tensor_tensor(bE[:, :, :], RD[:, :, HJ:32],
                                                        over(R[:, r:r + 1, 0:HJ], [P, TP, HJ]), ALU.mult))
                            link_beta(dve.tensor_scalar(bE[:, :, :], bE[:, :, :], 0.9999, None, ALU.min))
                            link_beta(dve.tensor_copy(part[0][:, :, :], bE[:, :, :]))
                        if pre and i == 5:
                            dve.wait_ge(L.exp4, n * 4 + 8)
                            dve.scalar_tensor_tensor(out=kT[other][:, :], in0=ex[:, 1, :], scalar=1.0,
                                                     in1=re[:, 1, :], op0=ALU.min, op1=ALU.add).then_inc(L.qf, 1)
                            link_beta(dve.tensor_tensor(bR[:, :, :], bE[:, :, :], part[0][:, :, :], ALU.subtract))
                            link_beta(dve.tensor_copy(part[1][:, :, :], bR[:, :, :]))
                            link_beta(dve.tensor_tensor(bE[:, :, :], bR[:, :, :], part[1][:, :, :], ALU.subtract))
                            link_beta(dve.tensor_copy(part[2][:, :, :], bE[:, :, :]))
                            for k, c in enumerate(BETA_ROWS):
                                last = dve.tensor_copy(BT[:, :, c:c + HJ], part[k][:, :, :])
                            last.then_inc(L.bt, 1)
                            link_beta.close()
                        if post and i == 5:
                            dve.wait_ge(L.wo, n)
                            dve.wait_ge(L.yr, n)
                            dve.tensor_tensor(HR[:, :, :], tiles(6), YR0[:, :, :], ALU.add).then_inc(L.hr, 1)
                            dve.wait_ge(L.hr, n)
                            token_stats(dve, lambda t: HR[:, t, :], st2, mv2, ve2, link_out, L.var2)
                        if post and i == 6:
                            dve.wait_ge(L.rstd2, n)
                            token_norm(dve, lambda t: HR[:, t, :], lambda t: HN[:, t, :], mv2, rs2).then_inc(L.hn, 1)
                        if pre and i == 7:
                            dve.wait_ge(L.vmg, n + 2)
                            dve.tensor_tensor(VG[other][:, :, :, 0:D0],
                                              tiles(6).rearrange("p t (h e) -> p t h e", e=D0),
                                              over(RD[:, :, H0:HJ].unsqueeze(3), [P, TP, H0, D0]), ALU.mult)
                            dve.tensor_copy(VG[other][:, :, :, D0], RD[:, :, H0:HJ]).then_inc(L.v_used, 1)
                            link_gate.close()
                        if main and i == 7:
                            scan(n, i, 2)
                        if post and i == 1:
                            finish_tiles(link_post, n, 1, other)
                        between(n, i)
                    if pre:
                        link_ln.close()
                    if post:
                        link_post.close()
                        link_out.close()
                        dve.wait_ge(L.xd, n)
                        at = bass.ds((n - 1) * TP, TP)
                        dve.tensor_tensor(X[:, at, :], X[:, at, :], HG[:, :, :], ALU.add).then_inc(x_of[xp], 1)
                return step

            def experts(run, xp):
                g8 = 8 * run
                SCALE = float(D1) ** -0.5

                def split_max(c, b):
                    index, evacuated, written, free = ((2 * c, A.m0ev, A.mwr0, c), (2 * c + 1, A.m1ev, A.mwr1, c))[b]
                    dve.wait_ge((A.m0T, A.m1T)[b], c + 1)
                    if later(free * 16):
                        dve.wait_ge(written, free * 16)
                    link = Link(dve, A.link_m, index, 1)
                    ps = bank[0][0:H1, 0:T]
                    link(dve.tensor_copy(MH[b][:, 0, :], ps))
                    dve.tensor_tensor(MH[b][:, 1, :], ps, MH[b][:, 0, :], ALU.subtract).then_inc(evacuated, 1)

                def take(n, e):
                    c = n + g8
                    if later(c * 4 + e):
                        dve.wait_ge(E.acc, c * 4 + e)
                    dve.wait_ge(E.y, c * 4 + (e + 1))
                    dve.tensor_tensor(YB[:, :, :], tiles(7), row4(f"b2_{e}"), ALU.add).then_inc(E.yused, 1)

                def gather(n, par, e):
                    c = n + g8
                    dve.wait_ge(E.yused, c * 4 + (e + 1))
                    if e == 0:
                        dve.wait_ge(E.mask, c + 1)
                        if later(c):
                            dve.wait_ge(E.norm, c)
                    for t in range(TP):
                        last = dve.scalar_tensor_tensor(out=AC[:, t, :], in0=YB[:, t, :],
                                                        scalar=MK[par][:, e, t:t + 1],
                                                        in1=(AC if e else XS[par])[:, t, :], op0=ALU.mult,
                                                        op1=ALU.add)
                    last.then_inc(E.acc, 1)

                def stats(src, st_, link):
                    for t in range(TP):
                        last = dve.bn_stats(st_[:, t, :], src(t))
                    link(last)

                def moments(st_, mv_, ve_, link, var_sem):
                    dve.memset(tick[:, :], 0.0)
                    for t in range(TP):
                        last = dve.bn_aggr(mv_[:, t, :], st_[:, t, :])
                    link(last)
                    dve.tensor_scalar(ve_[:, :], mv_[:, :, 1], LN_EPS, None, ALU.add).then_inc(var_sem, 1)

                def scale(src, dst, mv_, rs_, tt):
                    for t in tt:
                        last = dve.tensor_scalar(dst(t), src(t), mv_[:, t, 0:1], rs_[:, t:t + 1], ALU.subtract,
                                                 ALU.mult)
                    return last

                def masks(n, par, acc):
                    c = n + g8
                    link = Link(dve, E.link_key, c, 10)
                    dve.wait_ge(A.x1, c + 1)
                    if later(acc):
                        dve.wait_ge(E.acc, acc)
                    link(dve.tensor_tensor(KP[:, :, :], XS[par][:, :, :], row4("rw"), ALU.mult))
                    link(dve.tensor_reduce(key[0][:, :], KP[:, :, :], AX_X, ALU.add))
                    link(dve.tensor_scalar(key[0][:, :], key[0][:, :], row("rb")[:, 0:1], None, ALU.add))
                    link(dve.tensor_copy(kint[:, :], key[0][:, :]))
                    link(dve.tensor_copy(key[1][:, :], kint[:, :]))
                    link(dve.tensor_tensor(key[2][:, :], key[1][:, :], key[0][:, :], ALU.is_gt))
                    link(dve.tensor_tensor(key[1][:, :], key[1][:, :], key[2][:, :], ALU.subtract))
                    link(dve.tensor_copy(kint[:, :], key[1][:, :]))
                    link(dve.tensor_scalar(kint[:, :], kint[:, :], EXPERTS - 1, None, ALU.bitwise_and))
                    link(dve.tensor_copy(key[2][:, :], kint[:, :]))
                    for e in range(EXPERTS):
                        last = dve.tensor_scalar(MK[par][:, e, :], key[2][:, :], float(e), None, ALU.is_equal)
                    last.then_inc(E.mask, 1)
                    link.close()

                def step(n, par, pre, mx, att, post, exp, fin, between=nothing):
                    c = n + g8
                    other = 1 - par
                    if pre:
                        link_x = Link(dve, A.link_ln, c + 1, 2)
                    if post:
                        link_n, link_z = Link(dve, A.link_n, c - 2, 4), Link(dve, A.link_z, c - 2, 2)
                    if fin:
                        link_e = Link(dve, E.link_ln, c - 4, 2)

                    def divide(t):
                        ps = bank[0][:, :].rearrange("p (h e) -> p h e", e=32)
                        dve.wait_ge(A.pt, c * 4 + (t - 7))
                        link_n(dve.reciprocal(rec1[:, t, :], ps[:, :, D1]))
                        dve.tensor_tensor(AN[:, t, :].rearrange("p (h e) -> p h e", e=D1), ps[:, :, 0:D1],
                                          over(rec1[:, t, :].unsqueeze(2), [P, H1, D1]),
                                          ALU.mult).then_inc(A.norm1, 1)

                    def y(t):
                        return Y1[other][:, t, :]

                    for i in range(SLOTS_H):
                        b, s = i // 16, i % 16
                        if mx:
                            qt, a, g = s // 8, s % 2, s % 8 // 2 * 2
                            dve.wait_ge(A.mx, c * 32 + (i + 1))
                            h = 2 * g + a
                            dve.tensor_reduce(NM[:, 2 * b + qt, h:h + 3:2],
                                              bank[3 + i % 2][:, :].rearrange("p (u t) -> p u t", u=2), AX_X,
                                              ALU.max, negate=True).then_inc(A.red, 1)
                        if pre and i == 0:
                            dve.wait_ge(x_of[xp - 1], n + (base[xp - 1] + 2))
                            stats(xs(n + 1), st, link_x)
                        if pre and i == 1:
                            moments(st, mv, ve, link_x, A.var)
                        if pre and i == 3:
                            dve.wait_ge(A.rstd, c + 2)
                            if later(c):
                                dve.wait_ge(A.yr, c)
                            scale(xs(n + 1), y, mv, rs, (0, 1))
                        if pre and i == 9:
                            dve.wait_ge(A.q, c + 2)
                            if later(c * 2 + 2):
                                dve.wait_ge(A.r1, c * 2 + 2)
                            dve.tensor_scalar(qk32[0][:, :], bank[0][:, :], wt("bq")[:, 0:1], SCALE, ALU.add,
                                              ALU.mult).then_inc(A.qev, 1)
                        if att and i == 2:
                            split_max(c - 1, 1)
                        if post and i in (4, 6, 8, 10):
                            divide(i // 2 - 2)
                        if pre and i == 4:
                            scale(xs(n + 1), y, mv, rs, (2, 3)).then_inc(A.norm, 1)
                        if pre and i == 10:
                            dve.wait_ge(A.qev, c + 2)
                            if later(c * 192 + 192):
                                dve.wait_ge(A.scr, c * 192 + 192)
                            dve.tensor_copy(PQ[0][:, 0, :], qk32[0][:, :]).then_inc(A.hi, 1)
                        if pre and i == 11:
                            dve.wait_ge(A.kev, c + 2)
                            dve.tensor_copy(PQ[1][:, 0, :], qk32[1][:, :]).then_inc(A.hi, 1)
                        if pre and i in (12, 13):
                            h = i - 12
                            dve.wait_ge(A.r1, c * 2 + (3 + h))
                            dve.tensor_copy(PQ[h][:, 1, :], qkr[h][:, :]).then_inc(A.mid, 1)
                        if post and i == 14:
                            dve.wait_ge(A.wo, c - 1)
                            dve.wait_ge(A.yr, c - 1)
                            dve.tensor_tensor(Z[:, :, :], tiles(0), YR1[par][:, :, :], ALU.add).then_inc(A.z, 1)
                        if post and i == 16:
                            dve.wait_ge(A.z, c - 1)
                            stats(lambda t: Z[:, t, :], st2, link_z)
                        if post and i == 17:
                            moments(st2, mv2, ve2, link_z, A.var2)
                        if post and i == 20:
                            dve.wait_ge(A.rstd2, c - 1)
                            scale(lambda t: Z[:, t, :], lambda t: ZN[:, t, :], mv2, rs2, (0, 1))
                        if mx and i == 21:
                            split_max(c, 0)
                        if post and i == 21:
                            scale(lambda t: Z[:, t, :], lambda t: ZN[:, t, :], mv2, rs2, (2, 3)).then_inc(A.zn, 1)
                        if fin and i == 6:
                            take(n - 4, 3)
                        if fin and i == 7:
                            gather(n - 4, par, 3)
                        if fin and i == 11:
                            dve.wait_ge(E.acc, c * 4 - 12)
                            stats(lambda t: AC[:, t, :], st3, link_e)
                        if fin and i == 12:
                            moments(st3, mv3, ve3, link_e, E.var)
                        if exp and i == 14:
                            take(n - 3, 0)
                        if fin and i == 15:
                            dve.wait_ge(E.rstd, c - 3)
                            scale(lambda t: AC[:, t, :], lambda t: EN[:, t, :], mv3, rs3,
                                  range(TP)).then_inc(E.norm, 1)
                        if exp and i == 17:
                            gather(n - 3, other, 0)
                        if exp and i == 22:
                            take(n - 3, 1)
                        if exp and i == 23:
                            gather(n - 3, other, 1)
                        if fin and i == 25:
                            dve.wait_ge(E.b, c - 3)
                            at = bass.ds((n - 4) * TP, TP)
                            dve.tensor_tensor(X[:, at, :], X[:, at, :], EG[:, :, :], ALU.add).then_inc(x_of[xp], 1)
                        if post and i == 27:
                            masks(n - 2, par, (c - 2) * 4 - 2)
                        if exp and i == 30:
                            take(n - 3, 2)
                        if exp and i == 31:
                            gather(n - 3, other, 2)
                        between(n, i)
                return step

            def attn(run, xp):
                def step(n, par, pre, mid, main):
                    other = 1 - par
                    if pre:
                        link = Link(dve, V.link_ln, n + 2, 2)
                        dve.wait_ge(x_of[xp - 1], n + (base[xp - 1] + 3))
                        token_stats(dve, xs(n + 2), st, mv, ve, link, V.var)
                        link.close()
                    if pre:
                        dve.wait_ge(V.rstd, n + 3)
                        if later(n + 1):
                            dve.wait_ge(V.yx, n + 1)
                        token_norm(dve, xs(n + 2), lambda t: YV[par][:, t, :], mv, rs).then_inc(V.norm, 1)
                    if mid:
                        dve.wait_ge(V.rstd12, n + 2)
                        for u in range(12):
                            last = dve.tensor_scalar(KQV[other][:, u // 3, u % 3, :], RAW[:, u // 3, u % 3, :],
                                                     mean12[:, u:u + 1], rs12[:, u:u + 1], ALU.subtract, ALU.mult)
                        last.then_inc(V.norm12, 1)
                    if main:
                        for h in range(2):
                            dve.wait_ge(V.s, n * 2 + (1 + h))
                            dve.tensor_reduce(nmx[:, 2 * h:2 * h + 2],
                                              bank[5 + h][:, :].rearrange("p (u t) -> p u t", u=2), AX_X,
                                              ALU.max, negate=True).then_inc(V.nmx, 1)
                    if pre:
                        k = ROW["abk"]
                        if later(n + 2):
                            dve.wait_ge(V.norm12, n + 2)
                        for t in range(TP):
                            dve.wait_ge(V.proj, n * 4 + (t + 9))
                            dve.tensor_tensor(RAW[:, t, :, :].rearrange("p k c -> p (k c)"), bank[1 + t % 2][:, 0:3 * P],
                                              R[:, k:k + 3, :].rearrange("p k c -> p (k c)"),
                                              ALU.add).then_inc(V.biased, 1)
                        dve.wait_ge(V.biased, n * 4 + 12)
                        link = Link(dve, V.link_b, n + 2, 3)
                        for u in range(12):
                            last = dve.bn_stats(st12[:, u, :], RAW[:, u // 3, u % 3, :])
                        link(last)
                        dve.tensor_tensor(dif12[:, :], st12[:, :, 1], st12[:, :, 4], ALU.subtract)
                        dve.tensor_tensor(mean12[:, :], st12[:, :, 1], st12[:, :, 4], ALU.add)
                        link(dve.tensor_tensor(var12[:, :], st12[:, :, 2], st12[:, :, 5], ALU.add))
                        dve.tensor_tensor(dif12[:, :], dif12[:, :], dif12[:, :], ALU.mult)
                        dve.tensor_scalar(mean12[:, :], mean12[:, :], 0.5, None, ALU.mult)
                        link(dve.tensor_scalar(var12[:, :], var12[:, :], 1.0 / P, LN_EPS, ALU.mult, ALU.add))
                        dve.scalar_tensor_tensor(out=ve12[:, :], in0=dif12[:, :], scalar=0.25, in1=var12[:, :],
                                                 op0=ALU.mult, op1=ALU.add).then_inc(V.var12, 1)
                        link.close()
                    if main:
                        dve.wait_ge(V.e, n * 4 + 4)
                        dve.wait_ge(x_of[xp], n + base[xp])
                        dve.reciprocal(rsum[:, :], esum[:, :]).then_inc(V.sumr, 1)
                        dve.wait_ge(V.sumr, n + 1)
                        dve.wait_ge(V.av, n + 1)
                        dve.wait_ge(V.yx, n + 1)
                        for t in range(TP):
                            at = X[:, bass.ds(n * TP + t, 1), :].rearrange("p o c -> p (o c)")
                            last = dve.scalar_tensor_tensor(out=at, in0=bank[7][:, t * P:(t + 1) * P],
                                                            scalar=rsum[:, t:t + 1], in1=YX[par][:, t, :],
                                                            op0=ALU.mult, op1=ALU.add)
                        last.then_inc(x_of[xp], 1)
                return step

            dve.wait_ge(w_loaded, 32)
            link = Link(dve, setup_link, 0, 4)
            dve.memset(I0[:, :], 0.0)
            link(dve.tensor_scalar(row("scb"), row("scb"), 0.5 / 127.0, None, ALU.mult))
            for t in (0, 2):
                dve.tensor_copy(I0[:, t * P:(t + 1) * P], wt("ident"))
            for t in range(TP):
                dve.tensor_copy(I1[:, t * P:(t + 1) * P], wt("ident"))
            dve.tensor_tensor(wt("cbt"), wt("cbt"), row("scb"), ALU.mult)
            dve.tensor_scalar(row("qbias"), row("qbias"), 0.5, None, ALU.mult)
            a, b, c = (wt("ident")[:, r:r + HJ] for r in BETA_ROWS)
            link(dve.tensor_tensor(rowsel[:, :], a, b, ALU.add))
            link(dve.tensor_tensor(rowsel[:, :], rowsel[:, :], c, ALU.add))
            link(dve.tensor_copy(SEL[:, :, :], over(rowsel[:, :].unsqueeze(2), [P, HJ, P])))
            link.close()
            dve.tensor_copy(rs[:, :], I1[:, 0:TP]).then_inc(setup_done, 1)
            dve.wait_ge(x_loaded, 16 * PAIRS)
            dve.tensor_copy(rs2[:, :], I1[:, 0:TP]).then_inc(x_of[0], PAIRS)
            dve.tensor_copy(ve2[:, :], I1[:, 0:TP]).then_inc(x_of[1], PAIRS)
            run_phases(dve, {"ffn": ffn, "linear": linear, "experts": experts, "attn": attn})


def _lay_out(a):
    f = np.float32
    g = lambda k: np.asarray(a[k], dtype=f)
    pack = np.zeros((P, PACKED), f)

    def put(name, value):
        at, n = PACK[name]
        pack[:, at:at + n] = np.asarray(value).reshape(P, n)

    put("cbt", g("L0_ffn_CB").T)
    put("q0", g("L0_attn_Wq").T)
    put("k0", g("L0_attn_Wk").T)
    put("vmg", np.concatenate([g("L0_attn_Wv"), g("L0_attn_Wmix"), g("L0_attn_Wgate"),
                               g("L0_attn_Wbeta")], 0).T)
    put("out0", g("L0_attn_Wout").T)
    order = np.array([(2 * gg + aa) * D1 + d for aa in range(2) for d in range(D1) for gg in range(H1 // 2)])
    put("q1", g("L1_ffn_Wq")[:, order])
    put("k1", g("L1_ffn_Wk")[:, order])
    put("bq", g("L1_ffn_bq")[order])
    put("bk", g("L1_ffn_bk")[order])
    put("v1", g("L1_ffn_Wv"))
    put("o1", g("L1_ffn_Wo"))
    put("b1", g("L1_ffn_b1").reshape(EXPERTS * CH, P).T)
    put("kqv", np.concatenate([g("L1_attn_Wk"), g("L1_attn_Wq"), g("L1_attn_Wv")], 1))
    put("hmask", (np.arange(P)[:, None] // D0 == np.arange(H0)[None, :]).astype(f))
    put("ident", np.eye(P, dtype=f))
    vec = {"scb": "L0_ffn_SCB", "qbias": "L0_ffn_bias", "bout": "L0_attn_bout", "lng": "L0_attn_ln_g",
           "lnb": "L0_attn_ln_b", "bv": "L1_ffn_bv", "bo": "L1_ffn_bo", "ln1g": "L1_ffn_ln1_g",
           "ln1b": "L1_ffn_ln1_b", "ln2g": "L1_ffn_ln2_g", "ln2b": "L1_ffn_ln2_b", "abk": "L1_attn_bk",
           "abq": "L1_attn_bq", "abv": "L1_attn_bv", "agk": "L1_attn_gk", "agq": "L1_attn_gq", "agv": "L1_attn_gv",
           "aek": "L1_attn_betak", "aeq": "L1_attn_betaq", "aev": "L1_attn_betav"}
    rows = np.zeros((len(ROWS), P), f)
    for name, key in vec.items():
        rows[ROW[name]] = g(key)
    rows[ROW["bmg"], 0:16] = g("L0_attn_bmix")
    rows[ROW["bmg"], 16:24] = g("L0_attn_bgate")
    rows[ROW["bmg"], 24:40] = g("L0_attn_bbeta")
    slopes = np.array([2.0 ** (-8.0 * (h + 1) / H0) for h in range(H0)], f)
    rows[ROW["decay"], 0:HJ] = np.repeat(np.exp(-slopes), J0)
    rows[ROW["rw"]] = g("L1_ffn_router_w")[:, 0]
    rows[ROW["rb"], 0] = g("L1_ffn_router_b")[0]
    for e in range(EXPERTS):
        rows[ROW[f"b2_{e}"]] = g("L1_ffn_b2")[e]
    return {"in_x": g("L0_attn_x").reshape(SEQS * T, P), "in_pack": pack, "in_rows": rows.reshape(-1),
            "in_w1": g("L1_ffn_W1"), "in_w2": g("L1_ffn_W2")}


def kernel(**inputs):
    import concourse.bacc as _bacc
    from concourse.bass_utils import run_bass_kernel_spmd as _run

    nc = _bacc.Bacc("TRN2", target_bir_lowering=False, num_devices=1)
    arrays = {k: np.ascontiguousarray(v) for k, v in _lay_out(inputs).items()}
    args = [nc.dram_tensor(k, v.shape, F32, kind="ExternalInput").ap() for k, v in arrays.items()]
    out = nc.dram_tensor("out_0", (SEQS * T, P), F32, kind="ExternalOutput").ap()
    program(nc, *args, out)
    r = _run(nc, [arrays], core_ids=[0])
    return np.asarray(r.results[0]["out_0"]).reshape(SEQS, T, P)
```
